# Optimizing a Trainium2 kernel written in Bass

```python
import numpy as np
import jax
import jax.numpy as jnp

def _softmax(x, axis=-1):
    return jax.nn.softmax(x, axis=axis)

def _gelu(x):
    return jax.nn.gelu(x, approximate=True)

def _silu(x):
    return jax.nn.silu(x)

def _sigmoid(x):
    return jax.nn.sigmoid(x)

def _layernorm(x, axis=-1, eps=1e-05):
    m = jnp.mean(x, axis=axis, keepdims=True)
    v = jnp.var(x, axis=axis, keepdims=True)
    return (x - m) / jnp.sqrt(v + eps)

def _scatter_add(tgt, idx, src, axis=0):
    return tgt.at[idx].add(src)

def _segment_sum(src, seg, n):
    return jax.ops.segment_sum(src, seg, n)
kernel_name = 'mk_adaln_ffn_d4_seqx_r8_4fa4eb'

def setup_inputs(seed: int=0):
    np.random.seed(seed)
    _w = jnp.asarray

    def _rec_inputs():
        import jax
        import jax.numpy as jnp
        _rk = jax.random.key(seed)
        x = -0.000125 + 0.9999 * jax.random.normal(jax.random.fold_in(_rk, 1), (64, 32, 512), jnp.float32)
        _lenS = 32 - jax.random.randint(jax.random.fold_in(_rk, 7), (64,), 0, max(1, 32 // 4) + 1, jnp.int32)
        _lenS2 = 32 - jax.random.randint(jax.random.fold_in(_rk, 8), (64,), 0, max(1, 32 // 4) + 1, jnp.int32)
        cond_128 = 0.0061147 + 1.02565 * jax.random.normal(jax.random.fold_in(_rk, 11), (64, 128), jnp.float32)
        fside_S_0 = -0.022604 + 0.987366 * jax.random.normal(jax.random.fold_in(_rk, 12), (32,), jnp.float32)
        return (x, cond_128, fside_S_0)
    x, cond_128, fside_S_0 = _rec_inputs()

    def _L0_cond_setup():
        import jax, jax.numpy as jnp
        import numpy as np
        from jax import lax
        N, C_IN, L = (32, 32, 512)
        C_OUT, K, GROUPS = (32, 9, 4)
        C_DIM, PAD, STRIDE = (128, 4, 1)
        key = jax.random.key(seed)
        k1, k2, k3, k4, k5 = jax.random.split(key, 5)
        x = jax.random.normal(k1, (N, C_IN, L), dtype=jnp.float32)
        c = jax.random.normal(k2, (N, C_DIM), dtype=jnp.float32)
        weight = jax.random.normal(k3, (C_OUT, C_IN // GROUPS, K), dtype=jnp.float32)
        c_weight = jax.random.normal(k4, (C_OUT, C_DIM), dtype=jnp.float32)
        bias = jax.random.normal(k5, (C_OUT,), dtype=jnp.float32)
        return {'x': x, 'c': c, 'weight': weight, 'c_weight': c_weight, 'bias': bias}
    _L0_cond_all = _L0_cond_setup()
    _L0_cond_in = {k: v for k, v in _L0_cond_all.items() if k in ('weight', 'c_weight')}
    del _L0_cond_all

    def _L0_ffn_setup():
        import jax, jax.numpy as jnp
        import numpy as np
        import math
        B, S, IN, OUT = (4, 256, 512, 512)
        E, R, K = (8, 64, 128)
        SCALE = 64.0 / 64.0
        MULTIPLIER = 1.0
        key = jax.random.key(seed)
        ks = jax.random.split(key, 6)
        return {'x': jax.random.normal(ks[0], (B, S, IN), jnp.float32), 'W_org': jax.random.normal(ks[1], (OUT, IN), jnp.float32) * 0.02, 'lora_down': jax.random.normal(ks[2], (E, IN, R), jnp.float32) * 0.02, 'lora_up': jax.random.normal(ks[3], (E, R, OUT), jnp.float32) * 0.02, 'lora_keys': jax.random.normal(ks[4], (E, K), jnp.float32), 'Wq': jax.random.normal(ks[5], (K, IN), jnp.float32) * 0.02}
    _L0_ffn_all = _L0_ffn_setup()
    _L0_ffn_in = {k: v for k, v in _L0_ffn_all.items() if k in ('W_org', 'lora_down', 'lora_up', 'lora_keys', 'Wq')}
    del _L0_ffn_all

    def _L1_cond_setup():
        import jax, jax.numpy as jnp
        import numpy as np
        K = 8
        T = 1.0
        D_EMBD = 128
        IN_C = 32
        OUT_C = 32
        BS = 32
        H = 512
        HID = 128
        key = jax.random.key(seed)
        ks = jax.random.split(key, 10)
        s = lambda fan_in: 1.0 / np.sqrt(fan_in)
        return {'x': jax.random.normal(ks[0], (BS, IN_C, H), dtype=jnp.float32), 'embedding': jax.random.normal(ks[1], (BS, D_EMBD), dtype=jnp.float32), 'W0': jax.random.normal(ks[2], (D_EMBD, HID), dtype=jnp.float32) * s(D_EMBD), 'b0': jnp.zeros((HID,), dtype=jnp.float32), 'W1': jax.random.normal(ks[3], (HID, HID), dtype=jnp.float32) * s(HID), 'b1': jnp.zeros((HID,), dtype=jnp.float32), 'W2': jax.random.normal(ks[4], (HID, K), dtype=jnp.float32) * s(HID), 'b2': jnp.zeros((K,), dtype=jnp.float32), 'weight': jax.random.normal(ks[5], (K, OUT_C, IN_C, 1), dtype=jnp.float32) * s(IN_C), 'bias_k': jax.random.normal(ks[6], (K, OUT_C), dtype=jnp.float32) * 0.1}
    _L1_cond_all = _L1_cond_setup()
    _L1_cond_in = {k: v for k, v in _L1_cond_all.items() if k in ('W0', 'b0', 'W1', 'b1', 'W2', 'b2', 'weight', 'bias_k')}
    del _L1_cond_all

    def _L1_ffn_setup():
        import jax, jax.numpy as jnp
        import numpy as np
        IN_F = 512
        OUT_F = 512
        RANK = 8
        NUM_EXPERTS = 64
        TOP_K = 16
        ROUTER_DIM = 16
        ALPHA = 32
        SCALING = ALPHA / TOP_K
        BOTTLENECK = NUM_EXPERTS * RANK
        key = jax.random.key(seed)
        ks = jax.random.split(key, 5)
        x = jax.random.normal(ks[0], (4, 512, IN_F), dtype=jnp.float32)
        bound_a = float(np.sqrt(6.0 / IN_F))
        A_w = jax.random.uniform(ks[1], (BOTTLENECK, IN_F), jnp.float32, -bound_a, bound_a)
        B_w = jax.random.normal(ks[2], (OUT_F, BOTTLENECK), dtype=jnp.float32) * 0.02
        Wq_w = jax.random.normal(ks[3], (ROUTER_DIM, IN_F), dtype=jnp.float32) * 0.02
        keys = jax.random.normal(ks[4], (NUM_EXPERTS, ROUTER_DIM), dtype=jnp.float32) * 0.01
        return {'x': x, 'A_w': A_w, 'B_w': B_w, 'Wq_w': Wq_w, 'keys': keys}
    _L1_ffn_all = _L1_ffn_setup()
    _L1_ffn_in = {k: v for k, v in _L1_ffn_all.items() if k in ('A_w', 'B_w', 'Wq_w', 'keys')}
    del _L1_ffn_all

    def _L2_cond_setup():
        import jax, jax.numpy as jnp
        import numpy as np
        from jax import lax
        N, C_IN, L = (32, 32, 512)
        C_OUT, K, GROUPS = (32, 9, 4)
        C_DIM, PAD, STRIDE = (128, 4, 1)
        key = jax.random.key(seed)
        k1, k2, k3, k4, k5 = jax.random.split(key, 5)
        x = jax.random.normal(k1, (N, C_IN, L), dtype=jnp.float32)
        c = jax.random.normal(k2, (N, C_DIM), dtype=jnp.float32)
        weight = jax.random.normal(k3, (C_OUT, C_IN // GROUPS, K), dtype=jnp.float32)
        c_weight = jax.random.normal(k4, (C_OUT, C_DIM), dtype=jnp.float32)
        bias = jax.random.normal(k5, (C_OUT,), dtype=jnp.float32)
        return {'x': x, 'c': c, 'weight': weight, 'c_weight': c_weight, 'bias': bias}
    _L2_cond_all = _L2_cond_setup()
    _L2_cond_in = {k: v for k, v in _L2_cond_all.items() if k in ('weight', 'c_weight')}
    del _L2_cond_all

    def _L2_ffn_setup():
        import jax, jax.numpy as jnp
        import numpy as np
        NUM_EXPERTS = 8
        RANK = 32
        ALPHA = 16.0
        TOP_K = 2
        TEMPERATURE = 1.0
        GAMMA = 0.5
        SOFT_TOPK_TEMP = 0.5
        N_GRAM = 2
        EPS = 1e-06
        key = jax.random.key(seed)
        ks = jax.random.split(key, 6)
        d_in, d_out = (512, 512)
        Bsz, T = (4, 256)
        x = jax.random.normal(ks[0], (Bsz, T, d_in), dtype=jnp.float32)
        W = jax.random.normal(ks[1], (d_out, d_in), dtype=jnp.float32) / np.sqrt(d_in)
        b = jax.random.normal(ks[2], (d_out,), dtype=jnp.float32) * 0.01
        A = jax.random.normal(ks[3], (d_in, RANK), dtype=jnp.float32) / np.sqrt(d_in)
        Bmat = jax.random.normal(ks[4], (RANK, d_out), dtype=jnp.float32) * 0.01
        LiMEs = jax.random.normal(ks[5], (NUM_EXPERTS, RANK), dtype=jnp.float32) * 0.1
        return {'x': x, 'W': W, 'b': b, 'A': A, 'Bmat': Bmat, 'LiMEs': LiMEs}
    _L2_ffn_all = _L2_ffn_setup()
    _L2_ffn_in = {k: v for k, v in _L2_ffn_all.items() if k in ('W', 'b', 'A', 'Bmat', 'LiMEs')}
    del _L2_ffn_all

    def _L3_cond_setup():
        import jax, jax.numpy as jnp
        import numpy as np
        K = 8
        T = 1.0
        D_EMBD = 128
        IN_C = 32
        OUT_C = 32
        BS = 32
        H = 512
        HID = 128
        key = jax.random.key(seed)
        ks = jax.random.split(key, 10)
        s = lambda fan_in: 1.0 / np.sqrt(fan_in)
        return {'x': jax.random.normal(ks[0], (BS, IN_C, H), dtype=jnp.float32), 'embedding': jax.random.normal(ks[1], (BS, D_EMBD), dtype=jnp.float32), 'W0': jax.random.normal(ks[2], (D_EMBD, HID), dtype=jnp.float32) * s(D_EMBD), 'b0': jnp.zeros((HID,), dtype=jnp.float32), 'W1': jax.random.normal(ks[3], (HID, HID), dtype=jnp.float32) * s(HID), 'b1': jnp.zeros((HID,), dtype=jnp.float32), 'W2': jax.random.normal(ks[4], (HID, K), dtype=jnp.float32) * s(HID), 'b2': jnp.zeros((K,), dtype=jnp.float32), 'weight': jax.random.normal(ks[5], (K, OUT_C, IN_C, 1), dtype=jnp.float32) * s(IN_C), 'bias_k': jax.random.normal(ks[6], (K, OUT_C), dtype=jnp.float32) * 0.1}
    _L3_cond_all = _L3_cond_setup()
    _L3_cond_in = {k: v for k, v in _L3_cond_all.items() if k in ('W0', 'b0', 'W1', 'b1', 'W2', 'b2', 'weight', 'bias_k')}
    del _L3_cond_all

    def _L3_ffn_setup():
        import jax, jax.numpy as jnp
        import numpy as np
        key = jax.random.key(seed)
        k = jax.random.split(key, 6)
        x = jax.random.normal(k[0], (4, 256, 512), jnp.float32)
        W = jax.random.normal(k[1], (512, 512), jnp.float32) * 0.02
        bias = jax.random.normal(k[2], (512,), jnp.float32) * 0.02
        A = jax.random.normal(k[3], (16, 16, 512), jnp.float32) * 0.02
        Bf = jax.random.normal(k[4], (16, 512, 16), jnp.float32) * 0.02
        coeffs = jax.random.uniform(k[5], (16,), jnp.float32)
        scales = jnp.full((16,), 0.5, jnp.float32)
        return {'x': x, 'W': W, 'bias': bias, 'A': A, 'Bf': Bf, 'coeffs': coeffs, 'scales': scales}
    _L3_ffn_all = _L3_ffn_setup()
    _L3_ffn_in = {k: v for k, v in _L3_ffn_all.items() if k in ('W', 'bias', 'A', 'Bf', 'coeffs', 'scales')}
    del _L3_ffn_all
    return {'x': x, 'cond_128': cond_128, 'fside_S_0': fside_S_0, 'L0_cond_weight': _L0_cond_in['weight'], 'L0_cond_c_weight': _L0_cond_in['c_weight'], 'L0_ffn_W_org': _L0_ffn_in['W_org'], 'L0_ffn_lora_down': _L0_ffn_in['lora_down'], 'L0_ffn_lora_up': _L0_ffn_in['lora_up'], 'L0_ffn_lora_keys': _L0_ffn_in['lora_keys'], 'L0_ffn_Wq': _L0_ffn_in['Wq'], 'L1_cond_W0': _L1_cond_in['W0'], 'L1_cond_b0': _L1_cond_in['b0'], 'L1_cond_W1': _L1_cond_in['W1'], 'L1_cond_b1': _L1_cond_in['b1'], 'L1_cond_W2': _L1_cond_in['W2'], 'L1_cond_b2': _L1_cond_in['b2'], 'L1_cond_weight': _L1_cond_in['weight'], 'L1_cond_bias_k': _L1_cond_in['bias_k'], 'L1_ffn_A_w': _L1_ffn_in['A_w'], 'L1_ffn_B_w': _L1_ffn_in['B_w'], 'L1_ffn_Wq_w': _L1_ffn_in['Wq_w'], 'L1_ffn_keys': _L1_ffn_in['keys'], 'L2_cond_weight': _L2_cond_in['weight'], 'L2_cond_c_weight': _L2_cond_in['c_weight'], 'L2_ffn_W': _L2_ffn_in['W'], 'L2_ffn_b': _L2_ffn_in['b'], 'L2_ffn_A': _L2_ffn_in['A'], 'L2_ffn_Bmat': _L2_ffn_in['Bmat'], 'L2_ffn_LiMEs': _L2_ffn_in['LiMEs'], 'L3_cond_W0': _L3_cond_in['W0'], 'L3_cond_b0': _L3_cond_in['b0'], 'L3_cond_W1': _L3_cond_in['W1'], 'L3_cond_b1': _L3_cond_in['b1'], 'L3_cond_W2': _L3_cond_in['W2'], 'L3_cond_b2': _L3_cond_in['b2'], 'L3_cond_weight': _L3_cond_in['weight'], 'L3_cond_bias_k': _L3_cond_in['bias_k'], 'L3_ffn_W': _L3_ffn_in['W'], 'L3_ffn_bias': _L3_ffn_in['bias'], 'L3_ffn_A': _L3_ffn_in['A'], 'L3_ffn_Bf': _L3_ffn_in['Bf'], 'L3_ffn_coeffs': _L3_ffn_in['coeffs'], 'L3_ffn_scales': _L3_ffn_in['scales']}

def reference(x, cond_128, fside_S_0, L0_cond_weight, L0_cond_c_weight, L0_ffn_W_org, L0_ffn_lora_down, L0_ffn_lora_up, L0_ffn_lora_keys, L0_ffn_Wq, L1_cond_W0, L1_cond_b0, L1_cond_W1, L1_cond_b1, L1_cond_W2, L1_cond_b2, L1_cond_weight, L1_cond_bias_k, L1_ffn_A_w, L1_ffn_B_w, L1_ffn_Wq_w, L1_ffn_keys, L2_cond_weight, L2_cond_c_weight, L2_ffn_W, L2_ffn_b, L2_ffn_A, L2_ffn_Bmat, L2_ffn_LiMEs, L3_cond_W0, L3_cond_b0, L3_cond_W1, L3_cond_b1, L3_cond_W2, L3_cond_b2, L3_cond_weight, L3_cond_bias_k, L3_ffn_W, L3_ffn_bias, L3_ffn_A, L3_ffn_Bf, L3_ffn_coeffs, L3_ffn_scales):
    import jax
    import jax.numpy as jnp

    def _L0_cond_ref(x, c, weight, c_weight, bias):
        import jax, jax.numpy as jnp
        import numpy as np
        from jax import lax
        N, C_IN, L = (32, 32, 512)
        C_OUT, K, GROUPS = (32, 9, 4)
        C_DIM, PAD, STRIDE = (128, 4, 1)
        out = lax.conv_general_dilated(x, weight, window_strides=(STRIDE,), padding=[(PAD, PAD)], dimension_numbers=('NCH', 'OIH', 'NCH'), feature_group_count=GROUPS)
        ctx = jnp.einsum('nd,od->no', c, c_weight)
        out = out + ctx[:, :, None] + bias[None, :, None]
        return out

    def _L0_ffn_ref(x, W_org, lora_down, lora_up, lora_keys, Wq):
        import jax, jax.numpy as jnp
        import numpy as np
        import math
        B, S, IN, OUT = (4, 256, 512, 512)
        E, R, K = (8, 64, 128)
        SCALE = 64.0 / 64.0
        MULTIPLIER = 1.0
        base = jnp.einsum('bsi,oi->bso', x, W_org)
        q = jnp.einsum('bi,ki->bk', x.mean(axis=1), Wq)
        scores = jnp.einsum('bk,ek->be', q, lora_keys) / math.sqrt(K)
        coeffs = jax.nn.softmax(scores, axis=-1)
        h = jnp.einsum('bsi,eir->bser', x, lora_down)
        delta = jnp.einsum('be,bser,ero->bso', coeffs, h, lora_up)
        return base + delta * (SCALE * MULTIPLIER)

    def _L1_cond_ref(x, embedding, W0, b0, W1, b1, W2, b2, weight, bias_k):
        import jax, jax.numpy as jnp
        import numpy as np
        K = 8
        T = 1.0
        D_EMBD = 128
        IN_C = 32
        OUT_C = 32
        BS = 32
        H = 512
        HID = 128
        h = jax.nn.gelu(embedding @ W0 + b0, approximate=False)
        h = jax.nn.gelu(h @ W1 + b1, approximate=False)
        att = jax.nn.softmax((h @ W2 + b2) / T, axis=-1)
        agg_w = jnp.einsum('bk,koi->boi', att, weight[..., 0])
        agg_b = att @ bias_k
        out = jnp.einsum('boi,bih->boh', agg_w, x) + agg_b[:, :, None]
        return out

    def _L1_ffn_ref(x, A_w, B_w, Wq_w, keys):
        import jax, jax.numpy as jnp
        import numpy as np
        IN_F = 512
        OUT_F = 512
        RANK = 8
        NUM_EXPERTS = 64
        TOP_K = 16
        ROUTER_DIM = 16
        ALPHA = 32
        SCALING = ALPHA / TOP_K
        BOTTLENECK = NUM_EXPERTS * RANK
        q = jnp.einsum('bsd,rd->bsr', x, Wq_w)
        scores = jnp.einsum('bsr,er->bse', q, keys)
        top_vals, top_idx = jax.lax.top_k(scores, TOP_K)
        top_w = jax.nn.softmax(top_vals, axis=-1)
        gate = jnp.sum(jax.nn.one_hot(top_idx, NUM_EXPERTS, dtype=top_w.dtype) * top_w[..., None], axis=-2)
        z = jnp.einsum('bsd,nd->bsn', x, A_w)
        z = z.reshape(*z.shape[:-1], NUM_EXPERTS, RANK)
        z_gated = (z * gate[..., None]).reshape(*z.shape[:-2], BOTTLENECK)
        out = jnp.einsum('bsn,on->bso', z_gated, B_w) * SCALING
        return out

    def _L2_cond_ref(x, c, weight, c_weight, bias):
        import jax, jax.numpy as jnp
        import numpy as np
        from jax import lax
        N, C_IN, L = (32, 32, 512)
        C_OUT, K, GROUPS = (32, 9, 4)
        C_DIM, PAD, STRIDE = (128, 4, 1)
        out = lax.conv_general_dilated(x, weight, window_strides=(STRIDE,), padding=[(PAD, PAD)], dimension_numbers=('NCH', 'OIH', 'NCH'), feature_group_count=GROUPS)
        ctx = jnp.einsum('nd,od->no', c, c_weight)
        out = out + ctx[:, :, None] + bias[None, :, None]
        return out

    def _L2_ffn_ref(x, W, b, A, Bmat, LiMEs):
        import jax, jax.numpy as jnp
        import numpy as np
        NUM_EXPERTS = 8
        RANK = 32
        ALPHA = 16.0
        TOP_K = 2
        TEMPERATURE = 1.0
        GAMMA = 0.5
        SOFT_TOPK_TEMP = 0.5
        N_GRAM = 2
        EPS = 1e-06
        Bsz, T, d_in = x.shape
        E = LiMEs.shape[0]
        scaling = ALPHA / RANK
        H = jnp.einsum('btd,od->bto', x, W) + b
        z = jnp.einsum('btd,dr->btr', x, A)
        anchors = jnp.arange(N_GRAM - 1, T, N_GRAM)
        H_slice = H[:, anchors, :E]
        delta_slice = jnp.einsum('bar,er->bae', z[:, anchors], LiMEs)
        H_scale = jnp.maximum(jnp.max(jnp.abs(H_slice)), EPS)
        d_scale = jnp.maximum(jnp.max(jnp.abs(delta_slice)), EPS)
        logits = ((1.0 - GAMMA) * (H_slice / H_scale) + GAMMA * (delta_slice / d_scale)) / TEMPERATURE
        probs = jax.nn.softmax(logits, axis=-1)
        topk_vals, _ = jax.lax.top_k(probs, TOP_K)
        thresh = topk_vals[..., -1:]
        mask = jax.nn.sigmoid((probs - thresh) / SOFT_TOPK_TEMP)
        weights = probs * mask
        weights = weights / (jnp.sum(weights, axis=-1, keepdims=True) + 1e-09)
        weights_full = jnp.repeat(weights, N_GRAM, axis=1)
        p_mix = jnp.einsum('bte,er->btr', weights_full, LiMEs)
        delta = jnp.einsum('btr,ro->bto', z * p_mix, Bmat) * scaling
        return H + delta

    def _L3_cond_ref(x, embedding, W0, b0, W1, b1, W2, b2, weight, bias_k):
        import jax, jax.numpy as jnp
        import numpy as np
        K = 8
        T = 1.0
        D_EMBD = 128
        IN_C = 32
        OUT_C = 32
        BS = 32
        H = 512
        HID = 128
        h = jax.nn.gelu(embedding @ W0 + b0, approximate=False)
        h = jax.nn.gelu(h @ W1 + b1, approximate=False)
        att = jax.nn.softmax((h @ W2 + b2) / T, axis=-1)
        agg_w = jnp.einsum('bk,koi->boi', att, weight[..., 0])
        agg_b = att @ bias_k
        out = jnp.einsum('boi,bih->boh', agg_w, x) + agg_b[:, :, None]
        return out

    def _L3_ffn_ref(x, W, bias, A, Bf, coeffs, scales):
        import jax, jax.numpy as jnp
        import numpy as np
        out = jnp.einsum('bsd,od->bso', x, W) + bias
        xa = jnp.einsum('bsd,erd->ebsr', x, A)
        w = coeffs * scales
        upd = jnp.einsum('ebsr,eor,e->bso', xa, Bf, w)
        return out + upd
    x = x + _L0_ffn_ref(_L0_cond_ref(x, cond_128, L0_cond_weight, L0_cond_c_weight, fside_S_0), L0_ffn_W_org, L0_ffn_lora_down, L0_ffn_lora_up, L0_ffn_lora_keys, L0_ffn_Wq)
    x = x + _L1_ffn_ref(_L1_cond_ref(x, cond_128, L1_cond_W0, L1_cond_b0, L1_cond_W1, L1_cond_b1, L1_cond_W2, L1_cond_b2, L1_cond_weight, L1_cond_bias_k), L1_ffn_A_w, L1_ffn_B_w, L1_ffn_Wq_w, L1_ffn_keys)
    x = x + _L2_ffn_ref(_L2_cond_ref(x, cond_128, L2_cond_weight, L2_cond_c_weight, fside_S_0), L2_ffn_W, L2_ffn_b, L2_ffn_A, L2_ffn_Bmat, L2_ffn_LiMEs)
    x = x + _L3_ffn_ref(_L3_cond_ref(x, cond_128, L3_cond_W0, L3_cond_b0, L3_cond_W1, L3_cond_b1, L3_cond_W2, L3_cond_b2, L3_cond_weight, L3_cond_bias_k), L3_ffn_W, L3_ffn_bias, L3_ffn_A, L3_ffn_Bf, L3_ffn_coeffs, L3_ffn_scales)
    return x

_drawn_inputs = setup_inputs


def setup_inputs(seed=0):
    import zlib

    import numpy as np

    out = dict(_drawn_inputs(seed))
    spreads = {'L1_cond_b0': (0.0, 0.8),
     'L1_cond_b1': (0.0, 0.8),
     'L1_cond_b2': (0.0, 0.8),
     'L3_cond_b0': (0.0, 0.8),
     'L3_cond_b1': (0.0, 0.744),
     'L3_cond_b2': (0.0, 0.578),
     'L3_ffn_scales': (0.5, 0.6)}
    factors = {'L1_cond_W0': 8.0,
     'L1_cond_W1': 7.728,
     'L1_cond_W2': 7.525,
     'L1_cond_weight': 3.986,
     'L1_cond_bias_k': 8.0,
     'L1_ffn_A_w': 3.975,
     'L1_ffn_B_w': 3.815,
     'L1_ffn_Wq_w': 4.708,
     'L1_ffn_keys': 4.425,
     'L2_ffn_b': 200.0,
     'L2_ffn_A': 8.0,
     'L2_ffn_Bmat': 8.0,
     'L2_ffn_LiMEs': 8.0,
     'L3_cond_bias_k': 200.0,
     'L3_ffn_bias': 200.0,
     'L3_ffn_A': 2.885,
     'L3_ffn_Bf': 2.838,
     'L3_ffn_coeffs': 8.0,
     'L2_cond_c_weight': 2.671}
    for name, (base, spread) in spreads.items():
        noise = np.random.default_rng([zlib.crc32(name.encode()), seed]).standard_normal(out[name].shape)
        drawn = base * np.exp(spread * noise) if base else spread * noise
        out[name] = jnp.asarray(drawn.astype(out[name].dtype))
    for name, factor in factors.items():
        out[name] = (out[name] * factor).astype(out[name].dtype)
    return out
```

```python
from contextlib import ExitStack

import concourse.bass as bass
from concourse import mybir

ALU = mybir.AluOpType
ACT = mybir.ActivationFunctionType
AX = mybir.AxisListType
F32 = mybir.dt.float32
F32R = mybir.dt.float32r

P = 128
B, S, D = 64, 32, 512
R, M = 4, 128
TB = P // S
NT = B // TB
G = 4
NG = NT // G
GB = G * TB
E0 = 8
K1 = 8
E1, RANK1 = 64, 8
Z2, E2 = 32, 8
SLICES = Z2 + 2 * E2
EPS = 1e-6
TAKEN = -3.0e38

C_IDENT, C_EYE2, C_BLK, C_TILE, C_MOD = 0, 128, 192, 196, 212
C_ALL = 216


def build(nc, t_in, out, scratch):
    ctx = ExitStack()
    with ctx:
        def sb(name, shape, dt=F32):
            return ctx.enter_context(nc.sbuf_tensor(name, shape, dt))

        def sem(name):
            return ctx.enter_context(nc.semaphore(name))

        WA_at = -(-nc.sbuf_base // 32) * 32
        WA = [[sb(f"wa{j}_{h}", [P, 4, D], F32R) for h in ("hi", "lo")] for j in range(3)]
        WB_at = -(-nc.sbuf_base // 32) * 32
        WB = [[sb(f"wb{j}_{h}", [P, 4, D], F32R) for h in ("hi", "lo")] for j in range(2)]
        worg, lora_dn, lora_up = WA
        w2, w3 = WA[0], WA[1]
        a1, b1 = WB

        ST_at = -(-nc.sbuf_base // 32) * 32
        ST = [sb(f"st_{h}", [P, G, D], F32R) for h in ("hi", "lo")]

        def over(name, shape, at, room_at, room):
            size = 4
            for n in shape[1:]:
                size *= n
            assert at + size <= room
            return nc.alloc_sbuf_tensor_at(name, shape, F32, offset=room_at + at)

        def over_wb(name, shape, at):
            return over(name, shape, at, WB_at, 4 * 4 * D * 4)

        def over_st(name, shape, at):
            return over(name, shape, at, ST_at, 2 * G * D * 4)

        def over_up(name, shape, at):
            return over(name, shape, WA_ROOM + at, WA_at, 3 * WA_ROOM // 2)

        KB = 1024
        WA_ROOM = 2 * 2 * 4 * D * 4
        raw_dn = over_wb("raw_dn", [P, 4, D], 0)
        kmix = over_wb("kmix", [TB * K1, S, P], 8 * KB)
        raw_up = over_wb("raw_up", [P, 4, D], 24 * KB)
        z2 = over_wb("z2", [Z2, NT * P], 0)
        w3_raw = over_wb("w3_raw", [P, 4, D], 24 * KB)
        a3_raw = over_st("a3_raw", [P, 2, D], 0)
        b3_raw = over_st("b3_raw", [P, 2, D], 4 * KB)
        b3_scaled = over_st("b3_scaled", [P, 2, D], 8 * KB)
        w2T = over_st("w2T", [E2, G * P], 12 * KB)
        bmat = over_st("bmat", [Z2 + 1, D], 14 * KB)
        g1, g2, ge, gate = (over_up(n, [P, G, E1], j * KB) for j, n in enumerate(("g1", "g2", "ge", "gate")))
        sl_ring = over_up("sl_ring", [SLICES, G * P], 4 * KB)
        zp = over_up("zp", [Z2 + 1, G * P], 6 * KB)
        lg = over_up("lg", [P, 8, NT, E2], 8 * KB)
        anc = over_up("anc", [P, NT, 2 * E2], 12 * KB)
        ltop = over_up("ltop", [P, NT, 8], 13 * KB)
        wq0 = over_st("wq0", [P, D], 0)
        wq1 = over_st("wq1", [16, D], 2 * KB)
        a2T = over_st("a2T", [Z2, D], 4 * KB)
        mw = over_st("mw", [P, 2, 2, P], 6 * KB)
        hid = over_st("hid", [P, 2, 2, P], 8 * KB)
        slice_raw = over_st("slice_raw", [P, R, SLICES], 10 * KB)
        bias3_f = over_st("bias3_f", [2, D], 11 * KB)

        x = sb("x", [P, NT, D])
        F = sb("F", [P, G, D])
        Y = [sb(f"y_{h}", [P, R, G * P], F32R) for h in ("hi", "lo")]
        xf = sb("xf", [P, G, TB, M])
        XH = [sb(f"xhat_{h}", [P, 2, TB, M + 2], F32R) for h in ("hi", "lo")]
        conv_w = [[sb(f"conv{j}_{h}", [P, 3, P], F32R) for h in ("hi", "lo")] for j in range(2)]
        mix_at = -(-nc.sbuf_base // 32) * 32
        mix_f = sb("mix_f", [P, G, P])
        sc_p = over("sc_p", [GB, E0, 64], 0, mix_at, G * P * 4)
        MX = [sb(f"mix_{h}", [P, G, P], F32R) for h in ("hi", "lo")]
        agg = sb("agg", [P, 2, S, NT])
        rows = sb("rows", [P, 4, S])
        diag = sb("diag", [P, GB * S], F32R)
        added = sb("added", [P, G * P])
        stage = sb("stage", [P, 2, D])

        cst = sb("cst", [P, C_ALL])
        ident = cst[:, C_IDENT:C_IDENT + P]
        ones_r = sb("ones_r", [P, P], F32R)
        ones = sb("ones", [1, P])
        condT = sb("condT", [P, P])
        cw = sb("cw", [P, 2, S])
        fside = sb("fside", [1, S])
        keys0 = sb("keys0", [P, E0])
        kq0 = sb("kq0", [P, R, E0])
        keys1 = sb("keys1", [16, E1])
        KQ1 = [sb(f"kq1_{h}", [P, R, E1], F32R) for h in ("hi", "lo")]
        limesT = sb("limesT", [Z2, E2])
        limes = sb("limes", [E2, Z2])
        SLW = [sb(f"slice_{h}", [P, R, 96], F32R) for h in ("hi", "lo")]
        slice_bias = sb("slice_bias", [SLICES, 1])
        bias3 = sb("bias3", [2, D], F32R)
        mb = sb("mb", [P, 2, 2])
        mw2 = sb("mw2", [P, 2, K1])
        mb2 = sb("mb2", [1, 2, K1])
        mbk = sb("mbk", [K1, 2, S])
        att_nm = sb("att_nm", [P, 2])
        att_e = sb("att_e", [P, 2, K1])
        att_s = sb("att_s", [P, 2])
        att_r = sb("att_r", [P, 2])
        att = sb("att", [P, 2, K1])
        attT = sb("attT", [K1, 2, P])
        attm = sb("attm", [B, 2, TB, K1])
        attk = sb("attk", [TB * K1, 2, NT])
        row_hi = sb("row_hi", [P, 4, S], F32R)
        ysum = sb("ysum", [P, R, GB])
        sc_nm = sb("sc_nm", [GB, 1])
        sc_e = sb("sc_e", [GB, E0])
        sc_s = sb("sc_s", [GB, 1])
        sc_r = sb("sc_r", [GB, 1])
        coef = sb("coef", [P, 4, GB])
        top = sb("top", [P, G, 2, 8])
        g_nm = sb("g_nm", [P, G])
        g_s = sb("g_s", [P, G])
        g_r = sb("g_r", [P, G])
        amax = sb("amax", [P, 2])
        amax_all = sb("amax_all", [P, 2])
        ascale = sb("ascale", [P, 2])
        arecip = sb("arecip", [P, 2])
        lgs = sb("lgs", [P, 4, NT])
        e3s = sb("e3s", [P, 3, 2])

        pb = [ctx.enter_context(nc.psum_tensor(f"bank{i}", [P, D], F32)) for i in range(8)]

        NAMES = """cst_in cond_in w0_in kmix_in small_in x_in stage_in w2s_in out_done spill_done b3_in
            tables_ps tables_sb rows_ps rows_hi rows_lo raw0_hi raw0_lo conv_w_hi hid_ps hid_sb
            att_ps att_max att_exp att_inv att_ready attT_ps attT_sb attm_ready attk_ps attk_sb
            agg_ps agg_sb ones_set slice_raw_in slice_w_hi slice_w_lo kq1_hi kq1_lo tables0_sb raw_alt_sb
            xh_hi xh_lo y_ps y_f y_hi y_lo ysum_done diag_ready row_bc added_ready
            sc0_ps sc0_max sc0_exp sc0_inv coef_p coef_ps coef_sb h_ps h_f h_hi h_lo ff_ps x_new
            stage_hi stage_lo mix_f_ready mix_hi mix_lo st_hi st_lo sc1_ps sc1_sb top_a took_a top_b took_b
            top_neg gate_exp gate_sum gate_ready z_ps zg_f zt_ps zt_hi zt_lo
            sl_ps sl_sb z2_sb anc_ps anc_sb anc_max anc_all anc_eps anc_inv
            lg_step lg_exp lg_sig w_ready wT_ps wT_sb pm_ps zp_ready e3_ready b3_ready w3_ps w3_f w3_hi w3_lo
            bias3_in bias3_hi border_set zp_one""".split()
        s = {n: sem(n) for n in NAMES}

        xf_in = [sem(f"xf_in{t}") for t in range(G)]

        block = ctx.enter_context(nc.Block())

        def upto(layer, i, t):
            return G * i + (layer * NT + t + 1)

        def x_upto(layer, i, t):
            return G * i + ((layer + (layer == 3)) * NT + t + 1)

        def alone(eng):
            eng.wait_ge(s["cst_in"], 16)

        @block.sync
        def _(sp):
            sp.dma_start(cst[:, :], t_in["cst"]).then_inc(s["cst_in"], 16)
            sp.dma_start(condT[:, :], t_in["condT"]).then_inc(s["cond_in"], 16)
            sp.dma_start(cw[:, :, :], t_in["cw"]).then_inc(s["cond_in"], 16)
            sp.dma_start(fside[:, :], t_in["fside"]).then_inc(s["cond_in"], 16)
            sp.dma_start(stage[:, 0, 0:3 * P], t_in["conv0"]).then_inc(s["cond_in"], 16)
            sp.dma_start(stage[:, 1, 0:3 * P], t_in["conv2"]).then_inc(s["cond_in"], 16)
            xh_dram = t_in["x"].rearrange("(n b) i r m -> n (i r) b m", b=TB)
            for t in range(G):
                sp.dma_start(xf[:, t], xh_dram[t]).then_inc(xf_in[t], 16)
            sp.dma_start(F[:, :, :], t_in["worg"]).then_inc(s["w0_in"], 16)
            sp.dma_start(wq0[:, :], t_in["wq0"]).then_inc(s["small_in"], 16)
            sp.dma_start(keys0[:, :], t_in["keys0"]).then_inc(s["small_in"], 16)
            sp.dma_start(raw_dn[:, :, :], t_in["lora_dn"]).then_inc(s["w0_in"], 16)
            sp.dma_start(raw_up[:, :, :], t_in["lora_up"]).then_inc(s["w0_in"], 16)
            x_tok = t_in["x"].rearrange("(n b) i r m -> (b i) n (r m)", b=TB)
            for i in range(NG):
                sp.dma_start(x[:, G * i:G * i + G, :], x_tok[:, G * i:G * i + G, :]).then_inc(s["x_in"], 16)
            xh_rest = t_in["x"].rearrange("(n b) i r m -> n (i r) b m", b=TB)
            a1_dram = t_in["a1"].rearrange("p (c n) -> p c n", c=4)
            b1_dram = t_in["b1"].rearrange("p (c n) -> p c n", c=4)
            with sp.Fori(0, NG - 1) as i:
                sp.wait_ge(s["stage_lo"], 2 * i + 2)
                for j, w in enumerate((a1_dram, b1_dram)):
                    sp.dma_start(stage[:, j], w[:, bass.ds(i, 1), :].rearrange("p a n -> p (a n)")).then_inc(s["stage_in"], 16)
                for t in range(G):
                    sp.wait_ge(s["xh_lo"], upto(0, i, t))
                    sp.dma_start(xf[:, t], xh_rest[bass.ds(i * G + (G + t), 1)].rearrange("a p b m -> (a p) b m")).then_inc(xf_in[t], 16)
            sp.wait_ge(s["stage_lo"], 2 * NG)
            for j, w in enumerate((a1_dram, b1_dram)):
                sp.dma_start(stage[:, j], w[:, NG - 1, :]).then_inc(s["stage_in"], 16)
            spill = scratch.rearrange("(n b) i r m -> n (b i) (r m)", b=TB)
            refill = scratch.rearrange("(n b) i r m -> n (i r) b m", b=TB)
            w2_dram = t_in["w2"].rearrange("p (c n) -> p c n", c=4)
            with sp.Fori(0, NG - 1) as i:
                sp.wait_ge(s["stage_lo"], i + (2 * NG + 2))
                sp.dma_start(stage[:, 0], w2_dram[:, bass.ds(i, 1), :].rearrange("p a n -> p (a n)")).then_inc(s["w2s_in"], 16)
                for t in range(G):
                    sp.wait_ge(s["x_new"], x_upto(1, i, t))
                    sp.dma_start(spill[bass.ds(i * G + t, 1)].rearrange("a p n -> (a p) n"),
                                 x[:, bass.ds(i * G + t, 1), :].rearrange("p a n -> p (a n)")).then_inc(s["spill_done"], 16)
            sp.wait_ge(s["stage_lo"], 3 * NG + 1)
            sp.dma_start(stage[:, 0], w2_dram[:, NG - 1, :]).then_inc(s["w2s_in"], 16)
            sp.wait_ge(s["xh_lo"], NT)
            for t in range(G):
                sp.wait_ge(s["spill_done"], 16 * (NT - G))
                sp.dma_start(xf[:, t], refill[t]).then_inc(xf_in[t], 16)
            for t in range(G):
                sp.wait_ge(s["x_new"], x_upto(1, NG - 1, t))
                sp.dma_start(spill[NT - G + t], x[:, NT - G + t, :]).then_inc(s["spill_done"], 16)
            sp.dma_start(a3_raw[:, :, :], t_in["a3"]).then_inc(s["b3_in"], 16)
            sp.dma_start(b3_raw[:, :, :], t_in["b3"]).then_inc(s["b3_in"], 16)
            sp.dma_start(w3_raw[:, :, :], t_in["w3"]).then_inc(s["b3_in"], 16)
            sp.dma_start(bmat[:, :], t_in["bmat"]).then_inc(s["b3_in"], 16)
            sp.dma_start(kmix[:, :, :], t_in["kmix3"]).then_inc(s["kmix_in"], 16)
            sp.wait_ge(s["spill_done"], 16 * NT)
            with sp.Fori(0, NG - 1) as i:
                for t in range(G):
                    sp.wait_ge(s["xh_lo"], upto(1, i, t))
                    sp.dma_start(xf[:, t], refill[bass.ds(i * G + (G + t), 1)].rearrange("a p b m -> (a p) b m")).then_inc(xf_in[t], 16)
            out_tok = out.rearrange("(n b) i r m -> n (b i) (r m)", b=TB)
            with sp.Fori(0, NG) as i:
                for t in range(G):
                    sp.wait_ge(s["x_new"], x_upto(3, i, t))
                    sp.dma_start(out_tok[bass.ds(i * G + t, 1)].rearrange("a p n -> (a p) n"),
                                 x[:, bass.ds(i * G + t, 1), :].rearrange("p a n -> p (a n)")).then_inc(s["out_done"], 16)
            sp.wait_ge(s["out_done"], 16 * NT)

        @block.scalar
        def _(act):
            copy = nc.scalar.activation

            for dst, name in ((mw[:, :, :, :], "mw"), (mb[:, :, :], "mb"), (mw2[:, :, :], "mw2"),
                              (mb2[:, :, :], "mb2"), (mbk[:, :, :], "mbk")):
                act.dma_start(dst, t_in[name]).then_inc(s["small_in"], 16)
            act.dma_start(kmix[:, :, :], t_in["kmix1"]).then_inc(s["kmix_in"], 16)
            for dst, name in ((wq1[:, :], "wq1"), (keys1[:, :], "keys1"), (a2T[:, :], "a2T"), (limesT[:, :], "limesT"),
                              (limes[:, :], "limes"), (slice_bias[:, :], "slice_bias"),
                              (e3s[:, 0:2, :], "e3s")):
                act.dma_start(dst, t_in[name]).then_inc(s["small_in"], 16)
            act.dma_start(slice_raw[:, :, 0:Z2], t_in["a2"]).then_inc(s["slice_raw_in"], 16)
            act.dma_start(slice_raw[:, :, Z2 + E2:SLICES], t_in["w2slice"]).then_inc(s["slice_raw_in"], 16)
            act.dma_start(bias3_f[:, :], t_in["bias3"]).then_inc(s["bias3_in"], 16)

            act.wait_ge(s["cond_in"], 5 * 16)
            for j in range(2):
                copy(conv_w[j][0][:, :, :].rearrange("p a n -> p (a n)"), stage[:, j, 0:3 * P], ACT.Copy).then_inc(s["conv_w_hi"], 1)
            act.wait_ge(s["rows_ps"], 2)
            for j, layer in enumerate((0, 2)):
                copy(row_hi[:, layer, :], pb[j][:, 0:S], ACT.Copy).then_inc(s["rows_hi"], 1)

            def xhat_hi(layer, i, t):
                act.wait_ge(xf_in[t], 16 * i + 16 * (layer // 2 * NG + 1))
                copy(XH[0][:, t % 2, :, 1:M + 1], xf[:, t], ACT.Copy).then_inc(s["xh_hi"], 1)

            for j, raw in enumerate((F, raw_dn, raw_up)):
                act.wait_ge(s["w0_in"], 16 * 3)
                copy(WA[j][0][:, :, :], raw[:, :, :], ACT.Copy).then_inc(s["raw0_hi"], 1)
            act.wait_ge(s["tables_ps"], 1)
            copy(kq0[:, :, :], pb[2][:, 0:R * E0].rearrange("p (r e) -> p r e", r=R), ACT.Copy,
                 scale=1.0 / (S * float(P) ** 0.5)).then_inc(s["tables0_sb"], 1)
            copy(KQ1[0][:, :, :], pb[3][:, 0:R * E1].rearrange("p (r e) -> p r e", r=R), ACT.Copy).then_inc(s["kq1_hi"], 1)
            act.wait_ge(s["slice_raw_in"], 32)
            copy(slice_raw[:, :, Z2:Z2 + E2], pb[2][:, 64:64 + R * E2].rearrange("p (r e) -> p r e", r=R), ACT.Copy)\
                .then_inc(s["raw_alt_sb"], 1)
            act.wait_ge(s["raw_alt_sb"], 1)
            act.wait_ge(s["border_set"], 3)
            copy(SLW[0][:, :, 0:SLICES], slice_raw[:, :, :], ACT.Copy).then_inc(s["slice_w_hi"], 1)

            for j in range(2):
                for k in range(2):
                    act.wait_ge(s["hid_ps"], 2 * j + k + 1)
                    copy(hid[:, j, k, :], pb[4][:, 0:P], ACT.Gelu, bias=mb[:, j, k:k + 1]).then_inc(s["hid_sb"], 1)
            for j in range(2):
                act.wait_ge(s["att_max"], 2)
                copy(att_e[:, j, :], pb[5][:, j * K1:(j + 1) * K1], ACT.Exp, bias=att_nm[:, j:j + 1],
                     accum_out=att_s[:, j:j + 1]).then_inc(s["att_exp"], 1)
            for j in range(2):
                act.wait_ge(s["attT_ps"], j + 1)
                copy(attT[:, j, :], pb[6][0:K1, j * P:(j + 1) * P], ACT.Copy).then_inc(s["attT_sb"], 1)
                act.wait_ge(s["attk_ps"], j + 1)
                copy(attk[:, j, :], pb[7][0:TB * K1, j * NT:(j + 1) * NT], ACT.Copy).then_inc(s["attk_sb"], 1)
            act.wait_ge(s["rows_ps"], 4)
            for j, layer in enumerate((1, 3)):
                copy(row_hi[:, layer, :], pb[j][:, 0:S], ACT.Copy).then_inc(s["rows_hi"], 1)
            act.wait_ge(s["agg_ps"], 1)
            copy(agg[:, 0], pb[2][:, :].rearrange("p (o n) -> p o n", o=S), ACT.Copy).then_inc(s["agg_sb"], 1)

            def added_copy(layer, i, bank):
                act.wait_ge(s["row_bc"], i + (layer * NG + 1))
                copy(added[:, :], pb[bank][:, :], ACT.Copy).then_inc(s["added_ready"], 1)

            def y_hi(layer, i, t):
                act.wait_ge(s["y_f"], upto(layer, i, t))
                copy(Y[0][:, :, t * P:(t + 1) * P], F[:, t].rearrange("p (r n) -> p r n", r=R), ACT.Copy).then_inc(s["y_hi"], 1)

            def conv_layer(layer, i):
                for t in range(2):
                    xhat_hi(layer, i, t)
                act.wait_ge(s["y_ps"], upto(layer, i, 0))
                xhat_hi(layer, i, 2)
                added_copy(layer, i, 4)
                y_hi(layer, i, 0)
                act.wait_ge(s["y_ps"], upto(layer, i, 1))
                xhat_hi(layer, i, 3)
                for t in range(1, G):
                    y_hi(layer, i, t)

            def stage_hi(dst, i, slot):
                copy(dst[:, bass.ds(i, 1), :].rearrange("p a n -> p (a n)"), stage[:, slot], ACT.Copy).then_inc(s["stage_hi"], 1)

            with act.Fori(0, NG) as i:
                conv_layer(0, i)
                act.wait_ge(s["sc0_max"], i + 1)
                copy(sc_e[:, :], pb[0][0:GB, 0:E0], ACT.Exp, bias=sc_nm[:, 0:1], accum_out=sc_s[:, 0:1]).then_inc(s["sc0_exp"], 1)
                act.wait_ge(s["coef_ps"], i + 1)
                copy(coef[:, :, :], pb[1][:, 0:4 * GB].rearrange("p (c b) -> p c b", c=4), ACT.Copy).then_inc(s["coef_sb"], 1)
                for c in range(4):
                    act.wait_ge(s["h_f"], 4 * i + (c + 1))
                    copy(ST[0][:, c], F[:, c], ACT.Copy).then_inc(s["h_hi"], 1)
                act.wait_ge(s["raw0_lo"], 3)
                act.wait_ge(s["stage_in"], 32 * i + 32)
                stage_hi(a1[0], i, 0)
                stage_hi(b1[0], i, 1)

            def mix_layer(layer, i):
                for t in range(G):
                    act.wait_ge(s["mix_f_ready"], upto(layer // 2, i, t))
                    copy(MX[0][:, t], mix_f[:, t], ACT.Copy).then_inc(s["mix_hi"], 1)
                    if layer == 1:
                        act.wait_ge(s["x_new"], x_upto(layer, i, t) - G)
                    copy(ST[0][:, t], x[:, bass.ds(i * G + t, 1), :].rearrange("p a n -> p (a n)"), ACT.Copy).then_inc(s["st_hi"], 1)
                    if t == 0:
                        added_copy(layer, i, 0)
                for t in range(G):
                    y_hi(layer, i, t)

            with act.Fori(0, NG) as i:
                mix_layer(1, i)
                for t in range(G):
                    act.wait_ge(s["top_neg"], G * i + (t + 1))
                    copy(ge[:, t], pb[4 + t][:, 0:E1], ACT.Exp, bias=g_nm[:, t:t + 1]).then_inc(s["gate_exp"], 1)
                act.wait_ge(s["w2s_in"], 16 * i + 16)
                stage_hi(w2[0], i, 0)
                for t in range(G):
                    act.wait_ge(s["zt_ps"], G * i + (t + 1))
                    copy(ST[0][:, t], pb[4 + t][:, :], ACT.Copy).then_inc(s["zt_hi"], 1)

            with act.Fori(0, NG) as i:
                conv_layer(2, i)
                act.wait_ge(s["sl_ps"], i + 1)
                copy(sl_ring[Z2:SLICES, :].rearrange("p (j two) -> p j two", two=2),
                     pb[4][Z2:SLICES, :].rearrange("p (j two) -> p j two", two=2)[:, :, 1:2].broadcast_to((2 * E2, G * P // 2, 2)), ACT.Identity, bias=slice_bias[Z2:SLICES, 0:1]).then_inc(s["sl_sb"], 1)

            act.wait_ge(s["agg_ps"], 2)
            copy(agg[:, 1], pb[2][:, :].rearrange("p (o n) -> p o n", o=S), ACT.Copy).then_inc(s["agg_sb"], 1)
            act.wait_ge(s["lg_step"], 4)
            copy(lg[:, 3], lg[:, 2], ACT.Exp).then_inc(s["lg_exp"], 1)
            act.wait_ge(s["lg_step"], 8)
            copy(lg[:, 6], lg[:, 5], ACT.Exp, scale=-2.0).then_inc(s["lg_sig"], 1)
            for i in range(NG):
                act.wait_ge(s["wT_ps"], i + 1)
                copy(w2T[:, :], pb[0][0:E2, :], ACT.Copy).then_inc(s["wT_sb"], 1)
            for c in range(4):
                act.wait_ge(s["w3_f"], c + 1)
                copy(w3[0][:, c], F[:, c], ACT.Copy).then_inc(s["w3_hi"], 1)

            act.wait_ge(s["x_new"], 4 * NT)
            with act.Fori(0, NG) as i:
                mix_layer(3, i)

        @block.gpsimd
        def _(pool):
            def lo(dst, v, hi):
                return nc.gpsimd.tensor_tensor(dst, v, hi.bitcast(F32), ALU.subtract)

            nc.gpsimd.memset(ones[:, :], 1.0).then_inc(s["ones_set"], 1)
            for j in range(2):
                pool.wait_ge(s["conv_w_hi"], j + 1)
                lo(conv_w[j][1][:, :, :].rearrange("p a n -> p (a n)"), stage[:, j, 0:3 * P],
                   conv_w[j][0][:, :, :].rearrange("p a n -> p (a n)")).then_inc(s["stage_lo"], 1)

            def xhat_lo(layer, i, t):
                pool.wait_ge(s["xh_hi"], upto(layer // 2, i, t))
                lo(XH[1][:, t % 2, :, 1:M + 1], xf[:, t], XH[0][:, t % 2, :, 1:M + 1]).then_inc(s["xh_lo"], 1)

            def y_lo(layer, i, t):
                pool.wait_ge(s["y_hi"], upto(layer, i, t))
                lo(Y[1][:, :, t * P:(t + 1) * P], F[:, t].rearrange("p (r n) -> p r n", r=R),
                   Y[0][:, :, t * P:(t + 1) * P]).then_inc(s["y_lo"], 1)

            def conv_layer(layer, i):
                for t in range(2):
                    xhat_lo(layer, i, t)
                xhat_lo(layer, i, 2)
                y_lo(layer, i, 0)
                xhat_lo(layer, i, 3)
                for t in range(1, G):
                    y_lo(layer, i, t)

            def stage_lo(dst_hi, dst_lo, i, slot):
                lo(dst_lo[:, bass.ds(i, 1), :].rearrange("p a n -> p (a n)"), stage[:, slot],
                   dst_hi[:, bass.ds(i, 1), :].rearrange("p a n -> p (a n)")).then_inc(s["stage_lo"], 1)

            with pool.Fori(0, NG) as i:
                conv_layer(0, i)
                for c in range(4):
                    pool.wait_ge(s["h_hi"], 4 * i + (c + 1))
                    lo(ST[1][:, c], F[:, c], ST[0][:, c]).then_inc(s["h_lo"], 1)
                for j, w in enumerate((a1, b1)):
                    pool.wait_ge(s["stage_hi"], 2 * i + (j + 1))
                    stage_lo(w[0], w[1], i, j)

            def mix_layer(layer, i):
                for t in range(G):
                    pool.wait_ge(s["mix_hi"], upto(layer // 2, i, t))
                    lo(MX[1][:, t], mix_f[:, t], MX[0][:, t]).then_inc(s["mix_lo"], 1)
                    pool.wait_ge(s["st_hi"], upto(layer // 2, i, t))
                    lo(ST[1][:, t], x[:, bass.ds(i * G + t, 1), :].rearrange("p a n -> p (a n)"), ST[0][:, t]).then_inc(s["st_lo"], 1)
                for t in range(G):
                    y_lo(layer, i, t)

            with pool.Fori(0, NG) as i:
                mix_layer(1, i)
                pool.wait_ge(s["stage_hi"], i + (2 * NG + 1))
                stage_lo(w2[0], w2[1], i, 0)

            pool.wait_ge(s["stage_lo"], 3 * NG + 2)
            nc.gpsimd.memset(zp[Z2:Z2 + 1, :], 1.0).then_inc(s["zp_one"], 1)
            pool.wait_ge(s["zp_one"], 1)
            with pool.Fori(0, NG) as i:
                conv_layer(2, i)

            pool.wait_ge(s["anc_max"], 2)
            nc.gpsimd.partition_all_reduce(amax_all[:, :], amax[:, :], P, bass.bass_isa.ReduceOp.max).then_inc(s["anc_all"], 1)
            for c in range(4):
                pool.wait_ge(s["w3_hi"], c + 1)
                lo(w3[1][:, c], F[:, c], w3[0][:, c]).then_inc(s["w3_lo"], 1)

            with pool.Fori(0, NG) as i:
                mix_layer(3, i)

        @block.vector
        def _(dve):
            tt, stt, ts = nc.vector.tensor_tensor, nc.vector.scalar_tensor_tensor, nc.vector.tensor_scalar

            for h in range(2):
                nc.vector.memset(XH[h][:, :, :, 0:M + 2:M + 1].bitcast(F32), 0.0).then_inc(s["border_set"], 1)
            for h in range(2):
                nc.vector.memset(SLW[h][:, :, :].bitcast(F32), 0.0).then_inc(s["border_set"], 1)
            nc.vector.memset(ones_r[:, :].bitcast(F32), 1.0).then_inc(s["ones_set"], 1)

            def rows_split(layer, bank, n):
                dve.wait_ge(s["rows_hi"], n)
                nc.vector.tensor_copy(rows[0:B, layer, :], row_hi[0:B, layer, :].bitcast(F32)).then_inc(s["rows_lo"], 1)
                tt(rows[B:P, layer, :], pb[bank][B:P, 0:S], row_hi[B:P, layer, :].bitcast(F32), ALU.subtract)\
                    .then_inc(s["rows_lo"], 1)

            dve.wait_ge(s["cst_in"], 16)
            rows_split(0, 0, 1)
            rows_split(2, 1, 2)
            for j, raw in enumerate((F, raw_dn, raw_up)):
                dve.wait_ge(s["raw0_hi"], j + 1)
                tt(WA[j][1][:, :, :], raw[:, :, :], WA[j][0][:, :, :].bitcast(F32), ALU.subtract).then_inc(s["raw0_lo"], 1)
            dve.wait_ge(s["kq1_hi"], 1)
            tt(KQ1[1][:, :, :], pb[3][:, 0:R * E1].rearrange("p (r e) -> p r e", r=R), KQ1[0][:, :, :].bitcast(F32),
               ALU.subtract).then_inc(s["kq1_lo"], 1)
            dve.wait_ge(s["slice_w_hi"], 1)
            tt(SLW[1][:, :, 0:SLICES], slice_raw[:, :, :], SLW[0][:, :, 0:SLICES].bitcast(F32), ALU.subtract).then_inc(s["slice_w_lo"], 1)
            dve.wait_ge(s["bias3_in"], 16)
            nc.vector.tensor_copy(bias3[:, :], bias3_f[:, :]).then_inc(s["bias3_hi"], 1)
            dve.wait_ge(s["small_in"], 16 * 14)
            tt(e3s[:, 2, :], e3s[:, 0, :], e3s[:, 1, :], ALU.mult).then_inc(s["e3_ready"], 1)

            for j in range(2):
                dve.wait_ge(s["att_ps"], 1)
                nc.vector.reduce_max(att_nm[:, j:j + 1], pb[5][:, j * K1:(j + 1) * K1], AX.X, negate=True).then_inc(s["att_max"], 1)
            for j in range(2):
                dve.wait_ge(s["att_exp"], j + 1)
                nc.vector.reciprocal(att_r[:, j:j + 1], att_s[:, j:j + 1]).then_inc(s["att_inv"], 1)
                dve.wait_ge(s["att_inv"], j + 1)
                ts(att[:, j, :], att_e[:, j, :], att_r[:, j:j + 1], None, ALU.mult).then_inc(s["att_ready"], 1)
                dve.wait_ge(s["att_ready"], j + 1)
                tt(attm[:, j], att[0:B, j, :].unsqueeze(1).broadcast_to((B, TB, K1)),
                   cst[0:B, C_MOD:C_MOD + TB].unsqueeze(2).broadcast_to((B, TB, K1)), ALU.mult).then_inc(s["attm_ready"], 1)
            rows_split(1, 0, 3)
            rows_split(3, 1, 4)

            def diag_make(layer, i):
                tt(diag[:, :].rearrange("p (b o) -> p b o", b=GB),
                   cst[:, bass.ds(i * GB + C_EYE2, GB)].unsqueeze(2).broadcast_to((P, GB, S)),
                   rows[:, layer, :].unsqueeze(1).broadcast_to((P, GB, S)), ALU.mult).then_inc(s["diag_ready"], 1)

            def conv_y(layer, i, t):
                dve.wait_ge(s["y_ps"], upto(layer, i, t))
                if t == 0:
                    dve.wait_ge(s["added_ready"], i + (layer * NG + 1))
                tt(F[:, t].rearrange("p (r b o) -> p b r o", r=R, b=TB),
                   pb[t][:, :].rearrange("p (b r o) -> p b r o", b=TB, r=R),
                   added[:, t * P:(t + 1) * P].rearrange("p (b o) -> p b o", b=TB).unsqueeze(2).broadcast_to((P, TB, R, S)),
                   ALU.add).then_inc(s["y_f"], 1)

            def add_to_x(layer, i, t, bank, scale=None):
                dve.wait_ge(s["ff_ps"], x_upto(layer, i, t))
                xt = x[:, bass.ds(i * G + t, 1), :].rearrange("p a n -> p (a n)")
                if scale:
                    stt(xt, pb[bank][:, :], scale, xt, ALU.mult, ALU.add).then_inc(s["x_new"], 1)
                else:
                    tt(xt, pb[bank][:, :], xt, ALU.add).then_inc(s["x_new"], 1)

            dve.wait_ge(s["rows_lo"], 8)
            with dve.Fori(0, NG) as i:
                diag_make(0, i)
                for t in range(G):
                    conv_y(0, i, t)
                    dve.wait_ge(s["y_f"], upto(0, i, t))
                    nc.vector.reduce_sum(ysum[:, :, t * TB:(t + 1) * TB], F[:, t].rearrange("p (r b o) -> p r b o", r=R, b=TB),
                                         AX.X).then_inc(s["ysum_done"], 1)
                dve.wait_ge(s["sc0_ps"], i + 1)
                nc.vector.reduce_max(sc_nm[:, :], pb[0][0:GB, 0:E0], AX.X, negate=True).then_inc(s["sc0_max"], 1)
                dve.wait_ge(s["sc0_exp"], i + 1)
                nc.vector.reciprocal(sc_r[:, :], sc_s[:, :]).then_inc(s["sc0_inv"], 1)
                dve.wait_ge(s["sc0_inv"], i + 1)
                ts(sc_p[:, :, :], sc_e[:, :].unsqueeze(2).broadcast_to((GB, E0, 64)), sc_r[:, 0:1], None, ALU.mult).then_inc(s["coef_p"], 1)
                dve.wait_ge(s["coef_sb"], i + 1)
                for c in range(4):
                    dve.wait_ge(s["h_ps"], 4 * i + (c + 1))
                    tt(F[:, c].rearrange("p (b o) -> p b o", b=GB), pb[(c + 2) % 4][:, :].rearrange("p (b o) -> p b o", b=GB),
                       coef[:, c, :].unsqueeze(2).broadcast_to((P, GB, S)), ALU.mult).then_inc(s["h_f"], 1)
                dve.wait_ge(s["x_in"], 16 * NG)
                for t in range(G):
                    add_to_x(0, i, t, 4 + t)

            def mix_y(layer, i):
                dve.wait_ge(s["agg_sb"], layer // 2 + 1)
                diag_make(layer, i)
                for t in range(G):
                    tt(mix_f[:, t].rearrange("p (b o) -> p b o", b=TB),
                       agg[:, layer // 2, :, bass.ds(i * G + t, 1)].rearrange("p o a -> p a o").broadcast_to((P, TB, S)),
                       cst[:, C_BLK:C_BLK + TB].unsqueeze(2).broadcast_to((P, TB, S)), ALU.mult).then_inc(s["mix_f_ready"], 1)
                dve.wait_ge(s["added_ready"], i + (layer * NG + 1))
                for t in range(G):
                    dve.wait_ge(s["y_ps"], upto(layer, i, t))
                    tt(F[:, t].rearrange("p (r n) -> p r n", r=R), pb[(t + 1) % 4][:, :].rearrange("p (r n) -> p r n", r=R),
                       added[:, t * P:(t + 1) * P].unsqueeze(1).broadcast_to((P, R, P)), ALU.add).then_inc(s["y_f"], 1)

            with dve.Fori(0, NG) as i:
                mix_y(1, i)
                tile_no = [dve.snap(G * i + (t + 1)) for t in range(G)]
                for t in range(G):
                    n = tile_no[t]
                    sc = g2[:, t]
                    dve.wait_ge(s["sc1_ps"], n)
                    nc.vector.tensor_copy(sc, pb[4 + t][:, 0:E1]).then_inc(s["sc1_sb"], 1)
                    alone(dve)
                    dve.wait_ge(s["sc1_sb"], n)
                    nc.vector.max(top[:, t, 0], sc).then_inc(s["top_a"], 1)
                    dve.wait_ge(s["top_a"], n)
                    ts(g_nm[:, t:t + 1], top[:, t, 0, 0:1], -1.0, None, ALU.mult).then_inc(s["top_neg"], 1)
                    nc.vector.match_replace(g1[:, t], top[:, t, 0], sc, TAKEN).then_inc(s["took_a"], 1)
                    alone(dve)
                    dve.wait_ge(s["took_a"], n)
                    nc.vector.max(top[:, t, 1], g1[:, t]).then_inc(s["top_b"], 1)
                    alone(dve)
                    dve.wait_ge(s["top_b"], n)
                    nc.vector.match_replace(g2[:, t], top[:, t, 1], g1[:, t], TAKEN).then_inc(s["took_b"], 1)
                for t in range(G):
                    n = G * i + (t + 1)
                    dve.wait_ge(s["took_b"], n)
                    dve.wait_ge(s["gate_exp"], n)
                    stt(gate[:, t], g2[:, t], TAKEN, ge[:, t], ALU.is_equal, ALU.mult, accum_out=g_s[:, t:t + 1])\
                        .then_inc(s["gate_sum"], 1)
                    dve.wait_ge(s["gate_sum"], n)
                    nc.vector.reciprocal(g_r[:, t:t + 1], g_s[:, t:t + 1]).then_inc(s["gate_ready"], 1)
                for t in range(G):
                    n = G * i + (t + 1)
                    dve.wait_ge(s["gate_ready"], n)
                    dve.wait_ge(s["z_ps"], n)
                    stt(F[:, t].rearrange("p (e r) -> p e r", e=E1), pb[(t + 1) % 4][:, :].rearrange("p (e r) -> p e r", e=E1),
                        g_r[:, t:t + 1], gate[:, t].unsqueeze(2).broadcast_to((P, E1, RANK1)), ALU.mult, ALU.mult)\
                        .then_inc(s["zg_f"], 1)
                for t in range(G):
                    dve.wait_ge(s["zt_hi"], G * i + (t + 1))
                    tt(ST[1][:, t], pb[4 + t][:, :], ST[0][:, t].bitcast(F32), ALU.subtract).then_inc(s["zt_lo"], 1)
                for t in range(G):
                    add_to_x(1, i, t, t, scale=2.0)

            with dve.Fori(0, NG) as i:
                diag_make(2, i)
                for t in range(G):
                    conv_y(2, i, t)
                add_to_x(2, i, 0, 5)
                dve.wait_ge(s["sl_ps"], i + 1)
                ts(z2[:, bass.ds(i * (G * P), G * P)], pb[4][0:Z2, :], 1.0, None, ALU.mult).then_inc(s["z2_sb"], 1)
                add_to_x(2, i, 1, 6)
                dve.wait_ge(s["anc_ps"], i + 1)
                nc.vector.tensor_copy(anc[:, bass.ds(i * G, G), :], pb[2][:, 0:G * 2 * E2].rearrange("p (t e) -> p t e", t=G))\
                    .then_inc(s["anc_sb"], 1)
                add_to_x(2, i, 2, 7)
                add_to_x(2, i, 3, 3)

            dve.wait_ge(s["anc_sb"], NG)
            for h in range(2):
                nc.vector.tensor_reduce(amax[:, h:h + 1], anc[:, :, h * E2:(h + 1) * E2], AX.XY, ALU.max,
                                        apply_absolute_value=True).then_inc(s["anc_max"], 1)
            dve.wait_ge(s["b3_in"], 64)
            dve.wait_ge(s["e3_ready"], 1)
            for c in range(2):
                ts(b3_scaled[:, c], b3_raw[:, c], e3s[:, 2, c:c + 1], None, ALU.mult).then_inc(s["b3_ready"], 1)
            dve.wait_ge(s["anc_all"], 1)
            ts(ascale[:, :], amax_all[:, :], EPS, 2.0, ALU.max, ALU.mult).then_inc(s["anc_eps"], 1)
            dve.wait_ge(s["anc_eps"], 1)
            nc.vector.reciprocal(arecip[:, :], ascale[:, :]).then_inc(s["anc_inv"], 1)
            dve.wait_ge(s["anc_inv"], 1)

            step = [0]

            def then(ins):
                step[0] += 1
                ins.then_inc(s["lg_step"], 1)
                dve.wait_ge(s["lg_step"], step[0])

            def per_tile(v):
                return v.unsqueeze(2).broadcast_to((P, NT, E2))

            then(ts(lg[:, 0], anc[:, :, 0:E2], arecip[:, 0:1], None, ALU.mult))
            then(stt(lg[:, 1], anc[:, :, E2:2 * E2], arecip[:, 1:2], lg[:, 0], ALU.mult, ALU.add))
            then(nc.vector.reduce_max(lgs[:, 0], lg[:, 1], AX.X))
            then(tt(lg[:, 2], lg[:, 1], per_tile(lgs[:, 0]), ALU.subtract))
            dve.wait_ge(s["lg_exp"], 1)
            then(nc.vector.reduce_sum(lgs[:, 1], lg[:, 3], AX.X))
            then(nc.vector.reciprocal(lgs[:, 2], lgs[:, 1]))
            then(tt(lg[:, 4], lg[:, 3], per_tile(lgs[:, 2]), ALU.mult))
            for n in range(NT):
                last = nc.vector.max(ltop[:, n], lg[:, 4, n])
            last.then_inc(s["w_ready"], 1)
            dve.wait_ge(s["w_ready"], 1)
            then(tt(lg[:, 5], lg[:, 4], ltop[:, :, 1:2].broadcast_to((P, NT, E2)), ALU.subtract))
            dve.wait_ge(s["lg_sig"], 1)
            then(ts(lg[:, 5], lg[:, 6], 1.0, None, ALU.add))
            then(nc.vector.reciprocal(lg[:, 6], lg[:, 5]))
            then(tt(lg[:, 7], lg[:, 4], lg[:, 6], ALU.mult))
            then(nc.vector.reduce_sum(lgs[:, 1], lg[:, 7], AX.X))
            then(ts(lgs[:, 2], lgs[:, 1], 1e-9, None, ALU.add))
            then(nc.vector.reciprocal(lgs[:, 3], lgs[:, 2]))
            tt(lg[:, 0], lg[:, 7], per_tile(lgs[:, 3]), ALU.mult).then_inc(s["w_ready"], 1)
            for c in range(4):
                dve.wait_ge(s["w3_ps"], c + 1)
                tt(F[:, c], pb[4 + c][:, :], w3_raw[:, c], ALU.add).then_inc(s["w3_f"], 1)
            for i in range(NG):
                dve.wait_ge(s["pm_ps"], i + 1)
                stt(zp[0:Z2, :], pb[1][0:Z2, :], 0.5, z2[:, i * G * P:(i + 1) * G * P], ALU.mult, ALU.mult)\
                    .then_inc(s["zp_ready"], 1)
                for t in range(G):
                    n = 3 * NT + G * i + t + 1
                    dve.wait_ge(s["ff_ps"], n)
                    tt(x[:, G * i + t], pb[4 + t][:, :], x[:, G * i + t], ALU.add).then_inc(s["x_new"], 1)

            with dve.Fori(0, NG) as i:
                mix_y(3, i)
                for t in range(G):
                    add_to_x(3, i, t, 4 + t)

        @block.tensor
        def _(pe):
            mm = nc.tensor.matmul

            def mm3(out, lh, ll, rh, rl, first, last):
                mm(out, lh, rh, start=first, stop=False, skip_group_check=True)
                mm(out, lh, rl, start=False, stop=False, skip_group_check=True)
                return mm(out, ll, rh, start=False, stop=last, skip_group_check=True)

            pe.wait_ge(s["cst_in"], 16)
            pe.wait_ge(s["cond_in"], 5 * 16)
            pe.wait_ge(s["ones_set"], 2)
            for j in range(2):
                mm(pb[j][:, 0:S], condT[:, :], cw[:, j, :], start=True, stop=False)
                mm(pb[j][:, 0:S], ones[0:1, :], fside[:, :], start=False, stop=True).then_inc(s["rows_ps"], 1)
            pe.wait_ge(s["small_in"], 16 * 14)
            for r in range(R):
                mm(pb[2][:, r * E0:(r + 1) * E0], wq0[:, r * M:(r + 1) * M], keys0[:, :], start=(r == 0), stop=(r == R - 1), skip_group_check=True)
            for r in range(R):
                mm(pb[2][:, 64 + r * E2:64 + (r + 1) * E2], a2T[:, r * M:(r + 1) * M], limesT[:, :], start=False, stop=(r == R - 1), skip_group_check=True)
            for r in range(R):
                last = mm(pb[3][:, r * E1:(r + 1) * E1], wq1[:, r * M:(r + 1) * M], keys1[:, :], start=(r == 0), stop=(r == R - 1), skip_group_check=True)
            last.then_inc(s["tables_ps"], 1)
            for j in range(2):
                for k in range(2):
                    if 2 * j + k:
                        pe.wait_ge(s["hid_sb"], 2 * j + k)
                    mm(pb[4][:, 0:P], mw[:, j, k, :], condT[:, :] if k == 0 else hid[:, j, 0, :], start=True, stop=True)\
                        .then_inc(s["hid_ps"], 1)
            pe.wait_ge(s["hid_sb"], 4)
            for j in range(2):
                mm(pb[5][:, j * K1:(j + 1) * K1], hid[:, j, 1, :], mw2[:, j, :], start=(j == 0), stop=False, skip_group_check=True)
                last = mm(pb[5][:, j * K1:(j + 1) * K1], ones[0:1, :], mb2[:, j, :], start=False, stop=True, skip_group_check=True)
            last.then_inc(s["att_ps"], 1)
            for j in range(2):
                pe.wait_ge(s["rows_lo"], 4)
                pe.wait_ge(s["att_ready"], j + 1)
                nc.tensor.transpose(pb[6][0:K1, j * P:(j + 1) * P], att[:, j, :], ident).then_inc(s["attT_ps"], 1)
                pe.wait_ge(s["attm_ready"], j + 1)
                if j:
                    pe.wait_ge(s["attk_sb"], j)
                mm(pb[7][0:TB * K1, j * NT:(j + 1) * NT], attm[:, j].rearrange("p b k -> p (b k)"), cst[0:B, C_TILE:C_TILE + NT],
                   start=True, stop=True, skip_group_check=True).then_inc(s["attk_ps"], 1)
                pe.wait_ge(s["attT_sb"], j + 1)
                mm(pb[j][:, 0:S], attT[:, j, :], mbk[:, j, :], start=True, stop=True).then_inc(s["rows_ps"], 1)
            pe.wait_ge(s["kq1_lo"], 1)
            pe.wait_ge(s["raw_alt_sb"], 1)

            def mixed_kernels(j):
                pe.wait_ge(s["kmix_in"], 16 * (j + 1))
                pe.wait_ge(s["attk_sb"], j + 1)
                for o in range(S):
                    last = mm(pb[2][:, o * NT:(o + 1) * NT], kmix[:, o, :], attk[:, j, :], start=(o == 0), stop=True, skip_group_check=True)
                last.then_inc(s["agg_ps"], 1)

            mixed_kernels(0)
            pe.wait_ge(s["stage_lo"], 2)
            pe.wait_ge(s["border_set"], 4)
            pe.wait_ge(s["raw0_lo"], 3)
            pe.wait_ge(s["rows_lo"], 8)
            pe.wait_ge(s["agg_sb"], 1)
            pe.wait_ge(s["tables0_sb"], 1)

            def conv(layer, i, t):
                pe.wait_ge(s["xh_hi"], upto(layer // 2, i, t))
                pe.wait_ge(s["xh_lo"], upto(layer // 2, i, t))
                wh, wl = conv_w[layer // 2]
                for b in range(TB):
                    for d in range(3):
                        last = mm3(pb[t][:, b * P:(b + 1) * P], XH[0][:, t % 2, b, d:d + M], XH[1][:, t % 2, b, d:d + M],
                                   wh[:, d, :], wl[:, d, :], b == 0 and d == 0, b == TB - 1 and d == 2)
                last.then_inc(s["y_ps"], 1)

            def row_broadcast(layer, i, bank):
                pe.wait_ge(s["diag_ready"], i + (layer * NG + 1))
                mm(pb[bank][:, :], ones_r[:, :], diag[:, :], start=True, stop=True).then_inc(s["row_bc"], 1)

            def y_ready(layer, i, t):
                pe.wait_ge(s["y_hi"], upto(layer, i, t))
                pe.wait_ge(s["y_lo"], upto(layer, i, t))

            def from_y(bank, t, w, n, last_group=True):
                for r in range(R):
                    last = mm3(pb[bank][:, 0:n], Y[0][:, r, t * P:(t + 1) * P], Y[1][:, r, t * P:(t + 1) * P],
                               w[0][:, r, 0:n], w[1][:, r, 0:n], r == 0, last_group and r == R - 1)
                return last

            with pe.Fori(0, NG) as i:
                conv(0, i, 0)
                row_broadcast(0, i, 4)
                for t in range(1, G):
                    conv(0, i, t)
                for t in range(G):
                    y_ready(0, i, t)
                    from_y(4 + t, t, worg, D, last_group=False)
                    if t == 2:
                        pe.wait_ge(s["ysum_done"], upto(0, i, G - 1))
                        for r in range(R):
                            last = mm(pb[0][0:GB, 0:E0], ysum[:, r, :], kq0[:, r, :], start=(r == 0), stop=(r == R - 1), skip_group_check=True)
                        last.then_inc(s["sc0_ps"], 1)
                pe.wait_ge(s["coef_p"], i + 1)
                for c in range(4):
                    last = mm(pb[1][:, c * GB:(c + 1) * GB], sc_p[:, 2 * c:2 * c + 2].rearrange("p e k -> p (e k)"),
                              cst[0:GB, 0:GB], start=(c == 0), stop=True, skip_group_check=True)
                last.then_inc(s["coef_ps"], 1)
                for c in range(4):
                    if c == 3:
                        pe.wait_ge(s["coef_sb"], i + 1)
                    for r in range(R):
                        last = mm3(pb[(c + 2) % 4][:, :], lora_dn[0][:, r, c * P:(c + 1) * P], lora_dn[1][:, r, c * P:(c + 1) * P],
                                   Y[0][:, r, :], Y[1][:, r, :], r == 0, r == R - 1)
                    last.then_inc(s["h_ps"], 1)
                for c in range(4):
                    pe.wait_ge(s["h_hi"], 4 * i + (c + 1))
                    pe.wait_ge(s["h_lo"], 4 * i + (c + 1))
                    for t in range(G):
                        last = mm3(pb[4 + t][:, :], ST[0][:, c, t * P:(t + 1) * P], ST[1][:, c, t * P:(t + 1) * P],
                                   lora_up[0][:, c, :], lora_up[1][:, c, :], False, c == 3)
                        if c == 3:
                            last.then_inc(s["ff_ps"], 1)

            def mix(layer, i, t):
                for part in ("mix_hi", "mix_lo", "st_hi", "st_lo"):
                    pe.wait_ge(s[part], upto(layer // 2, i, t))
                for r in range(R):
                    last = mm3(pb[(t + 1) % 4][:, r * P:(r + 1) * P], ST[0][:, t, r * M:(r + 1) * M], ST[1][:, t, r * M:(r + 1) * M],
                               MX[0][:, t], MX[1][:, t], r == 0, r == R - 1)
                last.then_inc(s["y_ps"], 1)

            pe.wait_ge(s["stage_lo"], 2 * NG + 2)
            with pe.Fori(0, NG) as i:
                pe.wait_ge(s["x_new"], x_upto(1, i, 0) - G)
                row_broadcast(1, i, 0)
                for t in range(G):
                    if t < G - 1:
                        pe.wait_ge(s["x_new"], x_upto(1, i, t + 1) - G)
                    else:
                        pe.wait_ge(s["added_ready"], i + (NG + 1))
                    mix(1, i, t)
                for t in range(G):
                    y_ready(1, i, t)
                    from_y(4 + t, t, KQ1, E1).then_inc(s["sc1_ps"], 1)
                for t in range(G):
                    from_y((t + 1) % 4, t, a1, D).then_inc(s["z_ps"], 1)
                for t in range(G):
                    pe.wait_ge(s["zg_f"], G * i + (t + 1))
                    for c in range(4):
                        last = nc.tensor.transpose(pb[4 + t][:, c * P:(c + 1) * P], F[:, t, c * P:(c + 1) * P], ident)
                    last.then_inc(s["zt_ps"], 1)
                for t in range(G):
                    pe.wait_ge(s["zt_hi"], G * i + (t + 1))
                    pe.wait_ge(s["zt_lo"], G * i + (t + 1))
                    for c in range(4):
                        last = mm3(pb[t][:, :], ST[0][:, t, c * P:(c + 1) * P], ST[1][:, t, c * P:(c + 1) * P],
                                   b1[0][:, c, :], b1[1][:, c, :], c == 0, c == 3)
                    last.then_inc(s["ff_ps"], 1)

            pe.wait_ge(s["stage_lo"], 3 * NG + 2)
            pe.wait_ge(s["slice_w_lo"], 1)
            with pe.Fori(0, NG) as i:
                for t in range(G):
                    pe.wait_ge(s["x_new"], x_upto(2, i, t) - G)
                    conv(2, i, t)
                    if t == 0:
                        row_broadcast(2, i, 4)
                y_ready(2, i, 0)
                from_y(5, 0, w2, D).then_inc(s["ff_ps"], 1)
                for t in range(1, G):
                    y_ready(2, i, t)
                for r in range(R):
                    last = mm3(pb[4][0:96, :], SLW[0][:, r, :], SLW[1][:, r, :], Y[0][:, r, :], Y[1][:, r, :], r == 0, r == R - 1)
                last.then_inc(s["sl_ps"], 1)
                from_y(6, 1, w2, D).then_inc(s["ff_ps"], 1)
                pe.wait_ge(s["sl_sb"], i + 1)
                pe.wait_ge(s["z2_sb"], i + 1)
                for t in range(G):
                    last = mm(pb[2][:, t * 2 * E2:(t + 1) * 2 * E2], sl_ring[Z2:SLICES, t * P:(t + 1) * P], cst[Z2:SLICES, Z2:SLICES], start=(t == 0), stop=True, skip_group_check=True)
                last.then_inc(s["anc_ps"], 1)
                from_y(7, 2, w2, D).then_inc(s["ff_ps"], 1)
                from_y(3, 3, w2, D).then_inc(s["ff_ps"], 1)

            pe.wait_ge(s["b3_ready"], 2)
            pe.wait_ge(s["x_new"], 3 * NT)
            for c in range(4):
                for k in range(2):
                    last = mm(pb[4 + c][:, :], a3_raw[:, k, c * M:(c + 1) * M], b3_scaled[:, k, :], start=(k == 0), stop=(k == 1))
                last.then_inc(s["w3_ps"], 1)
            mixed_kernels(1)
            pe.wait_ge(s["w_ready"], 2)
            pe.wait_ge(s["zp_one"], 1)
            pe.wait_ge(s["w3_f"], 4)
            for i in range(NG):
                for t in range(G):
                    last = nc.tensor.transpose(pb[0][0:E2, t * P:(t + 1) * P], lg[:, 0, G * i + t], ident)
                last.then_inc(s["wT_ps"], 1)
                pe.wait_ge(s["wT_sb"], i + 1)
                mm(pb[1][0:Z2, :], limes[:, :], w2T[:, :], start=True, stop=True).then_inc(s["pm_ps"], 1)
                pe.wait_ge(s["zp_ready"], i + 1)
                for t in range(G):
                    if i:
                        pe.wait_ge(s["x_new"], 3 * NT + G * (i - 1) + t + 1)
                    mm(pb[4 + t][:, :], zp[:, t * P:(t + 1) * P], bmat[:, :], start=True, stop=True).then_inc(s["ff_ps"], 1)

            pe.wait_ge(s["w3_lo"], 4)
            pe.wait_ge(s["bias3_hi"], 1)
            with pe.Fori(0, NG) as i:
                row_broadcast(3, i, 0)
                for t in range(G):
                    if t == G - 1:
                        pe.wait_ge(s["added_ready"], i + (3 * NG + 1))
                    mix(3, i, t)
                for t in range(G):
                    y_ready(3, i, t)
                    pe.wait_ge(s["x_new"], x_upto(3, i, t) - G)
                    from_y(4 + t, t, w3, D, last_group=False)
                    mm(pb[4 + t][:, :], ones_r[0:2, :], bias3[:, :], start=False, stop=True, skip_group_check=True).then_inc(s["ff_ps"], 1)


def kernel(**inputs):
    import numpy as np
    import concourse.bacc as bacc
    from concourse.bass_utils import run_bass_kernel_spmd

    def a(name):
        return np.asarray(inputs[name])

    def dec(w):
        return w.reshape(*w.shape[:-1], M, R).swapaxes(-1, -2).reshape(w.shape)

    def chunks(w):
        return w.reshape(w.shape[0] // P, P, -1).swapaxes(0, 1)

    def banded(w):
        per = w.shape[1]
        out = np.zeros((S, R, 3, R, S), np.float32)
        for d in range(3):
            for rp in range(R):
                for r in range(R):
                    k = R * (d - 1) + rp - r + 4
                    if 0 <= k < w.shape[2]:
                        for g in range(S // per):
                            out[g * per:(g + 1) * per, rp, d, r, g * per:(g + 1) * per] = w[g * per:(g + 1) * per, :, k].T
        return out.reshape(P, 3 * P)

    def kernels_of(w):
        out = np.zeros((TB, K1, S, TB, S), np.float32)
        for b in range(TB):
            out[b, :, :, b, :] = w[..., 0]
        return out.reshape(TB * K1, S, P)

    cst = np.zeros((P, C_ALL), np.float32)
    cst[:, C_IDENT:C_IDENT + P] = np.eye(P)
    cst[:, C_EYE2:C_EYE2 + B] = np.concatenate([np.eye(B), np.eye(B)])
    for p in range(P):
        cst[p, C_BLK + p // S] = 1
    for b in range(B):
        cst[b, C_TILE + b // TB] = 1
        cst[b, C_MOD + b % TB] = 1

    w2t = a("L2_ffn_W").T
    w3t = a("L3_ffn_W").T

    def rows_dec(w):
        return w.reshape(M, R, -1)

    two = [(1, "L1"), (3, "L3")]
    arrays = {
        "x": a("x").reshape(B, S, M, R).transpose(0, 1, 3, 2),
        "cst": cst,
        "condT": np.concatenate([a("cond_128").T] * 2, 1),
        "cw": np.stack([a("L0_cond_c_weight").T, a("L2_cond_c_weight").T], 1),
        "fside": a("fside_S_0")[None],
        "conv0": banded(a("L0_cond_weight")),
        "conv2": banded(a("L2_cond_weight")),
        "worg": rows_dec(dec(a("L0_ffn_W_org").T)),
        "lora_dn": rows_dec(a("L0_ffn_lora_down").transpose(1, 0, 2).reshape(D, D)),
        "lora_up": chunks(dec(a("L0_ffn_lora_up").reshape(D, D))),
        "wq0": dec(a("L0_ffn_Wq")),
        "keys0": a("L0_ffn_lora_keys").T,
        "mw": np.stack([np.stack([a(f"{n}_cond_W0"), a(f"{n}_cond_W1")], 1) for _, n in two], 1),
        "mb": np.stack([np.stack([a(f"{n}_cond_b0"), a(f"{n}_cond_b1")], 1) for _, n in two], 1),
        "mw2": np.stack([a(f"{n}_cond_W2") for _, n in two], 1),
        "mb2": np.stack([a(f"{n}_cond_b2") for _, n in two], 0)[None],
        "mbk": np.stack([a(f"{n}_cond_bias_k") for _, n in two], 1),
        "kmix1": kernels_of(a("L1_cond_weight")),
        "kmix3": kernels_of(a("L3_cond_weight")),
        "a1": rows_dec(a("L1_ffn_A_w").T).reshape(P, -1),
        "b1": chunks(dec(a("L1_ffn_B_w").T)).reshape(P, -1),
        "wq1": dec(a("L1_ffn_Wq_w")),
        "keys1": a("L1_ffn_keys").T,
        "w2": rows_dec(dec(w2t)).reshape(P, -1),
        "w2slice": rows_dec(w2t[:, 0:E2]),
        "a2": rows_dec(a("L2_ffn_A")),
        "a2T": dec(a("L2_ffn_A").T),
        "limesT": a("L2_ffn_LiMEs").T,
        "limes": a("L2_ffn_LiMEs"),
        "slice_bias": np.concatenate([np.zeros(Z2 + E2, np.float32), a("L2_ffn_b")[0:E2]])[:, None],
        "bmat": np.concatenate([dec(a("L2_ffn_Bmat")), dec(a("L2_ffn_b")[None])]),
        "w3": rows_dec(dec(w3t)),
        "a3": chunks(dec(a("L3_ffn_A").reshape(256, D))),
        "b3": chunks(dec(a("L3_ffn_Bf").transpose(0, 2, 1).reshape(256, D))),
        "e3s": np.stack([np.repeat(a(f"L3_ffn_{n}"), 16).reshape(2, P).T for n in ("coeffs", "scales")], 1),
        "bias3": np.concatenate([dec(a("L3_ffn_bias")[None]), np.zeros((1, D), np.float32)]),
    }
    nc = bacc.Bacc("TRN2", target_bir_lowering=False, num_devices=1)
    arrays = {n: np.ascontiguousarray(v) for n, v in arrays.items()}
    t_in = {n: nc.dram_tensor(f"in_{n}", v.shape, mybir.dt.from_np(v.dtype), kind="ExternalInput").ap()
            for n, v in arrays.items()}
    out = nc.dram_tensor("out_x", (B, S, R, M), F32, kind="ExternalOutput").ap()
    scratch = nc.dram_tensor("scratch_x", (B, S, R, M), F32).ap()
    build(nc, t_in, out, scratch)
    res = run_bass_kernel_spmd(nc, [{f"in_{n}": v for n, v in arrays.items()}], core_ids=[0])
    got = res.results[0]["out_x"]
    return np.ascontiguousarray(got.transpose(0, 1, 3, 2).reshape(B, S, D))
```

```python
from contextlib import ExitStack

import concourse.bass as bass
from concourse import mybir

ALU = mybir.AluOpType
ACT = mybir.ActivationFunctionType
AX = mybir.AxisListType
F32 = mybir.dt.float32
F32R = mybir.dt.float32r

P = 128
B, S, D = 64, 32, 512
R, M = 4, 128
TB = P // S
NT = B // TB
G = 4
NG = NT // G
GB = G * TB
E0 = 8
K1 = 8
E1, RANK1 = 64, 8
Z2, E2 = 32, 8
SLICES = Z2 + 2 * E2
PAD = 96
EPS = 1e-6
TAKEN = -3.0e38


def columns(*sizes):
    starts = [0]
    for n in sizes:
        starts.append(starts[-1] + n)
    return starts


C_IDENT, C_BLK, C_TILE, C_MOD, C_FSIDE, C_MB, C_MW2, C_MB2, C_KEYS0, C_LIMES, C_SB, C_E3, C_LO, C_ALL = \
    columns(P, TB, NT, TB, 1, 4, 2 * K1, 2 * K1, E0, Z2, 1, 4, 2)
S_COND, S_CTX, S_MW, S_WQ0, S_SLICE, S_ALL = columns(B, 2 * P, 4 * P, D, R * SLICES)
T_A2T, T_LIMEST, T_WQ1, T_KEYS1, T_MBK, T_ALL = columns(D, E2, D, E1, 2 * P)


def build(nc, t_in, out, scratch, scratch_agg):
    ctx = ExitStack()
    with ctx:
        def sb(name, shape, dt=F32):
            return ctx.enter_context(nc.sbuf_tensor(name, shape, dt))

        def sem(name):
            return ctx.enter_context(nc.semaphore(name))

        WA_at = -(-nc.sbuf_base // 32) * 32
        WA = [[sb(f"wa{j}_{h}", [P, 4, D], F32R) for h in ("hi", "lo")] for j in range(3)]
        WB_at = -(-nc.sbuf_base // 32) * 32
        WB = [[sb(f"wb{j}_{h}", [P, 4, D], F32R) for h in ("hi", "lo")] for j in range(2)]
        worg, lora_dn, lora_up = WA
        w2, w3 = WA[0], WA[1]
        a1, b1 = WB

        ST_at = -(-nc.sbuf_base // 32) * 32
        ST = [sb(f"st_{h}", [P, G, D], F32R) for h in ("hi", "lo")]

        def over(name, shape, at, room_at, room, dt=F32):
            size = 4
            for n in shape[1:]:
                size *= n
            assert at + size <= room
            return nc.alloc_sbuf_tensor_at(name, shape, dt, offset=room_at + at)

        def over_wb(name, shape, at):
            return over(name, shape, at, WB_at, 4 * 4 * D * 4)

        def over_st(name, shape, at):
            return over(name, shape, at, ST_at, 2 * G * D * 4)

        def over_up(name, shape, at, dt=F32):
            return over(name, shape, WA_ROOM + at, WA_at, 3 * WA_ROOM // 2, dt)

        KB = 1024
        WA_ROOM = 2 * 2 * 4 * D * 4
        raw_dn = over_wb("raw_dn", [P, 4, D], 0)
        kernels = over_wb("kernels", [K1, 2, S * S], 8 * KB)
        agg_out = over_wb("agg_out", [B, 2, S * S], 16 * KB)
        raw_up = over_wb("raw_up", [P, 4, D], 24 * KB)
        z2 = over_wb("z2", [Z2, NT * P], 0)
        w2T = over_wb("w2T", [E2, NG, G * P], 8 * KB)
        zp = over_wb("zp", [Z2 + 1, NG, G * P], 16 * KB)
        w3_raw = over_wb("w3_raw", [P, 4, D], 24 * KB)
        setup = over_st("setup", [P, S_ALL], 0)
        setup32 = over_st("setup32", [Z2, T_ALL], 6 * KB + 512)
        bias3_f = over_st("bias3_f", [2, D], 12 * KB)
        hid = over_st("hid", [P, 2, 2, B], 14 * KB)
        a3_raw = over_st("a3_raw", [P, 2, D], 0)
        b3_raw = over_st("b3_raw", [P, 2, D], 4 * KB)
        b3_scaled = over_st("b3_scaled", [P, 2, D], 8 * KB)
        bmat = over_st("bmat", [Z2 + 1, D], 12 * KB)
        g1, g2, ge, gate = (over_up(n, [P, G, E1], j * KB) for j, n in enumerate(("g1", "g2", "ge", "gate")))
        scT = over_up("scT", [P, G * P], 4 * KB)
        sc1 = over_up("sc1", [P, G, E1], 14 * KB)
        BM = [over_up(f"bmat_{h}", [Z2 + 1, D], j * 2 * KB, F32R) for j, h in enumerate(("hi", "lo"))]
        sl_ring = over_up("sl_ring", [SLICES, G * P], 6 * KB)
        lg = over_up("lg", [P, 8, NT, E2], 8 * KB)
        anc = over_up("anc", [P, NT, 2 * E2], 12 * KB)
        ltop = over_up("ltop", [P, NT, 8], 13 * KB)

        x = sb("x", [P, NT, D])
        raw_org = x[:, NT - G:NT, :]
        F = sb("F", [P, G, D])
        Y = [sb(f"y_{h}", [P, R, G * P], F32R) for h in ("hi", "lo")]
        ZP = Y
        xf = sb("xf", [P, G, TB, M])
        XH = [sb(f"xhat_{h}", [P, 2, TB, M + 2], F32R) for h in ("hi", "lo")]
        conv_w = [[sb(f"conv{j}_{h}", [P, 3, P], F32R) for h in ("hi", "lo")] for j in range(2)]
        MX = [sb(f"mix_{h}", [P, G, P], F32R) for h in ("hi", "lo")]
        agg = sb("agg", [P, NT, S])
        AG = [sb(f"agg_{h}", [P, NT, S], F32R) for h in ("hi", "lo")]
        sc_p = sb("sc_p", [GB, E0, 64])
        stage = sb("stage", [P, 2, D])

        cst = sb("cst", [P, C_ALL])
        ident = cst[:, C_IDENT:C_IDENT + P]
        ones_r = sb("ones_r", [2, P], F32R)
        ones = sb("ones", [1, P])
        ctx_b = sb("ctx_b", [P, 2, B])
        agg_b = sb("agg_b", [P, 2, NT])
        kq0 = sb("kq0", [P, R, E0])
        KQ1 = [sb(f"kq1_{h}", [P, R, P], F32R) for h in ("hi", "lo")]
        SLW = [sb(f"slice_{h}", [P, R, PAD], F32R) for h in ("hi", "lo")]
        bias3 = sb("bias3", [2, D], F32R)
        bias3_t = [sb(f"bias3_t{j}", [2, D]) for j in range(1)][0]
        att_nm = sb("att_nm", [B, 2])
        att_e = sb("att_e", [B, 2, K1])
        att_s = sb("att_s", [B, 2])
        att_r = sb("att_r", [B, 2])
        att = sb("att", [B, 2, K1])
        attT = sb("attT", [K1, 2, B])
        attm = sb("attm", [B, 2, TB, K1])
        attk = sb("attk", [TB * K1, 2, NT])
        ysum = sb("ysum", [P, R, GB])
        sc_nm = sb("sc_nm", [GB, 1])
        sc_e = sb("sc_e", [GB, E0])
        sc_s = sb("sc_s", [GB, 1])
        sc_r = sb("sc_r", [GB, 1])
        coef = sb("coef", [P, 4, GB])
        top = sb("top", [P, G, 2, 8])
        g_nm = sb("g_nm", [P, G])
        g_s = sb("g_s", [P, G])
        g_r = sb("g_r", [P, G])
        amax = sb("amax", [P, 2])
        amax_all = sb("amax_all", [P, 2])
        ascale = sb("ascale", [P, 2])
        arecip = sb("arecip", [P, 2])
        lgs = sb("lgs", [P, 4, NT])
        e3w = sb("e3w", [P, 2])

        pb = [ctx.enter_context(nc.psum_tensor(f"bank{i}", [P, D], F32)) for i in range(8)]

        NAMES = """cst_in setup_in setup32_in kernels_in conv_in org_in dn_in up_in bias3_in x_in stage_in w2s_in
            agg_stored agg_in out_done spill_done b3_in
            ones_set border_set conv_w_hi conv_w_lo ctx_ps ctx_ready
            tables_ps kq0_sb kq1_hi kq1_lo alt_sb slice_w_hi slice_w_lo bias3_hi bias3_m bias3_ready
            hid_ps hid_sb att_ps att_max att_exp att_inv att_ready attm_ready attT_ps attT_sb attk_ps attk_sb
            aggb_ps aggb_sb agg_ps agg_sb agg_hi agg_lo raw_hi raw_lo
            xh_hi xh_lo y_ps y_f yt_ps y_hi y_lo ysum_done
            sc0_ps sc0_max sc0_exp sc0_inv coef_p coef_ps coef_sb h_ps h_f h_hi h_lo ff_ps x_new
            stage_hi stage_lo mx_ready st_hi st_lo
            sct_ps sct_sb sc1_ps sc1_sb top_a took_a top_b took_b top_neg gate_exp gate_sum gate_ready
            z_ps zg_f zt_ps zt_hi zt_lo
            sl_ps sl_sb z2_sb anc_ps anc_sb anc_max anc_all anc_eps anc_inv zp_one
            lg_step lg_exp lg_sig w_ready wT_ps wT_sb pm_ps zp_ready zp_hi zp_lo bm_hi bm_lo
            e3_ready b3_ready w3_ps w3_f w3_hi w3_lo""".split()
        s = {n: sem(n) for n in NAMES}
        xf_in = [sem(f"xf_in{t}") for t in range(G)]

        block = ctx.enter_context(nc.Block())

        def upto(layer, i, t):
            return G * i + (layer * NT + t + 1)

        def x_upto(layer, i, t):
            return G * i + ((layer + (layer == 3)) * NT + t + 1)

        def alone(eng):
            eng.wait_ge(s["cst_in"], 16)

        def x_tile(i, t):
            return x[:, bass.ds(i * G + t, 1), :].rearrange("p a n -> p (a n)")

        def conv_view(v):
            return v.rearrange("p (b r o) -> p r b o", b=TB, r=R)

        def y_view(v, t):
            return v[:, :, t * P:(t + 1) * P].rearrange("p r (b o) -> p r b o", b=TB)

        @block.sync
        def _(sp):
            sp.dma_start(stage[:, 0, 0:3 * P], t_in["conv0"]).then_inc(s["conv_in"], 16)
            xh_dram = t_in["x"].rearrange("(n b) i r m -> n (i r) b m", b=TB)
            sp.dma_start(xf[:, 0], xh_dram[0]).then_inc(xf_in[0], 16)
            sp.dma_start(xf[:, 1], xh_dram[1]).then_inc(xf_in[1], 16)
            sp.dma_start(raw_org, t_in["worg"]).then_inc(s["org_in"], 16)
            sp.dma_start(xf[:, 2], xh_dram[2]).then_inc(xf_in[2], 16)
            sp.dma_start(xf[:, 3], xh_dram[3]).then_inc(xf_in[3], 16)
            sp.dma_start(stage[:, 1, 0:3 * P], t_in["conv2"]).then_inc(s["conv_in"], 16)
            sp.dma_start(raw_dn[:, :, :], t_in["lora_dn"]).then_inc(s["dn_in"], 16)
            sp.dma_start(raw_up[:, :, :], t_in["lora_up"]).then_inc(s["up_in"], 16)
            x_tok = t_in["x"].rearrange("(n b) i r m -> (b i) n (r m)", b=TB)
            for i in range(NG):
                if i == NG - 1:
                    sp.wait_ge(s["raw_lo"], 4)
                sp.dma_start(x[:, G * i:G * i + G, :], x_tok[:, G * i:G * i + G, :]).then_inc(s["x_in"], 16)
            sp.wait_ge(s["agg_sb"], 4)
            for j in range(2):
                sp.dma_start(scratch_agg[j], agg_out[:, j, :]).then_inc(s["agg_stored"], 16)
            sp.wait_ge(s["agg_stored"], 32)
            agg_dram = scratch_agg.rearrange("j (n b) (i o) -> j (b i) n o", b=TB, o=S)
            sp.dma_start(agg[:, :, :], agg_dram[0]).then_inc(s["agg_in"], 16)
            xh_rest = t_in["x"].rearrange("(n b) i r m -> n (i r) b m", b=TB)
            a1_dram = t_in["a1"].rearrange("p (c n) -> p c n", c=4)
            b1_dram = t_in["b1"].rearrange("p (c n) -> p c n", c=4)
            sp.wait_ge(s["conv_w_lo"], 2)
            for j, w in enumerate((a1_dram, b1_dram)):
                sp.dma_start(stage[:, j], w[:, 0, :]).then_inc(s["stage_in"], 16)
            with sp.Fori(0, NG - 1) as i:
                for t in range(G):
                    sp.wait_ge(s["xh_lo"], upto(0, i, t))
                    sp.dma_start(xf[:, t], xh_rest[bass.ds(i * G + (G + t), 1)].rearrange("a p b m -> (a p) b m")).then_inc(xf_in[t], 16)
                sp.wait_ge(s["stage_lo"], 2 * i + 2)
                for j, w in enumerate((a1_dram, b1_dram)):
                    sp.dma_start(stage[:, j], w[:, bass.ds(i + 1, 1), :].rearrange("p a n -> p (a n)")).then_inc(s["stage_in"], 16)
            spill = scratch.rearrange("(n b) i r m -> n (b i) (r m)", b=TB)
            refill = scratch.rearrange("(n b) i r m -> n (i r) b m", b=TB)
            w2_dram = t_in["w2"].rearrange("p (c n) -> p c n", c=4)
            with sp.Fori(0, NG - 1) as i:
                sp.wait_ge(s["stage_lo"], i + 2 * NG)
                sp.dma_start(stage[:, 0], w2_dram[:, bass.ds(i, 1), :].rearrange("p a n -> p (a n)")).then_inc(s["w2s_in"], 16)
                for t in range(G):
                    sp.wait_ge(s["x_new"], x_upto(1, i, t))
                    sp.dma_start(spill[bass.ds(i * G + t, 1)].rearrange("a p n -> (a p) n"), x_tile(i, t)).then_inc(s["spill_done"], 16)
            sp.wait_ge(s["stage_lo"], 3 * NG - 1)
            sp.dma_start(stage[:, 0], w2_dram[:, NG - 1, :]).then_inc(s["w2s_in"], 16)
            sp.wait_ge(s["xh_lo"], NT)
            for t in range(G):
                sp.wait_ge(s["spill_done"], 16 * (NT - G))
                sp.dma_start(xf[:, t], refill[t]).then_inc(xf_in[t], 16)
            for t in range(G):
                sp.wait_ge(s["x_new"], x_upto(1, NG - 1, t))
                sp.dma_start(spill[NT - G + t], x[:, NT - G + t, :]).then_inc(s["spill_done"], 16)
            sp.dma_start(a3_raw[:, :, :], t_in["a3"]).then_inc(s["b3_in"], 16)
            sp.dma_start(b3_raw[:, :, :], t_in["b3"]).then_inc(s["b3_in"], 16)
            sp.dma_start(w3_raw[:, :, :], t_in["w3"]).then_inc(s["b3_in"], 16)
            sp.dma_start(bmat[:, :], t_in["bmat"]).then_inc(s["b3_in"], 16)
            sp.wait_ge(s["agg_lo"], 1)
            sp.dma_start(agg[:, :, :], agg_dram[1]).then_inc(s["agg_in"], 16)
            sp.wait_ge(s["spill_done"], 16 * NT)
            with sp.Fori(0, NG - 1) as i:
                for t in range(G):
                    sp.wait_ge(s["xh_lo"], upto(1, i, t))
                    sp.dma_start(xf[:, t], refill[bass.ds(i * G + (G + t), 1)].rearrange("a p b m -> (a p) b m")).then_inc(xf_in[t], 16)
            out_tok = out.rearrange("(n b) i r m -> n (b i) (r m)", b=TB)
            with sp.Fori(0, NG) as i:
                for t in range(G):
                    sp.wait_ge(s["x_new"], x_upto(3, i, t))
                    sp.dma_start(out_tok[bass.ds(i * G + t, 1)].rearrange("a p n -> (a p) n"), x_tile(i, t)).then_inc(s["out_done"], 16)
            sp.wait_ge(s["out_done"], 16 * NT)

        @block.scalar
        def _(act):
            copy = nc.scalar.activation

            act.dma_start(setup[:, :], t_in["setup"]).then_inc(s["setup_in"], 16)
            act.dma_start(cst[:, :], t_in["cst"]).then_inc(s["cst_in"], 16)
            act.dma_start(setup32[:, :], t_in["setup32"]).then_inc(s["setup32_in"], 16)
            act.dma_start(kernels[:, :, :], t_in["kernels"]).then_inc(s["kernels_in"], 16)
            act.dma_start(bias3_f[:, :], t_in["bias3"]).then_inc(s["bias3_in"], 16)

            def conv_w_hi(j):
                copy(conv_w[j][0][:, :, :].rearrange("p a n -> p (a n)"), stage[:, j, 0:3 * P], ACT.Copy).then_inc(s["conv_w_hi"], 1)

            def xhat_hi(layer, i, t):
                act.wait_ge(xf_in[t], 16 * i + 16 * (layer // 2 * NG + 1))
                copy(XH[0][:, t % 2, :, 1:M + 1], xf[:, t], ACT.Copy).then_inc(s["xh_hi"], 1)

            def conv_y_hi(layer, i, t):
                act.wait_ge(s["yt_ps"], upto(layer, i, t))
                copy(y_view(Y[0], t), conv_view(pb[4 + t][:, :]), ACT.Copy).then_inc(s["y_hi"], 1)

            def gelu(k):
                for j in range(2):
                    act.wait_ge(s["hid_ps"], 2 * k + 2)
                    copy(hid[:, j, k, :], pb[6][:, (2 * k + j) * B:(2 * k + j + 1) * B], ACT.Gelu,
                         bias=cst[:, C_MB + 2 * j + k:C_MB + 2 * j + k + 1]).then_inc(s["hid_sb"], 1)

            def raw_hi(j, raw, c):
                copy(WA[j][0][:, c], raw[:, c, :], ACT.Copy).then_inc(s["raw_hi"], 1)

            def experts0(i):
                act.wait_ge(s["sc0_max"], i + 1)
                copy(sc_e[:, :], pb[0][0:GB, 0:E0], ACT.Exp, bias=sc_nm[:, 0:1], accum_out=sc_s[:, 0:1]).then_inc(s["sc0_exp"], 1)
                act.wait_ge(s["coef_ps"], i + 1)
                copy(coef[:, :, :], pb[1][:, 0:4 * GB].rearrange("p (c b) -> p c b", c=4), ACT.Copy).then_inc(s["coef_sb"], 1)
                for c in range(4):
                    act.wait_ge(s["h_f"], 4 * i + (c + 1))
                    copy(ST[0][:, c], F[:, c], ACT.Copy).then_inc(s["h_hi"], 1)

            def stage_hi(dst, i, slot):
                copy(dst[:, bass.ds(i, 1), :].rearrange("p a n -> p (a n)"), stage[:, slot], ACT.Copy).then_inc(s["stage_hi"], 1)

            def stage1_hi(i):
                act.wait_ge(s["stage_in"], 32 * i + 32)
                stage_hi(a1[0], i, 0)
                stage_hi(b1[0], i, 1)

            act.wait_ge(s["conv_in"], 32)
            conv_w_hi(0)
            xhat_hi(0, 0, 0)
            xhat_hi(0, 0, 1)
            act.wait_ge(s["cst_in"], 16)
            gelu(0)
            act.wait_ge(s["tables_ps"], 1)
            copy(kq0[:, :, :], pb[5][:, 0:R * E0].rearrange("p (r e) -> p r e", r=R), ACT.Copy,
                 scale=1.0 / (S * float(P) ** 0.5)).then_inc(s["kq0_sb"], 1)
            slices = setup[:, S_SLICE:S_ALL].rearrange("p (r e) -> p r e", r=R)
            copy(slices[:, :, Z2:Z2 + E2], pb[5][:, R * E0:R * (E0 + E2)].rearrange("p (r e) -> p r e", r=R), ACT.Copy)\
                .then_inc(s["alt_sb"], 1)
            act.wait_ge(s["border_set"], 6)
            copy(KQ1[0][:, :, 0:E1], pb[5][:, 64:64 + R * E1].rearrange("p (r e) -> p r e", r=R), ACT.Copy).then_inc(s["kq1_hi"], 1)
            act.wait_ge(s["y_ps"], 1)
            xhat_hi(0, 0, 2)
            gelu(1)
            act.wait_ge(s["y_ps"], 2)
            xhat_hi(0, 0, 3)
            act.wait_ge(s["org_in"], 16)
            for c in range(4):
                raw_hi(0, raw_org, c)
            conv_y_hi(0, 0, 0)
            for j in range(2):
                act.wait_ge(s["att_max"], 2)
                copy(att_e[:, j, :], pb[6][0:B, 4 * B + j * K1:4 * B + (j + 1) * K1], ACT.Exp, bias=att_nm[:, j:j + 1],
                     accum_out=att_s[:, j:j + 1]).then_inc(s["att_exp"], 1)
            conv_y_hi(0, 0, 1)
            act.wait_ge(s["attT_ps"], 1)
            act.wait_ge(s["attk_ps"], 1)
            copy(attT[:, :, :], pb[7][0:K1, 0:2 * B].rearrange("p (j b) -> p j b", j=2), ACT.Copy).then_inc(s["attT_sb"], 1)
            copy(attk[:, :, :], pb[7][0:TB * K1, 2 * B:2 * B + 2 * NT].rearrange("p (j n) -> p j n", j=2), ACT.Copy).then_inc(s["attk_sb"], 1)
            conv_y_hi(0, 0, 2)
            conv_y_hi(0, 0, 3)
            conv_w_hi(1)
            act.wait_ge(s["alt_sb"], 1)
            copy(SLW[0][:, :, 0:SLICES], slices, ACT.Copy).then_inc(s["slice_w_hi"], 1)
            act.wait_ge(s["bias3_in"], 16)
            copy(bias3[:, :], bias3_f[:, :], ACT.Copy).then_inc(s["bias3_hi"], 1)
            act.wait_ge(s["dn_in"], 16)
            for c in range(4):
                raw_hi(1, raw_dn, c)
            for n in range(4):
                act.wait_ge(s["agg_ps"], n + 1)
                copy(agg_out[:, n // 2, (n % 2) * D:(n % 2 + 1) * D], pb[n][0:B, :], ACT.Copy).then_inc(s["agg_sb"], 1)
            act.wait_ge(s["aggb_ps"], 1)
            copy(agg_b[:, :, :], pb[2][:, 0:2 * NT].rearrange("p (j n) -> p j n", j=2), ACT.Copy).then_inc(s["aggb_sb"], 1)
            act.wait_ge(s["up_in"], 16)
            for c in range(4):
                raw_hi(2, raw_up, c)
            act.wait_ge(s["slice_w_lo"], 1)
            act.wait_ge(s["bias3_ready"], 1)
            experts0(0)
            act.wait_ge(s["agg_in"], 16)
            copy(AG[0][:, :, :], agg[:, :, :], ACT.Copy).then_inc(s["agg_hi"], 1)
            act.wait_ge(s["raw_lo"], 12)
            act.wait_ge(s["agg_stored"], 32)
            stage1_hi(0)

            def conv_layer(layer, i):
                for t in range(2):
                    xhat_hi(layer, i, t)
                for t in range(2, G):
                    act.wait_ge(s["y_ps"], upto(layer, i, t - 2))
                    xhat_hi(layer, i, t)
                for t in range(G):
                    conv_y_hi(layer, i, t)

            with act.Fori(1, NG) as i:
                conv_layer(0, i)
                experts0(i)
                stage1_hi(i)

            def mix_layer(layer, i):
                for t in range(G):
                    if layer == 1:
                        act.wait_ge(s["ff_ps"], x_upto(1, i, t) - G)
                    else:
                        act.wait_ge(s["y_ps"], upto(3, i, t) - G)
                        act.wait_ge(s["x_new"], G * i + (3 * NT + t + 1))
                    copy(ST[0][:, t], x_tile(i, t), ACT.Copy).then_inc(s["st_hi"], 1)
                for t in range(G):
                    act.wait_ge(s["y_ps"], upto(layer, i, t))
                    copy(F[:, t], pb[t][:, :], ACT.Identity, bias=agg_b[:, layer // 2, bass.ds(i * G + t, 1)]).then_inc(s["y_f"], 1)
                    if t:
                        mix_y_hi(layer, i, t - 1)
                mix_y_hi(layer, i, G - 1)

            def mix_y_hi(layer, i, t):
                act.wait_ge(s["yt_ps"], upto(layer, i, t))
                copy(Y[0][:, :, t * P:(t + 1) * P], pb[4 + t][:, :].rearrange("p (r n) -> p r n", r=R), ACT.Copy).then_inc(s["y_hi"], 1)

            with act.Fori(0, NG) as i:
                mix_layer(1, i)
                act.wait_ge(s["sct_ps"], i + 1)
                copy(scT[:, :], pb[0][:, :], ACT.Copy).then_inc(s["sct_sb"], 1)
                for t in range(G):
                    act.wait_ge(s["top_neg"], G * i + (t + 1))
                    copy(ge[:, t], sc1[:, t], ACT.Exp, bias=g_nm[:, t:t + 1]).then_inc(s["gate_exp"], 1)
                act.wait_ge(s["w2s_in"], 16 * i + 16)
                stage_hi(w2[0], i, 0)
                for t in range(G):
                    act.wait_ge(s["zt_ps"], G * i + (t + 1))
                    copy(ST[0][:, t], pb[t][:, :], ACT.Copy).then_inc(s["zt_hi"], 1)

            with act.Fori(0, NG) as i:
                conv_layer(2, i)
                act.wait_ge(s["sl_ps"], i + 1)
                copy(sl_ring[Z2:SLICES, :].rearrange("p (j two) -> p j two", two=2),
                     pb[0][Z2:SLICES, :].rearrange("p (j two) -> p j two", two=2)[:, :, 1:2].broadcast_to((2 * E2, G * P // 2, 2)),
                     ACT.Identity, bias=cst[Z2:SLICES, C_SB:C_SB + 1]).then_inc(s["sl_sb"], 1)

            act.wait_ge(s["b3_in"], 64)
            copy(BM[0][:, :], bmat[:, :], ACT.Copy).then_inc(s["bm_hi"], 1)
            act.wait_ge(s["agg_in"], 32)
            copy(AG[0][:, :, :], agg[:, :, :], ACT.Copy).then_inc(s["agg_hi"], 1)
            act.wait_ge(s["lg_step"], 4)
            copy(lg[:, 3], lg[:, 2], ACT.Exp).then_inc(s["lg_exp"], 1)
            act.wait_ge(s["lg_step"], 8)
            copy(lg[:, 6], lg[:, 5], ACT.Exp, scale=-2.0).then_inc(s["lg_sig"], 1)
            for i in range(NG):
                act.wait_ge(s["wT_ps"], i + 1)
                copy(w2T[:, i], pb[i][0:E2, :], ACT.Copy).then_inc(s["wT_sb"], 1)
            act.wait_ge(s["ff_ps"], 3 * NT)
            for i in range(NG):
                act.wait_ge(s["zp_ready"], i + 1)
                copy(ZP[0][0:Z2 + 1, i], zp[:, i], ACT.Copy).then_inc(s["zp_hi"], 1)
            for c in range(4):
                act.wait_ge(s["w3_f"], c + 1)
                copy(w3[0][:, c], F[:, c], ACT.Copy).then_inc(s["w3_hi"], 1)

            with act.Fori(0, NG) as i:
                mix_layer(3, i)

        @block.gpsimd
        def _(pool):
            def lo(dst, v, hi):
                return nc.gpsimd.tensor_tensor(dst, v, hi.bitcast(F32), ALU.subtract)

            def conv_w_lo(j):
                pool.wait_ge(s["conv_w_hi"], j + 1)
                lo(conv_w[j][1][:, :, :].rearrange("p a n -> p (a n)"), stage[:, j, 0:3 * P],
                   conv_w[j][0][:, :, :].rearrange("p a n -> p (a n)")).then_inc(s["conv_w_lo"], 1)

            def xhat_lo(layer, i, t):
                pool.wait_ge(s["xh_hi"], upto(layer // 2, i, t))
                lo(XH[1][:, t % 2, :, 1:M + 1], xf[:, t], XH[0][:, t % 2, :, 1:M + 1]).then_inc(s["xh_lo"], 1)

            def raw_lo(j, raw, c):
                pool.wait_ge(s["raw_hi"], 4 * j + c + 1)
                lo(WA[j][1][:, c], raw[:, c, :], WA[j][0][:, c]).then_inc(s["raw_lo"], 1)

            def h_lo(i):
                for c in range(4):
                    pool.wait_ge(s["h_hi"], 4 * i + (c + 1))
                    lo(ST[1][:, c], F[:, c], ST[0][:, c]).then_inc(s["h_lo"], 1)

            def stage_lo(w, i, slot, n):
                pool.wait_ge(s["stage_hi"], n)
                lo(w[1][:, bass.ds(i, 1), :].rearrange("p a n -> p (a n)"), stage[:, slot],
                   w[0][:, bass.ds(i, 1), :].rearrange("p a n -> p (a n)")).then_inc(s["stage_lo"], 1)

            conv_w_lo(0)
            for t in range(G):
                xhat_lo(0, 0, t)
            for c in range(4):
                raw_lo(0, raw_org, c)
            conv_w_lo(1)
            for c in range(4):
                raw_lo(1, raw_dn, c)
            for c in range(4):
                raw_lo(2, raw_up, c)
            h_lo(0)
            for j, w in enumerate((a1, b1)):
                stage_lo(w, 0, j, j + 1)
            with pool.Fori(1, NG) as i:
                for t in range(G):
                    xhat_lo(0, i, t)
                h_lo(i)
                for j, w in enumerate((a1, b1)):
                    stage_lo(w, i, j, 2 * i + (j + 1))

            def mix_layer(layer, i):
                pool.wait_ge(s["y_ps"], upto(layer, i, G - 1) - G)
                for h in range(2):
                    nc.gpsimd.tensor_tensor(
                        MX[h][:, :, :].rearrange("p t (b o) -> p t b o", b=TB),
                        AG[h][:, bass.ds(i * G, G), :].bitcast(F32).unsqueeze(2).broadcast_to((P, G, TB, S)),
                        cst[:, C_BLK:C_BLK + TB].unsqueeze(1).unsqueeze(3).broadcast_to((P, G, TB, S)), ALU.mult).then_inc(s["mx_ready"], 1)
                for t in range(G):
                    pool.wait_ge(s["st_hi"], upto(layer // 2, i, t))
                    lo(ST[1][:, t], x_tile(i, t), ST[0][:, t]).then_inc(s["st_lo"], 1)

            pool.wait_ge(s["agg_lo"], 1)
            with pool.Fori(0, NG) as i:
                mix_layer(1, i)
                stage_lo(w2, i, 0, i + (2 * NG + 1))

            pool.wait_ge(s["ff_ps"], 2 * NT)
            pool.wait_ge(s["stage_lo"], 3 * NG)
            nc.gpsimd.memset(zp[Z2:Z2 + 1, :, :], 1.0).then_inc(s["zp_one"], 1)
            pool.wait_ge(s["zp_one"], 1)
            with pool.Fori(0, NG) as i:
                for t in range(G):
                    xhat_lo(2, i, t)

            pool.wait_ge(s["anc_max"], 2)
            nc.gpsimd.partition_all_reduce(amax_all[:, :], amax[:, :], P, bass.bass_isa.ReduceOp.max).then_inc(s["anc_all"], 1)
            for c in range(4):
                pool.wait_ge(s["w3_hi"], c + 1)
                lo(w3[1][:, c], F[:, c], w3[0][:, c]).then_inc(s["w3_lo"], 1)

            pool.wait_ge(s["agg_lo"], 2)
            with pool.Fori(0, NG) as i:
                mix_layer(3, i)

        @block.vector
        def _(dve):
            tt, stt, ts = nc.vector.tensor_tensor, nc.vector.scalar_tensor_tensor, nc.vector.tensor_scalar

            for h in range(2):
                nc.vector.memset(XH[h][:, :, :, 0:M + 2:M + 1].bitcast(F32), 0.0).then_inc(s["border_set"], 1)
            nc.vector.memset(ones[:, :], 1.0).then_inc(s["ones_set"], 1)
            for w in (*SLW, *KQ1):
                nc.vector.memset(w[:, :, :].bitcast(F32), 0.0).then_inc(s["border_set"], 1)
            nc.vector.memset(ones_r[:, :].bitcast(F32), 1.0).then_inc(s["ones_set"], 1)

            def conv_y(layer, i, t):
                dve.wait_ge(s["y_ps"], upto(layer, i, t))
                tt(F[:, t].rearrange("p (b m) -> p b m", b=TB), pb[t][:, :].rearrange("p (b m) -> p b m", b=TB),
                   ctx_b[:, layer // 2, bass.ds(i * GB + t * TB, TB)].unsqueeze(2).broadcast_to((P, TB, M)),
                   ALU.add).then_inc(s["y_f"], 1)

            def conv_y_lo(layer, i, t):
                dve.wait_ge(s["y_hi"], upto(layer, i, t))
                tt(y_view(Y[1], t), conv_view(pb[4 + t][:, :]), y_view(Y[0], t).bitcast(F32), ALU.subtract).then_inc(s["y_lo"], 1)

            def sum_rows(t):
                nc.vector.reduce_sum(ysum[:, :, t * TB:(t + 1) * TB], conv_view(pb[4 + t][:, :]), AX.X).then_inc(s["ysum_done"], 1)

            def add_to_x(layer, i, t, scale=None):
                dve.wait_ge(s["ff_ps"], x_upto(layer, i, t))
                xt = x_tile(i, t)
                if scale:
                    stt(xt, pb[4 + t][:, :], scale, xt, ALU.mult, ALU.add).then_inc(s["x_new"], 1)
                else:
                    tt(xt, pb[4 + t][:, :], xt, ALU.add).then_inc(s["x_new"], 1)

            def experts0(i):
                dve.wait_ge(s["sc0_ps"], i + 1)
                nc.vector.reduce_max(sc_nm[:, :], pb[0][0:GB, 0:E0], AX.X, negate=True).then_inc(s["sc0_max"], 1)
                dve.wait_ge(s["sc0_exp"], i + 1)
                nc.vector.reciprocal(sc_r[:, :], sc_s[:, :]).then_inc(s["sc0_inv"], 1)
                dve.wait_ge(s["sc0_inv"], i + 1)
                ts(sc_p[:, :, :], sc_e[:, :].unsqueeze(2).broadcast_to((GB, E0, 64)), sc_r[:, 0:1], None, ALU.mult).then_inc(s["coef_p"], 1)
                dve.wait_ge(s["coef_sb"], i + 1)
                for c in range(4):
                    dve.wait_ge(s["h_ps"], 4 * i + (c + 1))
                    tt(F[:, c].rearrange("p (b o) -> p b o", b=GB), pb[(c + 2) % 4][:, :].rearrange("p (b o) -> p b o", b=GB),
                       coef[:, c, :].unsqueeze(2).broadcast_to((P, GB, S)), ALU.mult).then_inc(s["h_f"], 1)
                dve.wait_ge(s["x_in"], 16 * NG)
                for t in range(G):
                    add_to_x(0, i, t)

            dve.wait_ge(s["cst_in"], 16)
            dve.wait_ge(s["ctx_ps"], 1)
            ts(ctx_b[:, :, :], pb[7][:, 0:2 * B].rearrange("p (j b) -> p j b", j=2), cst[:, C_FSIDE:C_FSIDE + 1], None, ALU.add)\
                .then_inc(s["ctx_ready"], 1)
            dve.wait_ge(s["ctx_ready"], 1)
            conv_y(0, 0, 0)
            dve.wait_ge(s["kq1_hi"], 1)
            tt(KQ1[1][:, :, 0:E1], pb[5][:, 64:64 + R * E1].rearrange("p (r e) -> p r e", r=R), KQ1[0][:, :, 0:E1].bitcast(F32),
               ALU.subtract).then_inc(s["kq1_lo"], 1)
            conv_y(0, 0, 1)
            dve.wait_ge(s["att_ps"], 1)
            for j in range(2):
                nc.vector.reduce_max(att_nm[:, j:j + 1], pb[6][0:B, 4 * B + j * K1:4 * B + (j + 1) * K1], AX.X, negate=True)\
                    .then_inc(s["att_max"], 1)
            conv_y(0, 0, 2)
            conv_y_lo(0, 0, 0)
            sum_rows(0)
            for j in range(2):
                dve.wait_ge(s["att_exp"], j + 1)
                nc.vector.reciprocal(att_r[:, j:j + 1], att_s[:, j:j + 1]).then_inc(s["att_inv"], 1)
            for j in range(2):
                dve.wait_ge(s["att_inv"], j + 1)
                ts(att[:, j, :], att_e[:, j, :], att_r[:, j:j + 1], None, ALU.mult).then_inc(s["att_ready"], 1)
            for j in range(2):
                dve.wait_ge(s["att_ready"], j + 1)
                tt(attm[:, j], att[:, j, :].unsqueeze(1).broadcast_to((B, TB, K1)),
                   cst[0:B, C_MOD:C_MOD + TB].unsqueeze(2).broadcast_to((B, TB, K1)), ALU.mult).then_inc(s["attm_ready"], 1)
            conv_y_lo(0, 0, 1)
            sum_rows(1)
            conv_y(0, 0, 3)
            for t in range(2, G):
                conv_y_lo(0, 0, t)
                sum_rows(t)
            dve.wait_ge(s["slice_w_hi"], 1)
            tt(SLW[1][:, :, 0:SLICES], setup[:, S_SLICE:S_ALL].rearrange("p (r e) -> p r e", r=R), SLW[0][:, :, 0:SLICES].bitcast(F32),
               ALU.subtract).then_inc(s["slice_w_lo"], 1)
            dve.wait_ge(s["bias3_hi"], 1)
            ts(bias3_t[:, :], bias3[:, :].bitcast(F32), cst[0:2, C_LO:C_LO + 1], None, ALU.mult).then_inc(s["bias3_m"], 1)
            dve.wait_ge(s["bias3_m"], 1)
            stt(bias3[:, :], bias3_f[:, :], cst[0:2, C_LO + 1:C_LO + 2], bias3_t[:, :], ALU.mult, ALU.add).then_inc(s["bias3_ready"], 1)
            tt(e3w[:, :], cst[:, C_E3:C_E3 + 2], cst[:, C_E3 + 2:C_E3 + 4], ALU.mult).then_inc(s["e3_ready"], 1)
            experts0(0)
            dve.wait_ge(s["agg_hi"], 1)
            tt(AG[1][:, :, :], agg[:, :, :], AG[0][:, :, :].bitcast(F32), ALU.subtract).then_inc(s["agg_lo"], 1)

            with dve.Fori(1, NG) as i:
                conv_y(0, i, 0)
                for t in range(G):
                    if t < G - 1:
                        conv_y(0, i, t + 1)
                    conv_y_lo(0, i, t)
                    sum_rows(t)
                experts0(i)

            def mix_y_lo(layer, i, t):
                dve.wait_ge(s["y_hi"], upto(layer, i, t))
                tt(Y[1][:, :, t * P:(t + 1) * P], pb[4 + t][:, :].rearrange("p (r n) -> p r n", r=R),
                   Y[0][:, :, t * P:(t + 1) * P].bitcast(F32), ALU.subtract).then_inc(s["y_lo"], 1)

            with dve.Fori(0, NG) as i:
                group_no = dve.snap(i + 1)
                tile_no = [dve.snap(G * i + (t + 1)) for t in range(G)]
                for t in range(G):
                    mix_y_lo(1, i, t)
                dve.wait_ge(s["sc1_ps"], group_no)
                nc.vector.tensor_copy(sc1[:, :, :], pb[1][:, :].rearrange("p (t e) -> p t e", t=G)[:, :, 0:E1]).then_inc(s["sc1_sb"], 1)
                alone(dve)
                dve.wait_ge(s["sc1_sb"], group_no)
                for t in range(G):
                    nc.vector.max(top[:, t, 0], sc1[:, t]).then_inc(s["top_a"], 1)
                for t in range(G):
                    dve.wait_ge(s["top_a"], tile_no[t])
                    ts(g_nm[:, t:t + 1], top[:, t, 0, 0:1], -1.0, None, ALU.mult).then_inc(s["top_neg"], 1)
                    nc.vector.match_replace(g1[:, t], top[:, t, 0], sc1[:, t], TAKEN).then_inc(s["took_a"], 1)
                for t in range(G):
                    alone(dve)
                    dve.wait_ge(s["took_a"], tile_no[t])
                    nc.vector.max(top[:, t, 1], g1[:, t]).then_inc(s["top_b"], 1)
                for t in range(G):
                    alone(dve)
                    dve.wait_ge(s["top_b"], tile_no[t])
                    nc.vector.match_replace(g2[:, t], top[:, t, 1], g1[:, t], TAKEN).then_inc(s["took_b"], 1)
                for t in range(G):
                    dve.wait_ge(s["took_b"], tile_no[t])
                    dve.wait_ge(s["gate_exp"], tile_no[t])
                    stt(gate[:, t], g2[:, t], TAKEN, ge[:, t], ALU.is_equal, ALU.mult, accum_out=g_s[:, t:t + 1])\
                        .then_inc(s["gate_sum"], 1)
                for t in range(G):
                    dve.wait_ge(s["gate_sum"], tile_no[t])
                    nc.vector.reciprocal(g_r[:, t:t + 1], g_s[:, t:t + 1]).then_inc(s["gate_ready"], 1)
                for t in range(G):
                    dve.wait_ge(s["gate_ready"], tile_no[t])
                    dve.wait_ge(s["z_ps"], tile_no[t])
                    stt(F[:, t].rearrange("p (e r) -> p e r", e=E1), pb[4 + t][:, :].rearrange("p (e r) -> p e r", e=E1),
                        g_r[:, t:t + 1], gate[:, t].unsqueeze(2).broadcast_to((P, E1, RANK1)), ALU.mult, ALU.mult)\
                        .then_inc(s["zg_f"], 1)
                for t in range(G):
                    dve.wait_ge(s["zt_hi"], tile_no[t])
                    tt(ST[1][:, t], pb[t][:, :], ST[0][:, t].bitcast(F32), ALU.subtract).then_inc(s["zt_lo"], 1)
                for t in range(G):
                    add_to_x(1, i, t, scale=2.0)

            with dve.Fori(0, NG) as i:
                conv_y(2, i, 0)
                conv_y(2, i, 1)
                conv_y(2, i, 2)
                conv_y_lo(2, i, 0)
                conv_y(2, i, 3)
                for t in range(1, G):
                    conv_y_lo(2, i, t)
                add_to_x(2, i, 0)
                dve.wait_ge(s["sl_ps"], i + 1)
                ts(z2[:, bass.ds(i * (G * P), G * P)], pb[0][0:Z2, :], 1.0, None, ALU.mult).then_inc(s["z2_sb"], 1)
                add_to_x(2, i, 1)
                dve.wait_ge(s["anc_ps"], i + 1)
                nc.vector.tensor_copy(anc[:, bass.ds(i * G, G), :], pb[1][:, 0:G * 2 * E2].rearrange("p (t e) -> p t e", t=G))\
                    .then_inc(s["anc_sb"], 1)
                add_to_x(2, i, 2)
                add_to_x(2, i, 3)

            dve.wait_ge(s["anc_sb"], NG)
            for h in range(2):
                nc.vector.tensor_reduce(amax[:, h:h + 1], anc[:, :, h * E2:(h + 1) * E2], AX.XY, ALU.max,
                                        apply_absolute_value=True).then_inc(s["anc_max"], 1)
            dve.wait_ge(s["b3_in"], 64)
            dve.wait_ge(s["e3_ready"], 1)
            for c in range(2):
                ts(b3_scaled[:, c], b3_raw[:, c], e3w[:, c:c + 1], None, ALU.mult).then_inc(s["b3_ready"], 1)
            dve.wait_ge(s["anc_all"], 1)
            ts(ascale[:, :], amax_all[:, :], EPS, 2.0, ALU.max, ALU.mult).then_inc(s["anc_eps"], 1)
            dve.wait_ge(s["anc_eps"], 1)
            nc.vector.reciprocal(arecip[:, :], ascale[:, :]).then_inc(s["anc_inv"], 1)
            dve.wait_ge(s["anc_inv"], 1)

            step = [0]

            def then(ins):
                step[0] += 1
                ins.then_inc(s["lg_step"], 1)
                dve.wait_ge(s["lg_step"], step[0])

            def per_tile(v):
                return v.unsqueeze(2).broadcast_to((P, NT, E2))

            then(ts(lg[:, 0], anc[:, :, 0:E2], arecip[:, 0:1], None, ALU.mult))
            then(stt(lg[:, 1], anc[:, :, E2:2 * E2], arecip[:, 1:2], lg[:, 0], ALU.mult, ALU.add))
            then(nc.vector.reduce_max(lgs[:, 0], lg[:, 1], AX.X))
            then(tt(lg[:, 2], lg[:, 1], per_tile(lgs[:, 0]), ALU.subtract))
            dve.wait_ge(s["bm_hi"], 1)
            tt(BM[1][:, :], bmat[:, :], BM[0][:, :].bitcast(F32), ALU.subtract).then_inc(s["bm_lo"], 1)
            dve.wait_ge(s["lg_exp"], 1)
            then(nc.vector.reduce_sum(lgs[:, 1], lg[:, 3], AX.X))
            then(nc.vector.reciprocal(lgs[:, 2], lgs[:, 1]))
            then(tt(lg[:, 4], lg[:, 3], per_tile(lgs[:, 2]), ALU.mult))
            for n in range(NT):
                last = nc.vector.max(ltop[:, n], lg[:, 4, n])
            last.then_inc(s["w_ready"], 1)
            dve.wait_ge(s["w_ready"], 1)
            then(tt(lg[:, 5], lg[:, 4], ltop[:, :, 1:2].broadcast_to((P, NT, E2)), ALU.subtract))
            dve.wait_ge(s["agg_hi"], 2)
            tt(AG[1][:, :, :], agg[:, :, :], AG[0][:, :, :].bitcast(F32), ALU.subtract).then_inc(s["agg_lo"], 1)
            dve.wait_ge(s["lg_sig"], 1)
            then(ts(lg[:, 5], lg[:, 6], 1.0, None, ALU.add))
            then(nc.vector.reciprocal(lg[:, 6], lg[:, 5]))
            then(tt(lg[:, 7], lg[:, 4], lg[:, 6], ALU.mult))
            then(nc.vector.reduce_sum(lgs[:, 1], lg[:, 7], AX.X))
            then(ts(lgs[:, 2], lgs[:, 1], 1e-9, None, ALU.add))
            then(nc.vector.reciprocal(lgs[:, 3], lgs[:, 2]))
            tt(lg[:, 0], lg[:, 7], per_tile(lgs[:, 3]), ALU.mult).then_inc(s["w_ready"], 1)
            for c in range(4):
                dve.wait_ge(s["w3_ps"], c + 1)
                tt(F[:, c], pb[4 + c][:, :], w3_raw[:, c], ALU.add).then_inc(s["w3_f"], 1)
            dve.wait_ge(s["zp_one"], 1)
            for i in range(NG):
                dve.wait_ge(s["pm_ps"], i + 1)
                stt(zp[0:Z2, i], pb[i][0:Z2, :], 0.5, z2[:, i * G * P:(i + 1) * G * P], ALU.mult, ALU.mult)\
                    .then_inc(s["zp_ready"], 1)
                dve.wait_ge(s["zp_hi"], i + 1)
                tt(ZP[1][0:Z2 + 1, i], zp[:, i], ZP[0][0:Z2 + 1, i].bitcast(F32), ALU.subtract).then_inc(s["zp_lo"], 1)
            with dve.Fori(0, NG) as i:
                for t in range(G):
                    dve.wait_ge(s["ff_ps"], G * i + (3 * NT + t + 1))
                    xt = x_tile(i, t)
                    tt(xt, pb[4 + t][:, :], xt, ALU.add).then_inc(s["x_new"], 1)

            with dve.Fori(0, NG) as i:
                for t in range(G):
                    mix_y_lo(3, i, t)
                for t in range(G):
                    add_to_x(3, i, t)

        @block.tensor
        def _(pe):
            mm = nc.tensor.matmul

            def mm3(out, lh, ll, rh, rl, first, last):
                mm(out, lh, rh, start=first, stop=False, skip_group_check=True)
                mm(out, lh, rl, start=False, stop=False, skip_group_check=True)
                return mm(out, ll, rh, start=False, stop=last, skip_group_check=True)

            def conv(layer, i, t):
                pe.wait_ge(s["xh_hi"], upto(layer // 2, i, t))
                pe.wait_ge(s["xh_lo"], upto(layer // 2, i, t))
                wh, wl = conv_w[layer // 2]
                for d in range(3):
                    last = mm3(pb[t][:, :].rearrange("p (b m) -> p b m", b=TB), wh[:, d, :], wl[:, d, :],
                               XH[0][:, t % 2, :, d:d + M], XH[1][:, t % 2, :, d:d + M], d == 0, d == 2)
                last.then_inc(s["y_ps"], 1)

            def turn(layer, i, t):
                pe.wait_ge(s["y_f"], upto(layer, i, t))
                for n in range(4):
                    last = nc.tensor.transpose(pb[4 + t][:, n * P:(n + 1) * P], F[:, t, n * P:(n + 1) * P], ident)
                last.then_inc(s["yt_ps"], 1)

            def bank_read(layer, i, t):
                pe.wait_ge(s["x_new"], x_upto(layer, i, t) - G)

            def from_y(layer, i, t, w, last_group=True):
                pe.wait_ge(s["y_hi"], upto(layer, i, t))
                pe.wait_ge(s["y_lo"], upto(layer, i, t))
                if layer == 0:
                    pe.wait_ge(s["ysum_done"], upto(layer, i, t))
                for r in range(R):
                    last = mm3(pb[4 + t][:, :], Y[0][:, r, t * P:(t + 1) * P], Y[1][:, r, t * P:(t + 1) * P],
                               w[0][:, r, :], w[1][:, r, :], r == 0, last_group and r == R - 1)
                return last

            def scores0(i):
                pe.wait_ge(s["ysum_done"], upto(0, i, G - 1))
                for r in range(R):
                    last = mm(pb[0][0:GB, 0:E0], ysum[:, r, :], kq0[:, r, :], start=(r == 0), stop=(r == R - 1), skip_group_check=True)
                last.then_inc(s["sc0_ps"], 1)

            def experts0(i):
                pe.wait_ge(s["coef_p"], i + 1)
                for c in range(4):
                    last = mm(pb[1][:, c * GB:(c + 1) * GB], sc_p[:, 2 * c:2 * c + 2].rearrange("p e k -> p (e k)"),
                              cst[0:GB, 0:GB], start=(c == 0), stop=True, skip_group_check=True)
                last.then_inc(s["coef_ps"], 1)
                for c in range(4):
                    if c == 3:
                        pe.wait_ge(s["coef_sb"], i + 1)
                    for r in range(R):
                        last = mm3(pb[(c + 2) % 4][:, :], lora_dn[0][:, r, c * P:(c + 1) * P], lora_dn[1][:, r, c * P:(c + 1) * P],
                                   Y[0][:, r, :], Y[1][:, r, :], r == 0, r == R - 1)
                    last.then_inc(s["h_ps"], 1)
                for c in range(4):
                    pe.wait_ge(s["h_hi"], 4 * i + (c + 1))
                    pe.wait_ge(s["h_lo"], 4 * i + (c + 1))
                    for t in range(G):
                        last = mm3(pb[4 + t][:, :], ST[0][:, c, t * P:(t + 1) * P], ST[1][:, c, t * P:(t + 1) * P],
                                   lora_up[0][:, c, :], lora_up[1][:, c, :], False, c == 3)
                        if c == 3:
                            last.then_inc(s["ff_ps"], 1)

            pe.wait_ge(s["setup_in"], 16)
            condT = setup[:, S_COND:S_COND + B]
            for j in range(2):
                last = mm(pb[7][:, j * B:(j + 1) * B], setup[:, S_CTX + j * P:S_CTX + (j + 1) * P], condT,
                          start=(j == 0), stop=True, skip_group_check=True)
            last.then_inc(s["ctx_ps"], 1)

            def hidden(k):
                for j in range(2):
                    w = S_MW + (2 * j + k) * P
                    mm(pb[6][:, (2 * k + j) * B:(2 * k + j + 1) * B], setup[:, w:w + P], condT if k == 0 else hid[:, j, 0, :],
                       start=(j == 0), stop=True, skip_group_check=True).then_inc(s["hid_ps"], 1)

            hidden(0)
            pe.wait_ge(s["cst_in"], 16)
            pe.wait_ge(s["setup32_in"], 16)
            for r in range(R):
                mm(pb[5][:, r * E0:(r + 1) * E0], setup[:, S_WQ0 + r * M:S_WQ0 + (r + 1) * M], cst[:, C_KEYS0:C_KEYS0 + E0],
                   start=(r == 0), stop=True, skip_group_check=True)
            for r in range(R):
                mm(pb[5][:, 32 + r * E2:32 + (r + 1) * E2], setup32[:, T_A2T + r * M:T_A2T + (r + 1) * M],
                   setup32[:, T_LIMEST:T_LIMEST + E2], start=False, stop=True, skip_group_check=True)
            for r in range(R):
                last = mm(pb[5][:, 64 + r * E1:64 + (r + 1) * E1], setup32[0:16, T_WQ1 + r * M:T_WQ1 + (r + 1) * M],
                          setup32[0:16, T_KEYS1:T_KEYS1 + E1], start=False, stop=True, skip_group_check=True)
            last.then_inc(s["tables_ps"], 1)

            pe.wait_ge(s["conv_w_lo"], 1)
            pe.wait_ge(s["border_set"], 6)
            conv(0, 0, 0)
            pe.wait_ge(s["hid_sb"], 2)
            hidden(1)
            conv(0, 0, 1)
            turn(0, 0, 0)
            pe.wait_ge(s["hid_sb"], 4)
            pe.wait_ge(s["ones_set"], 2)
            for j in range(2):
                att_ps = pb[6][0:B, 4 * B + j * K1:4 * B + (j + 1) * K1]
                mm(att_ps, hid[:, j, 1, :], cst[:, C_MW2 + j * K1:C_MW2 + (j + 1) * K1], start=(j == 0), stop=False, skip_group_check=True)
                last = mm(att_ps, ones[0:1, 0:B], cst[0:1, C_MB2 + j * K1:C_MB2 + (j + 1) * K1], start=False, stop=True, skip_group_check=True)
            last.then_inc(s["att_ps"], 1)
            conv(0, 0, 2)
            pe.wait_ge(s["kq1_lo"], 1)
            pe.wait_ge(s["alt_sb"], 1)
            turn(0, 0, 1)
            conv(0, 0, 3)
            pe.wait_ge(s["att_max"], 2)
            pe.wait_ge(s["att_exp"], 2)
            turn(0, 0, 2)
            pe.wait_ge(s["attm_ready"], 2)
            pe.wait_ge(s["ctx_ready"], 1)
            for j in range(2):
                last = nc.tensor.transpose(pb[7][0:K1, j * B:(j + 1) * B], att[:, j, :], ident[0:B, 0:B])
            last.then_inc(s["attT_ps"], 1)
            for j in range(2):
                last = mm(pb[7][0:TB * K1, 2 * B + j * NT:2 * B + (j + 1) * NT], attm[:, j].rearrange("p b k -> p (b k)"),
                          cst[0:B, C_TILE:C_TILE + NT], start=(j == 0), stop=True, skip_group_check=True)
            last.then_inc(s["attk_ps"], 1)
            pe.wait_ge(s["raw_lo"], 4)
            from_y(0, 0, 0, worg, last_group=False)
            pe.wait_ge(s["attT_sb"], 1)
            pe.wait_ge(s["attk_sb"], 1)
            turn(0, 0, 3)
            pe.wait_ge(s["kernels_in"], 16)
            for n in range(4):
                mm(pb[n][0:B, :], attT[:, n // 2, :], kernels[:, n // 2, (n % 2) * D:(n % 2 + 1) * D], start=True, stop=True)\
                    .then_inc(s["agg_ps"], 1)
            for t in range(1, G):
                from_y(0, 0, t, worg, last_group=False)
            pe.wait_ge(s["agg_sb"], 4)
            pe.wait_ge(s["kq0_sb"], 1)
            for j in range(2):
                last = mm(pb[2][:, j * NT:(j + 1) * NT], setup32[:, T_MBK + j * P:T_MBK + (j + 1) * P], attk[:, j, :],
                          start=(j == 0), stop=True, skip_group_check=True)
            last.then_inc(s["aggb_ps"], 1)
            scores0(0)
            pe.wait_ge(s["aggb_sb"], 1)
            pe.wait_ge(s["raw_lo"], 12)
            experts0(0)

            with pe.Fori(1, NG) as i:
                conv(0, i, 0)
                for t in range(1, G):
                    conv(0, i, t)
                    bank_read(0, i, t - 1)
                    turn(0, i, t - 1)
                from_y(0, i, 0, worg, last_group=False)
                bank_read(0, i, G - 1)
                turn(0, i, G - 1)
                for t in range(1, G):
                    from_y(0, i, t, worg, last_group=False)
                scores0(i)
                experts0(i)

            def mix(layer, i, t):
                pe.wait_ge(s["mx_ready"], 2 * i + 2 * (layer // 2 * NG + 1))
                pe.wait_ge(s["st_hi"], upto(layer // 2, i, t))
                pe.wait_ge(s["st_lo"], upto(layer // 2, i, t))
                mm3(pb[t][:, :], MX[0][:, t], MX[1][:, t], ST[0][:, t], ST[1][:, t], True, True).then_inc(s["y_ps"], 1)

            pe.wait_ge(s["stage_lo"], 2 * NG)
            with pe.Fori(0, NG) as i:
                mix(1, i, 0)
                mix(1, i, 1)
                for t in range(2, G):
                    mix(1, i, t)
                    bank_read(1, i, t - 2)
                    turn(1, i, t - 2)
                for t in range(2, G):
                    bank_read(1, i, t)
                    turn(1, i, t)
                from_y(1, i, 0, a1).then_inc(s["z_ps"], 1)
                pe.wait_ge(s["y_hi"], upto(1, i, G - 1))
                pe.wait_ge(s["y_lo"], upto(1, i, G - 1))
                for r in range(R):
                    last = mm3(pb[0][:, :], KQ1[0][:, r, :], KQ1[1][:, r, :], Y[0][:, r, :], Y[1][:, r, :], r == 0, r == R - 1)
                last.then_inc(s["sct_ps"], 1)
                from_y(1, i, 1, a1).then_inc(s["z_ps"], 1)
                pe.wait_ge(s["sct_sb"], i + 1)
                for t in range(G):
                    last = nc.tensor.transpose(pb[1][:, t * P:(t + 1) * P], scT[:, t * P:(t + 1) * P], ident)
                last.then_inc(s["sc1_ps"], 1)
                from_y(1, i, 2, a1).then_inc(s["z_ps"], 1)
                from_y(1, i, 3, a1).then_inc(s["z_ps"], 1)
                for t in range(G):
                    pe.wait_ge(s["zg_f"], G * i + (t + 1))
                    for c in range(4):
                        last = nc.tensor.transpose(pb[t][:, c * P:(c + 1) * P], F[:, t, c * P:(c + 1) * P], ident)
                    last.then_inc(s["zt_ps"], 1)
                for t in range(G):
                    pe.wait_ge(s["zt_hi"], G * i + (t + 1))
                    pe.wait_ge(s["zt_lo"], G * i + (t + 1))
                    for c in range(4):
                        last = mm3(pb[4 + t][:, :], ST[0][:, t, c * P:(c + 1) * P], ST[1][:, t, c * P:(c + 1) * P],
                                   b1[0][:, c, :], b1[1][:, c, :], c == 0, c == 3)
                    last.then_inc(s["ff_ps"], 1)

            pe.wait_ge(s["stage_lo"], 3 * NG)
            pe.wait_ge(s["slice_w_lo"], 1)
            pe.wait_ge(s["conv_w_lo"], 2)
            with pe.Fori(0, NG) as i:
                conv(2, i, 0)
                pe.wait_ge(s["x_new"], x_upto(2, i, 2) - G)
                conv(2, i, 1)
                bank_read(2, i, 0)
                turn(2, i, 0)
                conv(2, i, 2)
                bank_read(2, i, 1)
                turn(2, i, 1)
                conv(2, i, 3)
                bank_read(2, i, 2)
                turn(2, i, 2)
                from_y(2, i, 0, w2).then_inc(s["ff_ps"], 1)
                bank_read(2, i, 3)
                turn(2, i, 3)
                from_y(2, i, 1, w2).then_inc(s["ff_ps"], 1)
                pe.wait_ge(s["y_hi"], upto(2, i, G - 1))
                pe.wait_ge(s["y_lo"], upto(2, i, G - 1))
                for r in range(R):
                    last = mm3(pb[0][0:PAD, :], SLW[0][:, r, :], SLW[1][:, r, :], Y[0][:, r, :], Y[1][:, r, :], r == 0, r == R - 1)
                last.then_inc(s["sl_ps"], 1)
                from_y(2, i, 2, w2).then_inc(s["ff_ps"], 1)
                pe.wait_ge(s["sl_sb"], i + 1)
                pe.wait_ge(s["z2_sb"], i + 1)
                for t in range(G):
                    last = mm(pb[1][:, t * 2 * E2:(t + 1) * 2 * E2], sl_ring[Z2:SLICES, t * P:(t + 1) * P], cst[Z2:SLICES, Z2:SLICES],
                              start=(t == 0), stop=True, skip_group_check=True)
                last.then_inc(s["anc_ps"], 1)
                from_y(2, i, 3, w2).then_inc(s["ff_ps"], 1)

            pe.wait_ge(s["b3_ready"], 2)
            pe.wait_ge(s["x_new"], 3 * NT)
            for c in range(4):
                for k in range(2):
                    last = mm(pb[4 + c][:, :], a3_raw[:, k, c * M:(c + 1) * M], b3_scaled[:, k, :], start=(k == 0), stop=(k == 1))
                last.then_inc(s["w3_ps"], 1)
            pe.wait_ge(s["w_ready"], 2)
            for i in range(NG):
                for t in range(G):
                    last = nc.tensor.transpose(pb[i][0:E2, t * P:(t + 1) * P], lg[:, 0, G * i + t], ident)
                last.then_inc(s["wT_ps"], 1)
            for i in range(NG):
                pe.wait_ge(s["wT_sb"], i + 1)
                mm(pb[i][0:Z2, :], cst[0:E2, C_LIMES:C_LIMES + Z2], w2T[:, i, :], start=True, stop=True).then_inc(s["pm_ps"], 1)
            pe.wait_ge(s["bm_lo"], 1)
            for i in range(NG):
                pe.wait_ge(s["zp_hi"], i + 1)
                pe.wait_ge(s["zp_lo"], i + 1)
                for t in range(G):
                    if i:
                        pe.wait_ge(s["x_new"], 3 * NT + G * (i - 1) + t + 1)
                    else:
                        pe.wait_ge(s["w3_f"], t + 1)
                    mm3(pb[4 + t][:, :], ZP[0][0:Z2 + 1, i, t * P:(t + 1) * P], ZP[1][0:Z2 + 1, i, t * P:(t + 1) * P],
                        BM[0][:, :], BM[1][:, :], True, True).then_inc(s["ff_ps"], 1)

            pe.wait_ge(s["bias3_ready"], 1)
            pe.wait_ge(s["w3_lo"], 4)
            with pe.Fori(0, NG) as i:
                def apply_w3(t):
                    from_y(3, i, t, w3, last_group=False)
                    mm(pb[4 + t][:, :], ones_r[:, :], bias3[:, :], start=False, stop=True, skip_group_check=True).then_inc(s["ff_ps"], 1)

                mix(3, i, 0)
                mix(3, i, 1)
                for t in range(2, G):
                    mix(3, i, t)
                    bank_read(3, i, t - 2)
                    turn(3, i, t - 2)
                bank_read(3, i, 2)
                turn(3, i, 2)
                apply_w3(0)
                bank_read(3, i, 3)
                turn(3, i, 3)
                for t in range(1, G):
                    apply_w3(t)


def kernel(**inputs):
    import numpy as np
    import concourse.bacc as bacc
    from concourse.bass_utils import run_bass_kernel_spmd

    def a(name):
        return np.asarray(inputs[name])

    def dec(w):
        return w.reshape(*w.shape[:-1], M, R).swapaxes(-1, -2).reshape(w.shape)

    def chunks(w):
        return w.reshape(w.shape[0] // P, P, -1).swapaxes(0, 1)

    def banded(w):
        per = w.shape[1]
        out = np.zeros((S, R, 3, R, S), np.float32)
        for d in range(3):
            for rp in range(R):
                for r in range(R):
                    k = R * (d - 1) + rp - r + 4
                    if 0 <= k < w.shape[2]:
                        for g in range(S // per):
                            out[g * per:(g + 1) * per, rp, d, r, g * per:(g + 1) * per] = w[g * per:(g + 1) * per, :, k].T
        return out.reshape(P, 3 * P)

    def block_rows(w):
        out = np.zeros((TB, K1, TB, S), np.float32)
        for b in range(TB):
            out[b, :, b, :] = w
        return out.reshape(TB * K1, P)

    def pack(rows, width, *parts):
        out = np.zeros((rows, width), np.float32)
        for at, v in parts:
            v = v.reshape(v.shape[0], -1)
            out[:v.shape[0], at:at + v.shape[1]] = v
        return out

    w2t = a("L2_ffn_W").T
    w3t = a("L3_ffn_W").T

    def rows_dec(w):
        return w.reshape(M, R, -1)

    two = ("L1", "L3")
    batch, row = np.arange(B), np.arange(P)
    cst = pack(P, C_ALL,
               (C_IDENT, np.eye(P)),
               (C_BLK, row[:, None] // S == np.arange(TB)),
               (C_TILE, batch[:, None] // TB == np.arange(NT)),
               (C_MOD, batch[:, None] % TB == np.arange(TB)),
               (C_FSIDE, np.tile(a("fside_S_0"), R)[:, None]),
               (C_MB, np.stack([a(f"{n}_cond_b{k}") for n in two for k in range(2)], 1)),
               (C_MW2, np.concatenate([a(f"{n}_cond_W2") for n in two], 1)),
               (C_MB2, np.concatenate([a(f"{n}_cond_b2") for n in two])[None]),
               (C_KEYS0, a("L0_ffn_lora_keys").T),
               (C_LIMES, a("L2_ffn_LiMEs")),
               (C_SB, np.concatenate([np.zeros(Z2 + E2, np.float32), a("L2_ffn_b")[0:E2]])[:, None]),
               (C_E3, np.concatenate([np.repeat(a(f"L3_ffn_{n}"), 16).reshape(2, P).T for n in ("coeffs", "scales")], 1)),
               (C_LO, np.array([[1.0, 0.0], [-1.0, 1.0]])))
    slices = np.zeros((P, R, SLICES), np.float32)
    slices[:, :, 0:Z2] = rows_dec(a("L2_ffn_A"))
    slices[:, :, Z2 + E2:] = rows_dec(w2t[:, 0:E2])
    setup = pack(P, S_ALL,
                 (S_COND, a("cond_128").T),
                 (S_CTX, np.concatenate([np.tile(a(f"{n}_cond_c_weight").T, (1, R)) for n in ("L0", "L2")], 1)),
                 (S_MW, np.concatenate([a(f"{n}_cond_W{k}") for n in two for k in range(2)], 1)),
                 (S_WQ0, dec(a("L0_ffn_Wq"))),
                 (S_SLICE, slices))
    setup32 = pack(Z2, T_ALL,
                   (T_A2T, dec(a("L2_ffn_A").T)),
                   (T_LIMEST, a("L2_ffn_LiMEs").T),
                   (T_WQ1, dec(a("L1_ffn_Wq_w"))),
                   (T_KEYS1, a("L1_ffn_keys").T),
                   (T_MBK, np.concatenate([block_rows(a(f"{n}_cond_bias_k")) for n in two], 1)))
    arrays = {
        "cst": cst,
        "setup": setup,
        "setup32": setup32,
        "kernels": np.stack([a(f"{n}_cond_weight")[..., 0].transpose(0, 2, 1).reshape(K1, S * S) for n in two], 1),
        "x": a("x").reshape(B, S, M, R).transpose(0, 1, 3, 2),
        "conv0": banded(a("L0_cond_weight")),
        "conv2": banded(a("L2_cond_weight")),
        "worg": rows_dec(dec(a("L0_ffn_W_org").T)),
        "lora_dn": rows_dec(a("L0_ffn_lora_down").transpose(1, 0, 2).reshape(D, D)),
        "lora_up": chunks(dec(a("L0_ffn_lora_up").reshape(D, D))),
        "a1": rows_dec(a("L1_ffn_A_w").T).reshape(P, -1),
        "b1": chunks(dec(a("L1_ffn_B_w").T)).reshape(P, -1),
        "w2": rows_dec(dec(w2t)).reshape(P, -1),
        "bmat": np.concatenate([dec(a("L2_ffn_Bmat")), dec(a("L2_ffn_b")[None])]),
        "w3": rows_dec(dec(w3t)),
        "a3": chunks(dec(a("L3_ffn_A").reshape(256, D))),
        "b3": chunks(dec(a("L3_ffn_Bf").transpose(0, 2, 1).reshape(256, D))),
        "bias3": np.tile(dec(a("L3_ffn_bias")[None]), (2, 1)),
    }
    nc = bacc.Bacc("TRN2", target_bir_lowering=False, num_devices=1)
    arrays = {n: np.ascontiguousarray(v) for n, v in arrays.items()}
    t_in = {n: nc.dram_tensor(f"in_{n}", v.shape, mybir.dt.from_np(v.dtype), kind="ExternalInput").ap()
            for n, v in arrays.items()}
    out = nc.dram_tensor("out_x", (B, S, R, M), F32, kind="ExternalOutput").ap()
    scratch = nc.dram_tensor("scratch_x", (B, S, R, M), F32).ap()
    scratch_agg = nc.dram_tensor("scratch_agg", (2, B, S * S), F32).ap()
    build(nc, t_in, out, scratch, scratch_agg)
    res = run_bass_kernel_spmd(nc, [{f"in_{n}": v for n, v in arrays.items()}], core_ids=[0])
    got = res.results[0]["out_x"]
    return np.ascontiguousarray(got.transpose(0, 1, 3, 2).reshape(B, S, D))
```

```python
from contextlib import ExitStack

import concourse.bass as bass
from concourse import mybir

ALU = mybir.AluOpType
ACT = mybir.ActivationFunctionType
AX = mybir.AxisListType
F32 = mybir.dt.float32
F32R = mybir.dt.float32r

P = 128
B, S, D = 64, 32, 512
R, M = 4, 128
TB = P // S
NT = B // TB
G = 4
NG = NT // G
GB = G * TB
E0 = 8
K1 = 8
E1, RANK1 = 64, 8
Z2, E2 = 32, 8
ZS = 3 * Z2
SLICES = ZS + 2 * E2
EPS = 1e-6
WARM_UP = 8
TAKEN = -3.0e38


def columns(*sizes):
    starts = [0]
    for n in sizes:
        starts.append(starts[-1] + n)
    return starts


C_IDENT, C_BLK, C_FSIDE, C_MB, C_MW2, C_MB2, C_KEYS0, C_LIMES, C_SB, C_E3, C_LO, C_ALL = \
    columns(P, TB, 1, 4, 2 * K1, 2 * K1, E0, ZS, 1, 4, 2)
S_COND, S_CTX, S_MW, S_WQ0, S_SLICE, S_ALL = columns(B, 2 * P, 4 * P, D, R * SLICES)
T_A2T, T_LIMEST, T_WQ1, T_KEYS1, T_MBK, T_ALL = columns(D, E2, D, E1, 2 * S)


def build(nc, t_in, out, scratch, scratch_agg, scratch_bias):
    ctx = ExitStack()
    with ctx:
        def sb(name, shape, dt=F32):
            return ctx.enter_context(nc.sbuf_tensor(name, shape, dt))

        def sem(name):
            return ctx.enter_context(nc.semaphore(name))

        WA_at = -(-nc.sbuf_base // 32) * 32
        WA = [[sb(f"wa{j}_{h}", [P, 4, D], F32R) for h in ("hi", "lo")] for j in range(3)]
        WB_at = -(-nc.sbuf_base // 32) * 32
        WB = [[sb(f"wb{j}_{h}", [P, 4, D], F32R) for h in ("hi", "lo")] for j in range(2)]
        worg, lora_dn, lora_up = WA
        w2, w3 = WA[0], WA[1]
        a1, b1 = WB

        ST_at = -(-nc.sbuf_base // 32) * 32
        ST = [sb(f"st_{h}", [P, G, D], F32R) for h in ("hi", "lo")]

        def over(name, shape, at, room_at, room, dt=F32):
            size = 4
            for n in shape[1:]:
                size *= n
            assert at + size <= room
            return nc.alloc_sbuf_tensor_at(name, shape, dt, offset=room_at + at)

        def over_wb(name, shape, at):
            return over(name, shape, at, WB_at, 4 * 4 * D * 4)

        def over_st(name, shape, at):
            return over(name, shape, at, ST_at, 2 * G * D * 4)

        def over_up(name, shape, at, dt=F32):
            return over(name, shape, WA_ROOM + at, WA_at, 3 * WA_ROOM // 2, dt)

        KB = 1024
        WA_ROOM = 2 * 2 * 4 * D * 4
        raw_dn = over_wb("raw_dn", [P, 4, D], 0)
        kernels = over_wb("kernels", [K1, 2, S * S], 8 * KB)
        agg_out = over_wb("agg_out", [B, 2, S * S], 16 * KB)
        raw_up = over_wb("raw_up", [P, 4, D], 24 * KB)
        z2 = over_wb("z2", [ZS, NT * P], 0)
        w2T = over_wb("w2T", [E2, NG, G * P], 8 * KB)
        zp = over_wb("zp", [ZS, NG, G * P], 16 * KB)
        w3_raw = over_wb("w3_raw", [P, 4, D], 24 * KB)
        setup = over_st("setup", [P, S_ALL], 0)
        setup32 = over_st("setup32", [Z2, T_ALL], 7 * KB)
        hid = over_st("hid", [P, 2, 2, B], 14 * KB + 512)
        a3_raw = over_st("a3_raw", [P, 2, D], 0)
        b3_raw = over_st("b3_raw", [P, 2, D], 4 * KB)
        b3_scaled = over_st("b3_scaled", [P, 2, D], 8 * KB)
        bmat = over_st("bmat", [ZS + 2, D], 12 * KB)
        bmat_t = over_st("bmat_t", [ZS + 2, D], 14 * KB)
        rows3 = over_st("rows3", [P, G, D], 0)
        g1, g2, ge, gate = (over_up(n, [P, G, E1], j * KB) for j, n in enumerate(("g1", "g2", "ge", "gate")))
        scT = over_up("scT", [P, G * P], 4 * KB)
        sc1 = over_up("sc1", [P, G, E1], 14 * KB)
        sl_ring = over_up("sl_ring", [SLICES, G * P], 6 * KB)
        lg = over_up("lg", [P, 8, NT, E2], 8 * KB)
        anc = over_up("anc", [P, NT, 2 * E2], 12 * KB)
        ltop = over_up("ltop", [P, NT, 8], 13 * KB)

        x = sb("x", [P, NT, D])
        raw_org = x[:, NT - G:NT, :]
        F = sb("F", [P, G, D])
        Y = [sb(f"y_{h}", [P, R, G * P], F32R) for h in ("hi", "lo")]
        xf_at = -(-nc.sbuf_base // 32) * 32
        xf = sb("xf", [P, G, TB, M])
        ZP = over("zp_r", [ZS + 2, G * P], 0, xf_at, G * D * 4, F32R)
        BM = over("bmat_r", [ZS + 2, D], 2 * KB, xf_at, G * D * 4, F32R)
        XH = [sb(f"xhat_{h}", [P, 2, TB, M + 2], F32R) for h in ("hi", "lo")]
        conv_w = [[sb(f"conv{j}_{h}", [P, 3, P], F32R) for h in ("hi", "lo")] for j in range(2)]
        MX = sb("mix", [P, G, P])
        agg = sb("agg", [P, NT, S])
        y_bias = sb("y_bias", [P, B * S])
        sc_p = sb("sc_p", [GB, E0, 64])
        stage = sb("stage", [P, 2, D])

        cst = sb("cst", [P, C_ALL])
        ident = cst[:, C_IDENT:C_IDENT + P]
        ones = sb("ones", [1, P])
        ctx_b = sb("ctx_b", [P, 2, B])
        bias_out = sb("bias_out", [B, 2, S])
        kq0 = sb("kq0", [P, R, E0])
        KQ1 = [sb(f"kq1_{h}", [P, R, P], F32R) for h in ("hi", "lo")]
        SLW = [sb(f"slice_{h}", [P, R, SLICES], F32R) for h in ("hi", "lo")]
        bias3 = sb("bias3", [P, D])
        act_table = sb("act_table", [1, 1])
        att_nm = sb("att_nm", [B, 2])
        att_e = sb("att_e", [B, 2, K1])
        att_s = sb("att_s", [B, 2])
        att_r = sb("att_r", [B, 2])
        att = sb("att", [B, 2, K1])
        attT = sb("attT", [K1, 2, B])
        ysum = sb("ysum", [P, R, GB])
        sc_nm = sb("sc_nm", [GB, 1])
        sc_e = sb("sc_e", [GB, E0])
        sc_s = sb("sc_s", [GB, 1])
        sc_r = sb("sc_r", [GB, 1])
        coef = sb("coef", [P, 4, GB])
        top = sb("top", [P, G, 2, 8])
        g_nm = sb("g_nm", [P, G])
        g_s = sb("g_s", [P, G])
        g_r = sb("g_r", [P, G])
        amax = sb("amax", [P, 2])
        amax_all = sb("amax_all", [P, 2])
        ascale = sb("ascale", [P, 2])
        arecip = sb("arecip", [P, 2])
        lgs = sb("lgs", [P, 4, NT])
        e3w = sb("e3w", [P, 2])

        pb = [ctx.enter_context(nc.psum_tensor(f"bank{i}", [P, D], F32)) for i in range(8)]

        NAMES = """cst_in setup_in setup2_in kernels_in conv0_in conv2_in org_in dn_in up_in x_in stage_in w2s_in
            agg_stored agg_in out_done spill_done b3_in
            ones_set border_set kq1_zero conv_w_hi conv_w_lo ctx_ps ctx_ready
            tables_ps kq0_sb kq1_hi kq1_lo delta_slice_sb slice_w_hi slice_w_lo bias3_added gelu_table
            hid_ps hid_sb att_ps att_max att_exp att_inv att_ready attT_ps attT_sb
            bias_ps bias_sb bias_stored bias_in agg_ps agg_sb org_lo raw_hi raw_lo
            xh_hi xh_lo y_ps y_f yt_ps y_hi y_lo ysum_done
            sc0_ps sc0_max sc0_exp sc0_inv coef_p coef_ps coef_sb h_ps h_f h_hi h_lo ff_ps x_new rows_sb
            stage_hi stage_lo mx_ready
            sct_ps sct_sb sc1_ps sc1_sb top_a took_a top_b took_b top_neg gate_exp gate_sum gate_ready
            z_ps zg_f zt_ps zt_hi zt_lo
            sl_ps sl_sb z2_sb anc_ps anc_sb anc_max anc_all anc_eps anc_inv
            lg_step lg_exp lg_sig w_ready wT_ps wT_sb pm_ps zp_ready zp_hi zp_lo ones2_set bm_hi bm_lo bm_m bm_ready delta_ps delta_new
            e3_ready b3_ready w3_ps w3_f w3_hi w3_lo""".split()
        s = {n: sem(n) for n in NAMES}
        xf_in = [sem(f"xf_in{t}") for t in range(G)]

        block = ctx.enter_context(nc.Block())

        def upto(layer, i, t):
            return G * i + (layer * NT + t + 1)

        def mix_bank(i):
            return 4 + i if i else 0

        def alone(eng):
            eng.wait_ge(s["cst_in"], 16)

        def x_tile(i, t):
            return x[:, bass.ds(i * G + t, 1), :].rearrange("p a n -> p (a n)")

        def conv_view(v):
            return v.rearrange("p (b r o) -> p r b o", b=TB, r=R)

        def y_view(v, t):
            return v[:, :, t * P:(t + 1) * P].rearrange("p r (b o) -> p r b o", b=TB)

        @block.sync
        def _(sp):
            sp.dma_start(stage[:, 0, 0:3 * P], t_in["conv0"]).then_inc(s["conv0_in"], 16)
            xh_dram = t_in["x"].rearrange("(n b) i r m -> n (i r) b m", b=TB)
            sp.dma_start(xf[:, 0], xh_dram[0]).then_inc(xf_in[0], 16)
            sp.dma_start(xf[:, 1], xh_dram[1]).then_inc(xf_in[1], 16)
            sp.dma_start(setup[:, S_WQ0:S_ALL], t_in["setup"][:, S_WQ0:S_ALL]).then_inc(s["setup2_in"], 16)
            sp.dma_start(setup32[:, :], t_in["setup32"]).then_inc(s["setup2_in"], 16)
            sp.dma_start(raw_org, t_in["worg"]).then_inc(s["org_in"], 16)
            sp.dma_start(xf[:, 2], xh_dram[2]).then_inc(xf_in[2], 16)
            sp.dma_start(xf[:, 3], xh_dram[3]).then_inc(xf_in[3], 16)
            sp.dma_start(kernels[:, :, :], t_in["kernels"]).then_inc(s["kernels_in"], 16)
            sp.dma_start(stage[:, 1, 0:3 * P], t_in["conv2"]).then_inc(s["conv2_in"], 16)
            sp.dma_start(raw_dn[:, :, :], t_in["lora_dn"]).then_inc(s["dn_in"], 16)
            sp.dma_start(raw_up[:, :, :], t_in["lora_up"]).then_inc(s["up_in"], 16)
            a1_dram = t_in["a1"].rearrange("p (c n) -> p c n", c=4)
            b1_dram = t_in["b1"].rearrange("p (c n) -> p c n", c=4)
            x_tok = t_in["x"].rearrange("(n b) i r m -> (b i) n (r m)", b=TB)
            for i in range(NG):
                if i == NG - 1:
                    sp.wait_ge(s["org_lo"], 4)
                sp.dma_start(x[:, G * i:G * i + G, :], x_tok[:, G * i:G * i + G, :]).then_inc(s["x_in"], 16)
            def next_xhat(i):
                for t in range(G):
                    sp.wait_ge(s["xh_lo"], upto(0, i, t))
                    sp.dma_start(xf[:, t], xh_dram[bass.ds(i * G + (G + t), 1)].rearrange("a p b m -> (a p) b m")).then_inc(xf_in[t], 16)

            def stage1_in(i, first=False):
                if first:
                    sp.wait_ge(s["conv_w_lo"], 2)
                else:
                    sp.wait_ge(s["stage_lo"], 2 * i)
                for j, w in enumerate((a1_dram, b1_dram)):
                    sp.dma_start(stage[:, j], w[:, bass.ds(i, 1), :].rearrange("p a n -> p (a n)")).then_inc(s["stage_in"], 16)

            next_xhat(0)
            sp.wait_ge(s["agg_sb"], 4)
            for j in range(2):
                sp.dma_start(scratch_agg[j], agg_out[:, j, :]).then_inc(s["agg_stored"], 16)
            sp.wait_ge(s["agg_stored"], 32)
            agg_dram = scratch_agg.rearrange("j (n b) (i o) -> j (b i) n o", b=TB, o=S)
            sp.dma_start(agg[:, :, :], agg_dram[0]).then_inc(s["agg_in"], 16)
            stage1_in(0, first=True)
            with sp.Fori(1, NG - 1) as i:
                stage1_in(i)
                next_xhat(i)
            stage1_in(NG - 1)
            sp.wait_ge(s["bias_sb"], 1)
            for j in range(2):
                sp.dma_start(scratch_bias[j], bias_out[:, j, :]).then_inc(s["bias_stored"], 16)
            sp.wait_ge(s["bias_stored"], 32)
            bias_dram = scratch_bias.rearrange("j b (a o) -> j a (b o)", a=1)
            sp.dma_start(y_bias[:, :], bias_dram[0].broadcast_to((P, B * S))).then_inc(s["bias_in"], 16)
            spill = scratch.rearrange("(n b) i r m -> n (b i) (r m)", b=TB)
            refill = scratch.rearrange("(n b) i r m -> n (i r) b m", b=TB)
            w2_dram = t_in["w2"].rearrange("p (c n) -> p c n", c=4)
            with sp.Fori(0, NG - 1) as i:
                sp.wait_ge(s["stage_lo"], i + 2 * NG)
                sp.dma_start(stage[:, 0], w2_dram[:, bass.ds(i, 1), :].rearrange("p a n -> p (a n)")).then_inc(s["w2s_in"], 16)
                for t in range(G):
                    sp.wait_ge(s["x_new"], upto(1, i, t))
                    sp.dma_start(spill[bass.ds(i * G + t, 1)].rearrange("a p n -> (a p) n"), x_tile(i, t)).then_inc(s["spill_done"], 16)
            sp.wait_ge(s["stage_lo"], 3 * NG - 1)
            sp.dma_start(stage[:, 0], w2_dram[:, NG - 1, :]).then_inc(s["w2s_in"], 16)
            for t in range(G):
                sp.wait_ge(s["y_ps"], upto(1, NG - 1, t))
                sp.wait_ge(s["spill_done"], 16 * (NT - G))
                sp.dma_start(xf[:, t], refill[t]).then_inc(xf_in[t], 16)
            for t in range(G):
                sp.wait_ge(s["x_new"], upto(1, NG - 1, t))
                sp.dma_start(spill[NT - G + t], x[:, NT - G + t, :]).then_inc(s["spill_done"], 16)
            sp.dma_start(a3_raw[:, :, :], t_in["a3"]).then_inc(s["b3_in"], 16)
            sp.dma_start(b3_raw[:, :, :], t_in["b3"]).then_inc(s["b3_in"], 16)
            sp.dma_start(w3_raw[:, :, :], t_in["w3"]).then_inc(s["b3_in"], 16)
            sp.dma_start(bmat[:, :], t_in["bmat"]).then_inc(s["b3_in"], 16)
            sp.dma_start(bias3[:, :], t_in["bias3"].broadcast_to((P, D))).then_inc(s["b3_in"], 16)
            sp.wait_ge(s["mx_ready"], NG)
            sp.dma_start(agg[:, :, :], agg_dram[1]).then_inc(s["agg_in"], 16)
            sp.wait_ge(s["y_f"], 2 * NT)
            sp.dma_start(y_bias[:, :], bias_dram[1].broadcast_to((P, B * S))).then_inc(s["bias_in"], 16)
            sp.wait_ge(s["spill_done"], 16 * NT)
            with sp.Fori(0, NG - 1) as i:
                for t in range(G):
                    sp.wait_ge(s["xh_lo"], upto(1, i, t))
                    sp.dma_start(xf[:, t], refill[bass.ds(i * G + (G + t), 1)].rearrange("a p b m -> (a p) b m")).then_inc(xf_in[t], 16)
            out_tok = out.rearrange("(n b) i r m -> n (b i) (r m)", b=TB)
            with sp.Fori(0, NG) as i:
                for t in range(G):
                    sp.wait_ge(s["x_new"], upto(3, i, t))
                    sp.dma_start(out_tok[bass.ds(i * G + t, 1)].rearrange("a p n -> (a p) n"), x_tile(i, t)).then_inc(s["out_done"], 16)
            sp.wait_ge(s["out_done"], 16 * NT)

        @block.scalar
        def _(act):
            copy = nc.scalar.activation

            act.dma_start(setup[:, 0:S_WQ0], t_in["setup"][:, 0:S_WQ0]).then_inc(s["setup_in"], 16)
            act.dma_start(cst[:, :], t_in["cst"]).then_inc(s["cst_in"], 16)
            act.wait_ge(s["ones_set"], 1)
            nc.scalar.activation(act_table[:, :], ones[0:1, 0:1], ACT.Gelu).then_inc(s["gelu_table"], 1)

            def conv_w_hi(j):
                copy(conv_w[j][0][:, :, :].rearrange("p a n -> p (a n)"), stage[:, j, 0:3 * P], ACT.Copy).then_inc(s["conv_w_hi"], 1)

            def xhat_hi(layer, i, t):
                act.wait_ge(xf_in[t], 16 * i + 16 * (layer // 2 * NG + 1))
                copy(XH[0][:, t % 2, :, 1:M + 1], xf[:, t], ACT.Copy).then_inc(s["xh_hi"], 1)

            def conv_y_hi(layer, i, t):
                act.wait_ge(s["yt_ps"], upto(layer // 2, i, t))
                copy(y_view(Y[0], t), conv_view(pb[4 + t][:, :]), ACT.Copy).then_inc(s["y_hi"], 1)

            def gelu(k):
                for j in range(2):
                    act.wait_ge(s["hid_ps"], 2 * k + 2)
                    copy(hid[:, j, k, :], pb[6][:, (2 * k + j) * B:(2 * k + j + 1) * B], ACT.Gelu,
                         bias=cst[:, C_MB + 2 * j + k:C_MB + 2 * j + k + 1]).then_inc(s["hid_sb"], 1)

            def raw_hi(j, raw, c):
                copy(WA[j][0][:, c], raw[:, c, :], ACT.Copy).then_inc(s["raw_hi"], 1)

            def exp0(i):
                act.wait_ge(s["sc0_max"], i + 1)
                copy(sc_e[:, :], pb[0][0:GB, 0:E0], ACT.Exp, bias=sc_nm[:, 0:1], accum_out=sc_s[:, 0:1]).then_inc(s["sc0_exp"], 1)
                act.wait_ge(s["coef_ps"], i + 1)
                copy(coef[:, :, :], pb[1][:, 0:4 * GB].rearrange("p (c b) -> p c b", c=4), ACT.Copy).then_inc(s["coef_sb"], 1)

            def h_hi(i):
                for c in range(4):
                    act.wait_ge(s["h_f"], 4 * i + (c + 1))
                    copy(ST[0][:, c], F[:, c], ACT.Copy).then_inc(s["h_hi"], 1)

            def stage_hi(dst, i, slot):
                copy(dst[:, bass.ds(i, 1), :].rearrange("p a n -> p (a n)"), stage[:, slot], ACT.Copy).then_inc(s["stage_hi"], 1)

            def stage1_hi(i):
                act.wait_ge(s["stage_in"], 32 * i + 32)
                stage_hi(a1[0], i, 0)
                stage_hi(b1[0], i, 1)

            act.wait_ge(s["conv0_in"], 16)
            conv_w_hi(0)
            xhat_hi(0, 0, 0)
            xhat_hi(0, 0, 1)
            act.wait_ge(s["cst_in"], 16)
            gelu(0)
            gelu(1)
            act.wait_ge(s["org_in"], 16)
            for c in range(4):
                raw_hi(0, raw_org, c)
            act.wait_ge(s["y_ps"], 1)
            xhat_hi(0, 0, 2)
            act.wait_ge(s["y_ps"], 2)
            xhat_hi(0, 0, 3)
            conv_y_hi(0, 0, 0)
            act.wait_ge(s["tables_ps"], 3)
            copy(kq0[:, :, :], pb[5][:, 0:R * E0].rearrange("p (r e) -> p r e", r=R), ACT.Copy,
                 scale=1.0 / (S * float(P) ** 0.5)).then_inc(s["kq0_sb"], 1)
            slices = setup[:, S_SLICE:S_ALL].rearrange("p (r e) -> p r e", r=R)
            copy(slices[:, :, ZS:ZS + E2], pb[5][:, R * E0:R * (E0 + E2)].rearrange("p (r e) -> p r e", r=R), ACT.Copy)\
                .then_inc(s["delta_slice_sb"], 1)
            act.wait_ge(s["kq1_zero"], 2)
            copy(KQ1[0][:, :, 0:E1], pb[5][:, 64:64 + R * E1].rearrange("p (r e) -> p r e", r=R), ACT.Copy).then_inc(s["kq1_hi"], 1)
            for j in range(2):
                act.wait_ge(s["att_max"], 2)
                copy(att_e[:, j, :], pb[6][0:B, 4 * B + j * K1:4 * B + (j + 1) * K1], ACT.Exp, bias=att_nm[:, j:j + 1],
                     accum_out=att_s[:, j:j + 1]).then_inc(s["att_exp"], 1)
            conv_y_hi(0, 0, 1)
            conv_y_hi(0, 0, 2)
            act.wait_ge(s["attT_ps"], 1)
            copy(attT[:, :, :], pb[7][0:K1, 0:2 * B].rearrange("p (j b) -> p j b", j=2), ACT.Copy).then_inc(s["attT_sb"], 1)
            conv_y_hi(0, 0, 3)
            for j, (raw, loaded) in enumerate(((raw_dn, "dn_in"), (raw_up, "up_in"))):
                act.wait_ge(s[loaded], 16)
                for c in range(4):
                    raw_hi(1 + j, raw, c)
                for h in range(2):
                    act.wait_ge(s["agg_ps"], 2 * j + h + 1)
                    copy(agg_out[:, j, h * D:(h + 1) * D], pb[2 * j + h][0:B, :], ACT.Copy).then_inc(s["agg_sb"], 1)
            act.wait_ge(s["bias_ps"], 1)
            copy(bias_out[:, :, :], pb[2][0:B, 0:2 * S].rearrange("p (j o) -> p j o", j=2), ACT.Copy).then_inc(s["bias_sb"], 1)
            exp0(0)
            act.wait_ge(s["delta_slice_sb"], 1)
            copy(SLW[0][:, :, :], slices, ACT.Copy).then_inc(s["slice_w_hi"], 1)
            act.wait_ge(s["conv2_in"], 16)
            conv_w_hi(1)
            act.wait_ge(s["slice_w_lo"], 1)
            h_hi(0)
            act.wait_ge(s["raw_lo"], 8)
            act.wait_ge(s["agg_stored"], 32)
            stage1_hi(0)

            def conv_layer(layer, i):
                for t in range(2):
                    xhat_hi(layer, i, t)
                for t in range(2, G):
                    act.wait_ge(s["y_ps"], upto(layer, i, t - 2))
                    xhat_hi(layer, i, t)
                for t in range(G):
                    conv_y_hi(layer, i, t)

            with act.Fori(1, NG) as i:
                conv_layer(0, i)
                exp0(i)
                h_hi(i)
                stage1_hi(i)

            def row_copy(layer, i, t):
                act.wait_ge(s["y_ps"], upto(layer, i, t) - G)
                if layer == 1:
                    act.wait_ge(s["xh_lo"], NT)
                    act.wait_ge(s["x_new"], upto(0, i, t))
                else:
                    act.wait_ge(s["delta_new"], G * i + (t + 1))
                rows = xf[:, t].rearrange("p b m -> p (b m)") if layer == 1 else rows3[:, t]
                copy(rows, x_tile(i, t), ACT.Copy).then_inc(s["rows_sb"], 1)

            def mix_y_hi(layer, i, t):
                act.wait_ge(s["y_f"], upto(layer, i, t))
                copy(Y[0][:, :, t * P:(t + 1) * P], F[:, t].rearrange("p (r n) -> p r n", r=R), ACT.Copy).then_inc(s["y_hi"], 1)

            with act.Fori(0, NG) as i:
                for t in range(G):
                    row_copy(1, i, t)
                for t in range(G):
                    mix_y_hi(1, i, t)
                act.wait_ge(s["sct_ps"], i + 1)
                for h in range(2):
                    half = slice(h * G * P // 2, (h + 1) * G * P // 2)
                    copy(scT[:, half], pb[0][:, half], ACT.Copy).then_inc(s["sct_sb"], 1)
                for t in range(G):
                    act.wait_ge(s["top_neg"], i + 1)
                    copy(ge[:, t], sc1[:, t], ACT.Exp, bias=g_nm[:, t:t + 1]).then_inc(s["gate_exp"], 1)
                act.wait_ge(s["w2s_in"], 16 * i + 16)
                stage_hi(w2[0], i, 0)
                for t in range(G):
                    act.wait_ge(s["zt_ps"], G * i + (t + 1))
                    copy(ST[0][:, t], pb[t][:, :], ACT.Copy).then_inc(s["zt_hi"], 1)

            with act.Fori(0, NG) as i:
                conv_layer(2, i)
                act.wait_ge(s["sl_ps"], i + 1)
                copy(sl_ring[ZS:SLICES, :].rearrange("p (j two) -> p j two", two=2),
                     pb[0][ZS:SLICES, :].rearrange("p (j two) -> p j two", two=2)[:, :, 1:2].broadcast_to((2 * E2, G * P // 2, 2)),
                     ACT.Identity, bias=cst[ZS:SLICES, C_SB:C_SB + 1]).then_inc(s["sl_sb"], 1)

            act.wait_ge(s["b3_in"], 80)
            act.wait_ge(s["y_ps"], 3 * NT)
            copy(BM[:, :], bmat[:, :], ACT.Copy).then_inc(s["bm_hi"], 1)
            act.wait_ge(s["lg_step"], 4)
            copy(lg[:, 3], lg[:, 2], ACT.Exp).then_inc(s["lg_exp"], 1)
            act.wait_ge(s["lg_step"], 8)
            copy(lg[:, 6], lg[:, 5], ACT.Exp, scale=-2.0).then_inc(s["lg_sig"], 1)

            def mix_w_sb(i):
                act.wait_ge(s["wT_ps"], i + 1)
                copy(w2T[:, i], pb[mix_bank(i)][0:E2, :], ACT.Copy).then_inc(s["wT_sb"], 1)

            def zp_hi(i):
                act.wait_ge(s["zp_ready"], i + 1)
                copy(ZP[0:ZS, :], zp[:, i], ACT.Copy).then_inc(s["zp_hi"], 1)

            def w3_hi(c):
                act.wait_ge(s["w3_f"], c + 1)
                copy(w3[0][:, c], w3_raw[:, c], ACT.Copy).then_inc(s["w3_hi"], 1)

            mix_w_sb(0)
            w3_hi(0)
            mix_w_sb(1)
            zp_hi(0)
            w3_hi(1)
            w3_hi(2)

            row_copy(3, 0, 0)
            row_copy(3, 0, 1)
            w3_hi(3)
            mix_w_sb(2)
            mix_w_sb(3)
            row_copy(3, 0, 2)
            row_copy(3, 0, 3)
            for t in range(G):
                mix_y_hi(3, 0, t)
            with act.Fori(1, NG) as i:
                act.wait_ge(s["delta_ps"], G * i)
                act.wait_ge(s["zp_ready"], NG)
                copy(ZP[0:ZS, :], zp[:, bass.ds(i, 1), :].rearrange("p a n -> p (a n)"), ACT.Copy).then_inc(s["zp_hi"], 1)
                for t in range(G):
                    row_copy(3, i, t)
                for t in range(G):
                    mix_y_hi(3, i, t)

        @block.gpsimd
        def _(pool):
            def lo(dst, v, hi):
                return nc.gpsimd.tensor_tensor(dst, v, hi.bitcast(F32), ALU.subtract)

            def conv_w_lo(j):
                pool.wait_ge(s["conv_w_hi"], j + 1)
                lo(conv_w[j][1][:, :, :].rearrange("p a n -> p (a n)"), stage[:, j, 0:3 * P],
                   conv_w[j][0][:, :, :].rearrange("p a n -> p (a n)")).then_inc(s["conv_w_lo"], 1)

            def xhat_lo(layer, i, t):
                pool.wait_ge(s["xh_hi"], upto(layer // 2, i, t))
                lo(XH[1][:, t % 2, :, 1:M + 1], xf[:, t], XH[0][:, t % 2, :, 1:M + 1]).then_inc(s["xh_lo"], 1)

            def raw_lo(j, raw, c):
                pool.wait_ge(s["raw_hi"], 4 * j + c + 1)
                lo(WA[j][1][:, c], raw[:, c, :], WA[j][0][:, c]).then_inc(s["raw_lo"], 1)

            def h_lo(i):
                for c in range(4):
                    pool.wait_ge(s["h_hi"], 4 * i + (c + 1))
                    lo(ST[1][:, c], F[:, c], ST[0][:, c]).then_inc(s["h_lo"], 1)

            def stage_lo(w, i, slot, n):
                pool.wait_ge(s["stage_hi"], n)
                lo(w[1][:, bass.ds(i, 1), :].rearrange("p a n -> p (a n)"), stage[:, slot],
                   w[0][:, bass.ds(i, 1), :].rearrange("p a n -> p (a n)")).then_inc(s["stage_lo"], 1)

            pool.wait_ge(s["xh_lo"], 2)
            for t in range(2, G):
                xhat_lo(0, 0, t)
            for c in range(4):
                raw_lo(1, raw_dn, c)
            for c in range(4):
                raw_lo(2, raw_up, c)
            conv_w_lo(1)
            h_lo(0)
            for j, w in enumerate((a1, b1)):
                stage_lo(w, 0, j, j + 1)
            with pool.Fori(1, NG) as i:
                for t in range(G):
                    xhat_lo(0, i, t)
                h_lo(i)
                for j, w in enumerate((a1, b1)):
                    stage_lo(w, i, j, 2 * i + (j + 1))

            def mixing(layer, i):
                pool.wait_ge(s["y_ps"], upto(layer, i, G - 1) - G)
                nc.gpsimd.tensor_tensor(
                    MX[:, :, :].rearrange("p t (b o) -> p t b o", b=TB),
                    agg[:, bass.ds(i * G, G), :].unsqueeze(2).broadcast_to((P, G, TB, S)),
                    cst[:, C_BLK:C_BLK + TB].unsqueeze(1).unsqueeze(3).broadcast_to((P, G, TB, S)), ALU.mult).then_inc(s["mx_ready"], 1)

            pool.wait_ge(s["agg_in"], 16)
            with pool.Fori(0, NG) as i:
                mixing(1, i)
                stage_lo(w2, i, 0, i + (2 * NG + 1))

            with pool.Fori(0, NG) as i:
                for t in range(G):
                    xhat_lo(2, i, t)

            pool.wait_ge(s["xh_lo"], 2 * NT)
            nc.gpsimd.memset(ZP[ZS:ZS + 2, :].bitcast(F32), 1.0).then_inc(s["ones2_set"], 1)
            pool.wait_ge(s["bm_hi"], 1)
            pool.wait_ge(s["ones2_set"], 1)
            lo(BM[2 * Z2:ZS, :], bmat[2 * Z2:ZS, :], BM[2 * Z2:ZS, :]).then_inc(s["bm_lo"], 1)

            pool.wait_ge(s["anc_max"], 2)
            pool.wait_ge(s["bm_lo"], 1)
            nc.gpsimd.partition_all_reduce(amax_all[:, :], amax[:, :], P, bass.bass_isa.ReduceOp.max).then_inc(s["anc_all"], 1)

            def add_bias(i):
                for t in range(G):
                    pool.wait_ge(s["rows_sb"], upto(1, i, t))
                    nc.gpsimd.tensor_tensor(x_tile(i, t), x_tile(i, t), bias3[:, :], ALU.add).then_inc(s["bias3_added"], 1)

            pool.wait_ge(s["agg_in"], 32)
            mixing(3, 0)
            for c in range(4):
                pool.wait_ge(s["w3_hi"], c + 1)
                lo(w3[1][:, c], w3_raw[:, c], w3[0][:, c]).then_inc(s["w3_lo"], 1)
            pool.wait_ge(s["b3_in"], 80)
            add_bias(0)
            with pool.Fori(1, NG) as i:
                mixing(3, i)
                add_bias(i)

        @block.vector
        def _(dve):
            tt, stt, ts = nc.vector.tensor_tensor, nc.vector.scalar_tensor_tensor, nc.vector.tensor_scalar

            nc.vector.memset(ones[:, :], 1.0).then_inc(s["ones_set"], 1)
            for w in KQ1:
                nc.vector.memset(w[:, :, :].bitcast(F32), 0.0).then_inc(s["kq1_zero"], 1)
            for h in range(2):
                nc.vector.memset(XH[h][:, :, :, 0:M + 2:M + 1].bitcast(F32), 0.0).then_inc(s["border_set"], 1)

            def conv_y(layer, i, t):
                dve.wait_ge(s["y_ps"], upto(layer, i, t))
                tt(F[:, t].rearrange("p (b m) -> p b m", b=TB), pb[t][:, :].rearrange("p (b m) -> p b m", b=TB),
                   ctx_b[:, layer // 2, bass.ds(i * GB + t * TB, TB)].unsqueeze(2).broadcast_to((P, TB, M)),
                   ALU.add).then_inc(s["y_f"], 1)

            def conv_y_lo(layer, i, t):
                dve.wait_ge(s["y_hi"], upto(layer, i, t))
                tt(y_view(Y[1], t), conv_view(pb[4 + t][:, :]), y_view(Y[0], t).bitcast(F32), ALU.subtract).then_inc(s["y_lo"], 1)

            def sum_rows(t):
                nc.vector.reduce_sum(ysum[:, :, t * TB:(t + 1) * TB], conv_view(pb[4 + t][:, :]), AX.X).then_inc(s["ysum_done"], 1)

            def add_to_x(layer, i, t, scale=None):
                dve.wait_ge(s["ff_ps"], upto(layer, i, t))
                if layer == 3:
                    dve.wait_ge(s["bias3_added"], G * i + (t + 1))
                xt = x_tile(i, t)
                if scale:
                    stt(xt, pb[4 + t][:, :], scale, xt, ALU.mult, ALU.add).then_inc(s["x_new"], 1)
                else:
                    tt(xt, pb[4 + t][:, :], xt, ALU.add).then_inc(s["x_new"], 1)

            def softmax0(i):
                dve.wait_ge(s["sc0_ps"], i + 1)
                nc.vector.reduce_max(sc_nm[:, :], pb[0][0:GB, 0:E0], AX.X, negate=True).then_inc(s["sc0_max"], 1)
                dve.wait_ge(s["sc0_exp"], i + 1)
                nc.vector.reciprocal(sc_r[:, :], sc_s[:, :]).then_inc(s["sc0_inv"], 1)
                dve.wait_ge(s["sc0_inv"], i + 1)
                ts(sc_p[:, :, :], sc_e[:, :].unsqueeze(2).broadcast_to((GB, E0, 64)), sc_r[:, 0:1], None, ALU.mult).then_inc(s["coef_p"], 1)

            def experts0(i):
                dve.wait_ge(s["coef_sb"], i + 1)
                for c in range(4):
                    dve.wait_ge(s["h_ps"], 4 * i + (c + 1))
                    tt(F[:, c].rearrange("p (b o) -> p b o", b=GB), pb[(c + 2) % 4][:, :].rearrange("p (b o) -> p b o", b=GB),
                       coef[:, c, :].unsqueeze(2).broadcast_to((P, GB, S)), ALU.mult).then_inc(s["h_f"], 1)
                dve.wait_ge(s["x_in"], 16 * NG)
                for t in range(G):
                    add_to_x(0, i, t)

            dve.wait_ge(s["conv_w_hi"], 1)
            tt(conv_w[0][1][:, :, :].rearrange("p a n -> p (a n)"), stage[:, 0, 0:3 * P],
               conv_w[0][0][:, :, :].rearrange("p a n -> p (a n)").bitcast(F32), ALU.subtract).then_inc(s["conv_w_lo"], 1)
            for t in range(2):
                dve.wait_ge(s["xh_hi"], t + 1)
                dve.wait_ge(s["border_set"], 2)
                tt(XH[1][:, t, :, 1:M + 1], xf[:, t], XH[0][:, t, :, 1:M + 1].bitcast(F32), ALU.subtract).then_inc(s["xh_lo"], 1)
            dve.wait_ge(s["cst_in"], 16)
            dve.wait_ge(s["ctx_ps"], 1)
            ts(ctx_b[:, :, :], pb[7][:, 0:2 * B].rearrange("p (j b) -> p j b", j=2), cst[:, C_FSIDE:C_FSIDE + 1], None, ALU.add)\
                .then_inc(s["ctx_ready"], 1)
            dve.wait_ge(s["ctx_ready"], 1)
            conv_y(0, 0, 0)
            for c in range(4):
                dve.wait_ge(s["raw_hi"], c + 1)
                tt(worg[1][:, c], raw_org[:, c, :], worg[0][:, c].bitcast(F32), ALU.subtract).then_inc(s["org_lo"], 1)
            conv_y(0, 0, 1)
            dve.wait_ge(s["att_ps"], 1)
            for j in range(2):
                nc.vector.reduce_max(att_nm[:, j:j + 1], pb[6][0:B, 4 * B + j * K1:4 * B + (j + 1) * K1], AX.X, negate=True)\
                    .then_inc(s["att_max"], 1)
            dve.wait_ge(s["kq1_hi"], 1)
            tt(KQ1[1][:, :, 0:E1], pb[5][:, 64:64 + R * E1].rearrange("p (r e) -> p r e", r=R), KQ1[0][:, :, 0:E1].bitcast(F32),
               ALU.subtract).then_inc(s["kq1_lo"], 1)
            conv_y(0, 0, 2)
            conv_y_lo(0, 0, 0)
            sum_rows(0)
            for j in range(2):
                dve.wait_ge(s["att_exp"], j + 1)
                nc.vector.reciprocal(att_r[:, j:j + 1], att_s[:, j:j + 1]).then_inc(s["att_inv"], 1)
            for j in range(2):
                dve.wait_ge(s["att_inv"], j + 1)
                ts(att[:, j, :], att_e[:, j, :], att_r[:, j:j + 1], None, ALU.mult).then_inc(s["att_ready"], 1)
            conv_y_lo(0, 0, 1)
            sum_rows(1)
            conv_y(0, 0, 3)
            for t in range(2, G):
                conv_y_lo(0, 0, t)
                sum_rows(t)
            softmax0(0)
            dve.wait_ge(s["slice_w_hi"], 1)
            tt(SLW[1][:, :, :], setup[:, S_SLICE:S_ALL].rearrange("p (r e) -> p r e", r=R), SLW[0][:, :, :].bitcast(F32),
               ALU.subtract).then_inc(s["slice_w_lo"], 1)
            tt(e3w[:, :], cst[:, C_E3:C_E3 + 2], cst[:, C_E3 + 2:C_E3 + 4], ALU.mult).then_inc(s["e3_ready"], 1)
            experts0(0)

            with dve.Fori(1, NG) as i:
                conv_y(0, i, 0)
                for t in range(G):
                    if t < G - 1:
                        conv_y(0, i, t + 1)
                    conv_y_lo(0, i, t)
                    sum_rows(t)
                softmax0(i)
                experts0(i)

            def mix_y(layer, i, t):
                dve.wait_ge(s["y_ps"], upto(layer, i, t))
                tt(F[:, t].rearrange("p (r n) -> p r n", r=R), pb[t][:, :].rearrange("p (r n) -> p r n", r=R),
                   y_bias[:, bass.ds((i * G + t) * P, P)].unsqueeze(1).broadcast_to((P, R, P)), ALU.add).then_inc(s["y_f"], 1)

            def mix_y_lo(layer, i, t):
                dve.wait_ge(s["y_hi"], upto(layer, i, t))
                tt(Y[1][:, :, t * P:(t + 1) * P], F[:, t].rearrange("p (r n) -> p r n", r=R),
                   Y[0][:, :, t * P:(t + 1) * P].bitcast(F32), ALU.subtract).then_inc(s["y_lo"], 1)

            dve.wait_ge(s["bias_in"], 16)
            with dve.Fori(0, NG) as i:
                group_no = dve.snap(i + 1)
                tile_no = [dve.snap(G * i + (t + 1)) for t in range(G)]

                def zt_lo(t):
                    dve.wait_ge(s["zt_hi"], tile_no[t])
                    tt(ST[1][:, t], pb[t][:, :], ST[0][:, t].bitcast(F32), ALU.subtract).then_inc(s["zt_lo"], 1)

                mix_y(1, i, 0)
                for t in range(1, G):
                    mix_y(1, i, t)
                    mix_y_lo(1, i, t - 1)
                mix_y_lo(1, i, G - 1)
                dve.wait_ge(s["sc1_ps"], group_no)
                nc.vector.tensor_copy(sc1[:, :, :], pb[1][:, :].rearrange("p (t e) -> p t e", t=G)[:, :, 0:E1]).then_inc(s["sc1_sb"], 1)
                alone(dve)
                dve.wait_ge(s["sc1_sb"], group_no)
                for t in range(G):
                    nc.vector.max(top[:, t, 0], sc1[:, t]).then_inc(s["top_a"], 1)
                dve.wait_ge(s["top_a"], tile_no[G - 1])
                ts(g_nm[:, :].unsqueeze(2), top[:, :, 0, 0:1], -1.0, None, ALU.mult).then_inc(s["top_neg"], 1)
                for t in range(G):
                    nc.vector.match_replace(g1[:, t], top[:, t, 0], sc1[:, t], TAKEN).then_inc(s["took_a"], 1)
                alone(dve)
                dve.wait_ge(s["took_a"], tile_no[G - 1])
                for t in range(G):
                    nc.vector.max(top[:, t, 1], g1[:, t]).then_inc(s["top_b"], 1)
                alone(dve)
                dve.wait_ge(s["top_b"], tile_no[G - 1])
                for t in range(G):
                    nc.vector.match_replace(g2[:, t], top[:, t, 1], g1[:, t], TAKEN).then_inc(s["took_b"], 1)
                dve.wait_ge(s["took_b"], tile_no[G - 1])
                for t in range(G):
                    dve.wait_ge(s["gate_exp"], tile_no[t])
                    stt(gate[:, t], g2[:, t], TAKEN, ge[:, t], ALU.is_equal, ALU.mult, accum_out=g_s[:, t:t + 1])\
                        .then_inc(s["gate_sum"], 1)
                dve.wait_ge(s["gate_sum"], tile_no[G - 1])
                nc.vector.reciprocal(g_r[:, :], g_s[:, :]).then_inc(s["gate_ready"], 1)
                dve.wait_ge(s["gate_ready"], group_no)
                for t in range(G):
                    if t == G - 1:
                        zt_lo(0)
                    dve.wait_ge(s["z_ps"], tile_no[t])
                    stt(F[:, t].rearrange("p (e r) -> p e r", e=E1), pb[4 + t][:, :].rearrange("p (e r) -> p e r", e=E1),
                        g_r[:, t:t + 1], gate[:, t].unsqueeze(2).broadcast_to((P, E1, RANK1)), ALU.mult, ALU.mult)\
                        .then_inc(s["zg_f"], 1)
                for t in range(1, G):
                    zt_lo(t)
                for t in range(G):
                    add_to_x(1, i, t, scale=2.0)

            def split_b():
                ts(bmat_t[ZS:ZS + 2, :], BM[ZS:ZS + 2, :].bitcast(F32), cst[ZS:ZS + 2, C_LO:C_LO + 1], None, ALU.mult).then_inc(s["bm_m"], 1)
                dve.wait_ge(s["bm_m"], 1)
                stt(BM[ZS:ZS + 2, :], bmat[ZS:ZS + 2, :], cst[ZS:ZS + 2, C_LO + 1:C_LO + 2], bmat_t[ZS:ZS + 2, :], ALU.mult, ALU.add)\
                    .then_inc(s["bm_ready"], 1)

            def conv2_y(i, last=False):
                conv_y(2, i, 0)
                conv_y(2, i, 1)
                conv_y(2, i, 2)
                conv_y_lo(2, i, 0)
                conv_y(2, i, 3)
                for t in range(1, G):
                    conv_y_lo(2, i, t)
                add_to_x(2, i, 0)
                dve.wait_ge(s["sl_ps"], i + 1)
                ts(z2[:, bass.ds(i * (G * P), G * P)], pb[0][0:ZS, :], 1.0, None, ALU.mult).then_inc(s["z2_sb"], 1)
                if not last:
                    add_to_x(2, i, 1)
                dve.wait_ge(s["anc_ps"], i + 1)
                nc.vector.tensor_copy(anc[:, bass.ds(i * G, G), :], pb[1][:, 0:G * 2 * E2].rearrange("p (t e) -> p t e", t=G))\
                    .then_inc(s["anc_sb"], 1)

            with dve.Fori(0, NG - 1) as i:
                conv2_y(i)
                add_to_x(2, i, 2)
                add_to_x(2, i, 3)
            dve.wait_ge(s["b3_in"], 80)
            dve.wait_ge(s["e3_ready"], 1)
            for c in range(2):
                ts(b3_scaled[:, c], b3_raw[:, c], e3w[:, c:c + 1], None, ALU.mult).then_inc(s["b3_ready"], 1)
            conv2_y(NG - 1, last=True)

            dve.wait_ge(s["anc_sb"], NG)
            for h in range(2):
                nc.vector.tensor_reduce(amax[:, h:h + 1], anc[:, :, h * E2:(h + 1) * E2], AX.XY, ALU.max,
                                        apply_absolute_value=True).then_inc(s["anc_max"], 1)
            add_to_x(2, NG - 1, 1)
            dve.wait_ge(s["anc_all"], 1)
            ts(ascale[:, :], amax_all[:, :], EPS, 2.0, ALU.max, ALU.mult).then_inc(s["anc_eps"], 1)
            dve.wait_ge(s["anc_eps"], 1)
            nc.vector.reciprocal(arecip[:, :], ascale[:, :]).then_inc(s["anc_inv"], 1)
            dve.wait_ge(s["anc_inv"], 1)

            step = [0]

            def then(ins):
                step[0] += 1
                ins.then_inc(s["lg_step"], 1)
                dve.wait_ge(s["lg_step"], step[0])

            def per_tile(v):
                return v.unsqueeze(2).broadcast_to((P, NT, E2))

            then(ts(lg[:, 0], anc[:, :, 0:E2], arecip[:, 0:1], None, ALU.mult))
            then(stt(lg[:, 1], anc[:, :, E2:2 * E2], arecip[:, 1:2], lg[:, 0], ALU.mult, ALU.add))
            then(nc.vector.reduce_max(lgs[:, 0], lg[:, 1], AX.X))
            then(tt(lg[:, 2], lg[:, 1], per_tile(lgs[:, 0]), ALU.subtract))
            add_to_x(2, NG - 1, 2)
            dve.wait_ge(s["lg_exp"], 1)
            then(nc.vector.reduce_sum(lgs[:, 1], lg[:, 3], AX.X))
            then(nc.vector.reciprocal(lgs[:, 2], lgs[:, 1]))
            then(tt(lg[:, 4], lg[:, 3], per_tile(lgs[:, 2]), ALU.mult))
            for n in range(NT):
                last = nc.vector.max(ltop[:, n], lg[:, 4, n])
            last.then_inc(s["w_ready"], 1)
            dve.wait_ge(s["w_ready"], 1)
            then(tt(lg[:, 5], lg[:, 4], ltop[:, :, 1:2].broadcast_to((P, NT, E2)), ALU.subtract))
            add_to_x(2, NG - 1, 3)
            dve.wait_ge(s["lg_sig"], 1)
            then(ts(lg[:, 5], lg[:, 6], 1.0, None, ALU.add))
            then(nc.vector.reciprocal(lg[:, 6], lg[:, 5]))
            then(tt(lg[:, 7], lg[:, 4], lg[:, 6], ALU.mult))
            then(nc.vector.reduce_sum(lgs[:, 1], lg[:, 7], AX.X))
            then(ts(lgs[:, 2], lgs[:, 1], 1e-9, None, ALU.add))
            then(nc.vector.reciprocal(lgs[:, 3], lgs[:, 2]))
            tt(lg[:, 0], lg[:, 7], per_tile(lgs[:, 3]), ALU.mult).then_inc(s["w_ready"], 1)

            def scale_z(i):
                dve.wait_ge(s["pm_ps"], i + 1)
                stt(zp[:, i], pb[mix_bank(i)][0:ZS, :], 0.5, z2[:, i * G * P:(i + 1) * G * P], ALU.mult, ALU.mult).then_inc(s["zp_ready"], 1)

            def zp_lo(i):
                dve.wait_ge(s["zp_hi"], i + 1)
                zp_i = zp[Z2:2 * Z2, bass.ds(i, 1), :].rearrange("p a n -> p (a n)")
                tt(ZP[Z2:2 * Z2, :], zp_i, ZP[Z2:2 * Z2, :].bitcast(F32), ALU.subtract).then_inc(s["zp_lo"], 1)

            def add_delta(i, t):
                dve.wait_ge(s["delta_ps"], G * i + (t + 1))
                xt = x_tile(i, t)
                tt(xt, pb[t][:, :], xt, ALU.add).then_inc(s["delta_new"], 1)

            def w3_sum(c):
                dve.wait_ge(s["w3_ps"], c + 1)
                tt(w3_raw[:, c], pb[4 + c][:, :], w3_raw[:, c], ALU.add).then_inc(s["w3_f"], 1)

            w3_sum(0)
            w3_sum(1)
            dve.wait_ge(s["bm_hi"], 1)
            split_b()
            scale_z(0)
            w3_sum(2)
            zp_lo(0)
            add_delta(0, 0)
            w3_sum(3)
            for t in range(1, G):
                add_delta(0, t)

            dve.wait_ge(s["bias_in"], 32)
            mix_y(3, 0, 0)
            mix_y(3, 0, 1)
            mix_y_lo(3, 0, 0)
            scale_z(1)
            mix_y(3, 0, 2)
            mix_y_lo(3, 0, 1)
            scale_z(2)
            mix_y(3, 0, 3)
            mix_y_lo(3, 0, 2)
            scale_z(3)
            mix_y_lo(3, 0, 3)
            with dve.Fori(1, NG) as i:
                zp_lo(i)
                add_to_x(3, i - 1, 0)
                add_to_x(3, i - 1, 1)
                for t in range(G):
                    add_delta(i, t)
                add_to_x(3, i - 1, 2)
                mix_y(3, i, 0)
                mix_y(3, i, 1)
                mix_y_lo(3, i, 0)
                mix_y_lo(3, i, 1)
                add_to_x(3, i - 1, 3)
                mix_y(3, i, 2)
                mix_y_lo(3, i, 2)
                mix_y(3, i, 3)
                mix_y_lo(3, i, 3)
            for t in range(G):
                add_to_x(3, NG - 1, t)

        @block.tensor
        def _(pe):
            mm = nc.tensor.matmul

            def mm3(out, lh, ll, rh, rl, first, last):
                mm(out, lh, rh, start=first, stop=False, skip_group_check=True)
                mm(out, lh, rl, start=False, stop=False, skip_group_check=True)
                return mm(out, ll, rh, start=False, stop=last, skip_group_check=True)

            def conv(layer, i, t):
                pe.wait_ge(s["xh_hi"], upto(layer // 2, i, t))
                pe.wait_ge(s["xh_lo"], upto(layer // 2, i, t))
                wh, wl = conv_w[layer // 2]
                for d in range(3):
                    last = mm3(pb[t][:, :].rearrange("p (b m) -> p b m", b=TB), wh[:, d, :], wl[:, d, :],
                               XH[0][:, t % 2, :, d:d + M], XH[1][:, t % 2, :, d:d + M], d == 0, d == 2)
                last.then_inc(s["y_ps"], 1)

            def turn(layer, i, t):
                pe.wait_ge(s["y_f"], upto(layer, i, t))
                for n in range(4):
                    last = nc.tensor.transpose(pb[4 + t][:, n * P:(n + 1) * P], F[:, t, n * P:(n + 1) * P], ident)
                last.then_inc(s["yt_ps"], 1)

            def bank_read(layer, i, t):
                pe.wait_ge(s["x_new"], upto(layer, i, t) - G)

            def from_y(layer, i, t, w, last_group=True, phases=range(R)):
                pe.wait_ge(s["y_hi"], upto(layer, i, t))
                pe.wait_ge(s["y_lo"], upto(layer, i, t))
                if layer == 0:
                    pe.wait_ge(s["ysum_done"], upto(layer, i, t))
                for r in phases:
                    last = mm3(pb[4 + t][:, :], Y[0][:, r, t * P:(t + 1) * P], Y[1][:, r, t * P:(t + 1) * P],
                               w[0][:, r, :], w[1][:, r, :], r == 0, last_group and r == R - 1)
                return last

            def scores0(i):
                pe.wait_ge(s["ysum_done"], upto(0, i, G - 1))
                for r in range(R):
                    last = mm(pb[0][0:GB, 0:E0], ysum[:, r, :], kq0[:, r, :], start=(r == 0), stop=(r == R - 1), skip_group_check=True)
                last.then_inc(s["sc0_ps"], 1)

            def coefficients0(i):
                pe.wait_ge(s["coef_p"], i + 1)
                for c in range(4):
                    last = mm(pb[1][:, c * GB:(c + 1) * GB], sc_p[:, 2 * c:2 * c + 2].rearrange("p e k -> p (e k)"),
                              cst[0:GB, 0:GB], start=(c == 0), stop=True, skip_group_check=True)
                last.then_inc(s["coef_ps"], 1)

            def h0(i):
                for c in range(4):
                    if c == 3:
                        pe.wait_ge(s["coef_sb"], i + 1)
                    for r in range(R):
                        last = mm3(pb[(c + 2) % 4][:, :], lora_dn[0][:, r, c * P:(c + 1) * P], lora_dn[1][:, r, c * P:(c + 1) * P],
                                   Y[0][:, r, :], Y[1][:, r, :], r == 0, r == R - 1)
                    last.then_inc(s["h_ps"], 1)

            def up0(i):
                for c in range(4):
                    pe.wait_ge(s["h_hi"], 4 * i + (c + 1))
                    pe.wait_ge(s["h_lo"], 4 * i + (c + 1))
                    for t in range(G):
                        last = mm3(pb[4 + t][:, :], ST[0][:, c, t * P:(t + 1) * P], ST[1][:, c, t * P:(t + 1) * P],
                                   lora_up[0][:, c, :], lora_up[1][:, c, :], False, c == 3)
                        if c == 3:
                            last.then_inc(s["ff_ps"], 1)

            pe.wait_ge(s["kq1_zero"], 1)
            for _ in range(WARM_UP):
                mm(pb[3][:, :], KQ1[0][:, 0, :], KQ1[0][:, :, :].rearrange("p r e -> p (r e)"), start=True, stop=True)

            pe.wait_ge(s["setup_in"], 16)
            condT = setup[:, S_COND:S_COND + B]
            for j in range(2):
                last = mm(pb[7][:, j * B:(j + 1) * B], setup[:, S_CTX + j * P:S_CTX + (j + 1) * P], condT,
                          start=(j == 0), stop=True, skip_group_check=True)
            last.then_inc(s["ctx_ps"], 1)

            def hidden(k):
                for j in range(2):
                    w = S_MW + (2 * j + k) * P
                    mm(pb[6][:, (2 * k + j) * B:(2 * k + j + 1) * B], setup[:, w:w + P], condT if k == 0 else hid[:, j, 0, :],
                       start=(j == 0), stop=True, skip_group_check=True).then_inc(s["hid_ps"], 1)

            hidden(0)

            def tables(part):
                for r in range(R):
                    if part == 0:
                        last = mm(pb[5][:, r * E0:(r + 1) * E0], setup[:, S_WQ0 + r * M:S_WQ0 + (r + 1) * M], cst[:, C_KEYS0:C_KEYS0 + E0],
                                  start=(r == 0), stop=True, skip_group_check=True)
                    elif part == 1:
                        last = mm(pb[5][:, 32 + r * E2:32 + (r + 1) * E2], setup32[:, T_A2T + r * M:T_A2T + (r + 1) * M],
                                  setup32[:, T_LIMEST:T_LIMEST + E2], start=False, stop=True, skip_group_check=True)
                    else:
                        last = mm(pb[5][:, 64 + r * E1:64 + (r + 1) * E1], setup32[0:16, T_WQ1 + r * M:T_WQ1 + (r + 1) * M],
                                  setup32[0:16, T_KEYS1:T_KEYS1 + E1], start=False, stop=True, skip_group_check=True)
                last.then_inc(s["tables_ps"], 1)

            pe.wait_ge(s["conv_w_lo"], 1)
            pe.wait_ge(s["border_set"], 2)
            conv(0, 0, 0)
            pe.wait_ge(s["hid_sb"], 2)
            hidden(1)
            conv(0, 0, 1)
            pe.wait_ge(s["cst_in"], 16)
            pe.wait_ge(s["setup2_in"], 32)
            tables(0)
            tables(1)
            turn(0, 0, 0)
            pe.wait_ge(s["hid_sb"], 4)
            pe.wait_ge(s["cst_in"], 16)
            pe.wait_ge(s["ones_set"], 1)
            for j in range(2):
                att_ps = pb[6][0:B, 4 * B + j * K1:4 * B + (j + 1) * K1]
                mm(att_ps, hid[:, j, 1, :], cst[:, C_MW2 + j * K1:C_MW2 + (j + 1) * K1], start=(j == 0), stop=False, skip_group_check=True)
                last = mm(att_ps, ones[0:1, 0:B], cst[0:1, C_MB2 + j * K1:C_MB2 + (j + 1) * K1], start=False, stop=True, skip_group_check=True)
            last.then_inc(s["att_ps"], 1)
            tables(2)
            conv(0, 0, 2)
            pe.wait_ge(s["kq1_lo"], 1)
            pe.wait_ge(s["delta_slice_sb"], 1)
            turn(0, 0, 1)
            conv(0, 0, 3)
            pe.wait_ge(s["att_max"], 2)
            pe.wait_ge(s["att_exp"], 2)
            turn(0, 0, 2)
            pe.wait_ge(s["att_ready"], 2)
            pe.wait_ge(s["ctx_ready"], 1)
            for j in range(2):
                last = nc.tensor.transpose(pb[7][0:K1, j * B:(j + 1) * B], att[:, j, :], ident[0:B, 0:B])
            last.then_inc(s["attT_ps"], 1)
            pe.wait_ge(s["org_lo"], 4)
            from_y(0, 0, 0, worg, last_group=False)
            pe.wait_ge(s["attT_sb"], 1)
            turn(0, 0, 3)
            pe.wait_ge(s["kernels_in"], 16)

            def mix_kernels(j):
                for h in range(2):
                    mm(pb[2 * j + h][0:B, :], attT[:, j, :], kernels[:, j, h * D:(h + 1) * D], start=True, stop=True)\
                        .then_inc(s["agg_ps"], 1)

            mix_kernels(0)
            from_y(0, 0, 1, worg, last_group=False)
            mix_kernels(1)
            from_y(0, 0, 2, worg, last_group=False)
            pe.wait_ge(s["agg_sb"], 4)
            for j in range(2):
                last = mm(pb[2][0:B, j * S:(j + 1) * S], attT[:, j, :], setup32[0:K1, T_MBK + j * S:T_MBK + (j + 1) * S],
                          start=(j == 0), stop=True, skip_group_check=True)
            last.then_inc(s["bias_ps"], 1)
            pe.wait_ge(s["kq0_sb"], 1)
            scores0(0)
            from_y(0, 0, 3, worg, last_group=False)
            pe.wait_ge(s["bias_sb"], 1)
            pe.wait_ge(s["raw_lo"], 4)
            coefficients0(0)
            h0(0)
            pe.wait_ge(s["raw_lo"], 8)
            up0(0)

            with pe.Fori(1, NG) as i:
                conv(0, i, 0)
                for t in range(1, G):
                    conv(0, i, t)
                    bank_read(0, i, t - 1)
                    turn(0, i, t - 1)
                from_y(0, i, 0, worg, last_group=False)
                bank_read(0, i, G - 1)
                turn(0, i, G - 1)
                from_y(0, i, 1, worg, last_group=False)
                from_y(0, i, 2, worg, last_group=False)
                scores0(i)
                from_y(0, i, 3, worg, last_group=False)
                coefficients0(i)
                h0(i)
                up0(i)

            def mix(layer, i, t):
                pe.wait_ge(s["mx_ready"], i + (layer // 2 * NG + 1))
                pe.wait_ge(s["rows_sb"], upto(layer // 2, i, t))
                for r in range(R):
                    rows = xf[:, t, r, :] if layer == 1 else rows3[:, t, r * M:(r + 1) * M]
                    last = mm(pb[t][:, r * P:(r + 1) * P], rows, MX[:, t], start=True, stop=True)
                last.then_inc(s["y_ps"], 1)

            def turn_z(i, t):
                pe.wait_ge(s["zg_f"], G * i + (t + 1))
                for c in range(4):
                    last = nc.tensor.transpose(pb[t][:, c * P:(c + 1) * P], F[:, t, c * P:(c + 1) * P], ident)
                last.then_inc(s["zt_ps"], 1)

            pe.wait_ge(s["stage_lo"], 2 * NG)
            with pe.Fori(0, NG) as i:
                for t in range(G):
                    mix(1, i, t)
                bank_read(1, i, 0)
                from_y(1, i, 0, a1).then_inc(s["z_ps"], 1)
                bank_read(1, i, G - 1)
                from_y(1, i, 1, a1, phases=range(1))
                pe.wait_ge(s["y_hi"], upto(1, i, G - 1))
                pe.wait_ge(s["y_lo"], upto(1, i, G - 1))
                for r in range(R):
                    last = mm3(pb[0][:, :], KQ1[0][:, r, :], KQ1[1][:, r, :], Y[0][:, r, :], Y[1][:, r, :], r == 0, r == R - 1)
                last.then_inc(s["sct_ps"], 1)
                from_y(1, i, 1, a1, phases=range(1, 2))
                for t in range(G):
                    if t % 2 == 0:
                        pe.wait_ge(s["sct_sb"], 2 * i + (t // 2 + 1))
                    last = nc.tensor.transpose(pb[1][:, t * P:(t + 1) * P], scT[:, t * P:(t + 1) * P], ident)
                last.then_inc(s["sc1_ps"], 1)
                from_y(1, i, 1, a1, phases=range(2, R)).then_inc(s["z_ps"], 1)
                from_y(1, i, 2, a1).then_inc(s["z_ps"], 1)
                from_y(1, i, 3, a1, phases=range(R - 1))
                turn_z(i, 0)
                from_y(1, i, 3, a1, phases=range(R - 1, R)).then_inc(s["z_ps"], 1)
                turn_z(i, 1)
                turn_z(i, 2)
                for t in range(G):
                    if t == 1:
                        turn_z(i, 3)
                    pe.wait_ge(s["zt_hi"], G * i + (t + 1))
                    pe.wait_ge(s["zt_lo"], G * i + (t + 1))
                    for c in range(4):
                        last = mm3(pb[4 + t][:, :], ST[0][:, t, c * P:(c + 1) * P], ST[1][:, t, c * P:(c + 1) * P],
                                   b1[0][:, c, :], b1[1][:, c, :], c == 0, c == 3)
                    last.then_inc(s["ff_ps"], 1)

            pe.wait_ge(s["stage_lo"], 3 * NG)
            pe.wait_ge(s["slice_w_lo"], 1)
            pe.wait_ge(s["conv_w_lo"], 2)
            with pe.Fori(0, NG) as i:
                conv(2, i, 0)
                pe.wait_ge(s["x_new"], upto(2, i, 2) - G)
                conv(2, i, 1)
                bank_read(2, i, 0)
                turn(2, i, 0)
                conv(2, i, 2)
                bank_read(2, i, 1)
                turn(2, i, 1)
                conv(2, i, 3)
                bank_read(2, i, 2)
                turn(2, i, 2)
                from_y(2, i, 0, w2, phases=range(2))
                bank_read(2, i, 3)
                turn(2, i, 3)
                from_y(2, i, 0, w2, phases=range(2, R)).then_inc(s["ff_ps"], 1)
                from_y(2, i, 1, w2, phases=range(1))
                pe.wait_ge(s["y_hi"], upto(2, i, G - 1))
                pe.wait_ge(s["y_lo"], upto(2, i, G - 1))
                for r in range(R):
                    last = mm3(pb[0][0:SLICES, :], SLW[0][:, r, :], SLW[1][:, r, :], Y[0][:, r, :], Y[1][:, r, :], r == 0, r == R - 1)
                last.then_inc(s["sl_ps"], 1)
                from_y(2, i, 1, w2, phases=range(1, R - 1))
                pe.wait_ge(s["sl_sb"], i + 1)
                pe.wait_ge(s["z2_sb"], i + 1)
                for t in range(G):
                    last = mm(pb[1][:, t * 2 * E2:(t + 1) * 2 * E2], sl_ring[ZS:SLICES, t * P:(t + 1) * P], cst[ZS:SLICES, ZS:SLICES],
                              start=(t == 0), stop=True, skip_group_check=True)
                last.then_inc(s["anc_ps"], 1)
                from_y(2, i, 1, w2, phases=range(R - 1, R)).then_inc(s["ff_ps"], 1)
                from_y(2, i, 2, w2).then_inc(s["ff_ps"], 1)
                from_y(2, i, 3, w2).then_inc(s["ff_ps"], 1)

            pe.wait_ge(s["b3_ready"], 2)

            def merge_w3(c, k):
                return mm(pb[4 + c][:, :], a3_raw[:, k, c * M:(c + 1) * M], b3_scaled[:, k, :], start=(k == 0), stop=(k == 1))

            for c in range(3):
                pe.wait_ge(s["x_new"], 3 * NT - G + c + 1)
                merge_w3(c, 0)
                merge_w3(c, 1).then_inc(s["w3_ps"], 1)

            pe.wait_ge(s["w_ready"], 2)

            def turn_w(i):
                for t in range(G):
                    last = nc.tensor.transpose(pb[mix_bank(i)][0:E2, t * P:(t + 1) * P], lg[:, 0, G * i + t], ident)
                last.then_inc(s["wT_ps"], 1)

            def mix_limes(i):
                pe.wait_ge(s["wT_sb"], i + 1)
                mm(pb[mix_bank(i)][0:ZS, :], cst[0:E2, C_LIMES:C_LIMES + ZS], w2T[:, i, :], start=True, stop=True).then_inc(s["pm_ps"], 1)

            def deltas(i):
                pe.wait_ge(s["zp_hi"], i + 1)
                pe.wait_ge(s["zp_lo"], i + 1)
                for t in range(G):
                    mm(pb[t][:, :], ZP[:, t * P:(t + 1) * P], BM[:, :], start=True, stop=True).then_inc(s["delta_ps"], 1)

            turn_w(0)
            pe.wait_ge(s["x_new"], 3 * NT)
            merge_w3(3, 0)
            mix_limes(0)
            pe.wait_ge(s["w3_f"], 2)
            turn_w(1)
            merge_w3(3, 1).then_inc(s["w3_ps"], 1)
            mix_limes(1)
            pe.wait_ge(s["bm_lo"], 1)
            pe.wait_ge(s["bm_ready"], 1)
            pe.wait_ge(s["ones2_set"], 1)
            deltas(0)
            pe.wait_ge(s["w3_f"], 3)
            turn_w(2)

            def apply_w3(i, t):
                from_y(3, i, t, w3).then_inc(s["ff_ps"], 1)

            mix(3, 0, 0)
            pe.wait_ge(s["w3_f"], 4)
            turn_w(3)
            mix(3, 0, 1)
            mix_limes(2)
            mix_limes(3)
            mix(3, 0, 2)
            mix(3, 0, 3)
            pe.wait_ge(s["w3_lo"], 4)
            apply_w3(0, 0)
            with pe.Fori(1, NG) as i:
                pe.wait_ge(s["zp_ready"], 2)
                bank_read(3, i - 1, G - 1)
                apply_w3(i - 1, 1)
                pe.wait_ge(s["y_f"], upto(3, i - 1, G - 1))
                deltas(i)
                pe.wait_ge(s["zp_ready"], NG)
                apply_w3(i - 1, 2)
                mix(3, i, 0)
                mix(3, i, 1)
                apply_w3(i - 1, 3)
                mix(3, i, 2)
                mix(3, i, 3)
                bank_read(3, i, 0)
                apply_w3(i, 0)
            bank_read(3, NG - 1, G - 1)
            for t in range(1, G):
                apply_w3(NG - 1, t)


def kernel(**inputs):
    import numpy as np
    import concourse.bacc as bacc
    from concourse.bass_utils import run_bass_kernel_spmd

    def a(name):
        return np.asarray(inputs[name])

    def dec(w):
        return w.reshape(*w.shape[:-1], M, R).swapaxes(-1, -2).reshape(w.shape)

    def chunks(w):
        return w.reshape(w.shape[0] // P, P, -1).swapaxes(0, 1)

    def banded(w):
        per = w.shape[1]
        out = np.zeros((S, R, 3, R, S), np.float32)
        for d in range(3):
            for rp in range(R):
                for r in range(R):
                    k = R * (d - 1) + rp - r + 4
                    if 0 <= k < w.shape[2]:
                        for g in range(S // per):
                            out[g * per:(g + 1) * per, rp, d, r, g * per:(g + 1) * per] = w[g * per:(g + 1) * per, :, k].T
        return out.reshape(P, 3 * P)

    def pack(rows, width, *parts):
        out = np.zeros((rows, width), np.float32)
        for at, v in parts:
            v = v.reshape(v.shape[0], -1)
            out[:v.shape[0], at:at + v.shape[1]] = v
        return out

    w2t = a("L2_ffn_W").T
    w3t = a("L3_ffn_W").T

    def rows_dec(w):
        return w.reshape(M, R, -1)

    two = ("L1", "L3")
    row = np.arange(P)
    cst = pack(P, C_ALL,
               (C_IDENT, np.eye(P)),
               (C_BLK, row[:, None] // S == np.arange(TB)),
               (C_FSIDE, np.tile(a("fside_S_0"), R)[:, None]),
               (C_MB, np.stack([a(f"{n}_cond_b{k}") for n in two for k in range(2)], 1)),
               (C_MW2, np.concatenate([a(f"{n}_cond_W2") for n in two], 1)),
               (C_MB2, np.concatenate([a(f"{n}_cond_b2") for n in two])[None]),
               (C_KEYS0, a("L0_ffn_lora_keys").T),
               (C_LIMES, np.tile(a("L2_ffn_LiMEs"), (1, 3))),
               (C_SB, np.concatenate([np.zeros(ZS + E2, np.float32), a("L2_ffn_b")[0:E2]])[:, None]),
               (C_E3, np.concatenate([np.repeat(a(f"L3_ffn_{n}"), 16).reshape(2, P).T for n in ("coeffs", "scales")], 1)),
               (C_LO, np.concatenate([np.zeros((ZS, 2)), [[1.0, 0.0], [-1.0, 1.0]]])))
    slices = np.zeros((P, R, SLICES), np.float32)
    slices[:, :, 0:ZS] = np.tile(rows_dec(a("L2_ffn_A")), (1, 1, 3))
    slices[:, :, ZS + E2:] = rows_dec(w2t[:, 0:E2])
    setup = pack(P, S_ALL,
                 (S_COND, a("cond_128").T),
                 (S_CTX, np.concatenate([np.tile(a(f"{n}_cond_c_weight").T, (1, R)) for n in ("L0", "L2")], 1)),
                 (S_MW, np.concatenate([a(f"{n}_cond_W{k}") for n in two for k in range(2)], 1)),
                 (S_WQ0, dec(a("L0_ffn_Wq"))),
                 (S_SLICE, slices))
    setup32 = pack(Z2, T_ALL,
                   (T_A2T, dec(a("L2_ffn_A").T)),
                   (T_LIMEST, a("L2_ffn_LiMEs").T),
                   (T_WQ1, dec(a("L1_ffn_Wq_w"))),
                   (T_KEYS1, a("L1_ffn_keys").T),
                   (T_MBK, np.concatenate([a(f"{n}_cond_bias_k") for n in two], 1)))
    arrays = {
        "cst": cst,
        "setup": setup,
        "setup32": setup32,
        "kernels": np.stack([a(f"{n}_cond_weight")[..., 0].transpose(0, 2, 1).reshape(K1, S * S) for n in two], 1),
        "x": a("x").reshape(B, S, M, R).transpose(0, 1, 3, 2),
        "conv0": banded(a("L0_cond_weight")),
        "conv2": banded(a("L2_cond_weight")),
        "worg": rows_dec(dec(a("L0_ffn_W_org").T)),
        "lora_dn": rows_dec(a("L0_ffn_lora_down").transpose(1, 0, 2).reshape(D, D)),
        "lora_up": chunks(dec(a("L0_ffn_lora_up").reshape(D, D))),
        "a1": rows_dec(a("L1_ffn_A_w").T).reshape(P, -1),
        "b1": chunks(dec(a("L1_ffn_B_w").T)).reshape(P, -1),
        "w2": rows_dec(dec(w2t)).reshape(P, -1),
        "bmat": np.concatenate([dec(a("L2_ffn_Bmat"))] * 3 + [dec(a("L2_ffn_b")[None])] * 2),
        "w3": rows_dec(dec(w3t)),
        "a3": chunks(dec(a("L3_ffn_A").reshape(256, D))),
        "b3": chunks(dec(a("L3_ffn_Bf").transpose(0, 2, 1).reshape(256, D))),
        "bias3": dec(a("L3_ffn_bias")[None]),
    }
    nc = bacc.Bacc("TRN2", target_bir_lowering=False, num_devices=1)
    arrays = {n: np.ascontiguousarray(v) for n, v in arrays.items()}
    t_in = {n: nc.dram_tensor(f"in_{n}", v.shape, mybir.dt.from_np(v.dtype), kind="ExternalInput").ap()
            for n, v in arrays.items()}
    out = nc.dram_tensor("out_x", (B, S, R, M), F32, kind="ExternalOutput").ap()
    scratch = nc.dram_tensor("scratch_x", (B, S, R, M), F32).ap()
    scratch_agg = nc.dram_tensor("scratch_agg", (2, B, S * S), F32).ap()
    scratch_bias = nc.dram_tensor("scratch_bias", (2, B, S), F32).ap()
    build(nc, t_in, out, scratch, scratch_agg, scratch_bias)
    res = run_bass_kernel_spmd(nc, [{f"in_{n}": v for n, v in arrays.items()}], core_ids=[0])
    got = res.results[0]["out_x"]
    return np.ascontiguousarray(got.transpose(0, 1, 3, 2).reshape(B, S, D))
```
